# Optimizing a Trainium2 kernel written in Bass

```python
import numpy as np
import jax
import jax.numpy as jnp

def _softmax(x, axis=-1):
    return jax.nn.softmax(x, axis=axis)

def _gelu(x):
    return jax.nn.gelu(x, approximate=True)

def _silu(x):
    return jax.nn.silu(x)

def _sigmoid(x):
    return jax.nn.sigmoid(x)

def _layernorm(x, axis=-1, eps=1e-05):
    m = jnp.mean(x, axis=axis, keepdims=True)
    v = jnp.var(x, axis=axis, keepdims=True)
    return (x - m) / jnp.sqrt(v + eps)

def _scatter_add(tgt, idx, src, axis=0):
    return tgt.at[idx].add(src)

def _segment_sum(src, seg, n):
    return jax.ops.segment_sum(src, seg, n)
kernel_name = 'mk_seq_preln_d2_jaxref_r8_cc1824'

def setup_inputs(seed: int=0):
    np.random.seed(seed)
    _w = jnp.asarray

    def _L0_attn_setup():
        import jax, jax.numpy as jnp
        import numpy as np
        E = 128
        H = 16
        HD = E // H
        MAX_REL = 20
        key = jax.random.key(seed)
        ks = jax.random.split(key, 12)
        B, S = (4, 128)

        def lin_w(k):
            return jax.random.normal(k, (E, E), dtype=jnp.float32) * (1.0 / np.sqrt(E))
        return {'hidden_states': jax.random.normal(ks[0], (B, S, E), dtype=jnp.float32), 'Wq': lin_w(ks[1]), 'bq': jnp.zeros((E,), jnp.float32), 'Wk': lin_w(ks[2]), 'bk': jnp.zeros((E,), jnp.float32), 'Wv': lin_w(ks[3]), 'bv': jnp.zeros((E,), jnp.float32), 'Wo': lin_w(ks[4]), 'bo': jnp.zeros((E,), jnp.float32), 'rel_k': jax.random.uniform(ks[5], (2 * MAX_REL + 1, HD), jnp.float32, -0.24, 0.24), 'rel_v': jax.random.uniform(ks[6], (2 * MAX_REL + 1, HD), jnp.float32, -0.24, 0.24)}
    _L0_attn_in = _L0_attn_setup()

    def _L0_ffn_setup():
        import jax, jax.numpy as jnp
        import numpy as np
        D = 128
        H = 16
        HD = D // H
        L = 64
        E = 8
        B, T = (4, 256)
        EPS = 1e-06

        def _glorot(k, shape):
            fan_in, fan_out = (shape[-2], shape[-1])
            lim = np.sqrt(6.0 / (fan_in + fan_out)).astype(np.float32)
            return jax.random.uniform(k, shape, jnp.float32, -lim, lim)

        def _rmsnorm(x, gamma):
            return gamma * x * jax.lax.rsqrt(jnp.mean(x * x, axis=-1, keepdims=True) + EPS)
        key = jax.random.key(seed)
        ks = jax.random.split(key, 8)
        return {'x': jax.random.normal(ks[0], (B, T, D), jnp.float32), 'gamma1': jnp.ones((D,), jnp.float32), 'Wq': _glorot(ks[1], (D, D)), 'bq': jnp.zeros((D,), jnp.float32), 'Wdown': _glorot(ks[2], (D, L)), 'bdown': jnp.zeros((L,), jnp.float32), 'Wup': _glorot(ks[3], (L, 2 * D)), 'bup': jnp.zeros((2 * D,), jnp.float32), 'Wo': _glorot(ks[4], (D, D)), 'bo': jnp.zeros((D,), jnp.float32), 'gamma2': jnp.ones((D,), jnp.float32), 'Wg': _glorot(ks[5], (D, E)), 'bg': jnp.zeros((E,), jnp.float32), 'We': _glorot(ks[6], (E, D, D))}
    _L0_ffn_in = _L0_ffn_setup()

    def _L1_attn_setup():
        import jax, jax.numpy as jnp
        import numpy as np
        DIM = 128
        DIM_HEAD = 16
        HEADS = 8
        EPS = 1e-05

        def rms_norm(x, gamma):
            n = jnp.sqrt(jnp.sum(x * x, axis=-1, keepdims=True))
            return gamma * (x / jnp.maximum(n, 1e-12)) * x.shape[-1] ** 0.5

        def second_taylor_expansion(x):
            d = x.shape[-1]
            x0 = jnp.ones(x.shape[:-1] + (1,), dtype=x.dtype)
            x2 = jnp.einsum('...i,...j->...ij', x, x) * 0.5 ** 0.5
            x2 = x2.reshape(x.shape[:-1] + (d * d,))
            return jnp.concatenate([x0, x, x2], axis=-1)
        key = jax.random.key(seed)
        ks = jax.random.split(key, 4)
        b, n = (4, 1024)
        dim_inner = DIM_HEAD * HEADS
        x = jax.random.normal(ks[0], (b, n, DIM), dtype=jnp.float32)
        gamma = jnp.ones((DIM,), dtype=jnp.float32)
        w_q = jax.random.normal(ks[1], (DIM, dim_inner), dtype=jnp.float32) * DIM ** (-0.5)
        w_kv = jax.random.normal(ks[2], (DIM, dim_inner * 2), dtype=jnp.float32) * DIM ** (-0.5)
        w_out = jax.random.normal(ks[3], (dim_inner, DIM), dtype=jnp.float32) * dim_inner ** (-0.5)
        return {'x': x, 'gamma': gamma, 'w_q': w_q, 'w_kv': w_kv, 'w_out': w_out}
    _L1_attn_in = _L1_attn_setup()

    def _L1_ffn_setup():
        import jax, jax.numpy as jnp
        import numpy as np
        from jax import lax
        D = 128
        H = 176
        E = 8
        K = 2
        ROUTER_SCALE = 1.0

        def _expert(x, w1, b1, w3, b3, w2, b2):
            h = jax.nn.silu((x @ w1 + b1) * (x @ w3 + b3))
            return h @ w2 + b2
        key = jax.random.key(seed)
        ks = jax.random.split(key, 16)
        s = 0.02
        inp = {'x': jax.random.normal(ks[0], (2, 256, D), dtype=jnp.float32), 'gate_w': jax.random.normal(ks[1], (E, D), dtype=jnp.float32) * s, 'gate_b': jax.random.normal(ks[2], (E,), dtype=jnp.float32) * s, 'w1': jax.random.normal(ks[3], (E, D, H), dtype=jnp.float32) * s, 'b1': jax.random.normal(ks[4], (E, H), dtype=jnp.float32) * s, 'w3': jax.random.normal(ks[5], (E, D, H), dtype=jnp.float32) * s, 'b3': jax.random.normal(ks[6], (E, H), dtype=jnp.float32) * s, 'w2': jax.random.normal(ks[7], (E, H, D), dtype=jnp.float32) * s, 'b2': jax.random.normal(ks[8], (E, D), dtype=jnp.float32) * s, 'sw1': jax.random.normal(ks[9], (D, H), dtype=jnp.float32) * s, 'sb1': jax.random.normal(ks[10], (H,), dtype=jnp.float32) * s, 'sw3': jax.random.normal(ks[11], (D, H), dtype=jnp.float32) * s, 'sb3': jax.random.normal(ks[12], (H,), dtype=jnp.float32) * s, 'sw2': jax.random.normal(ks[13], (H, D), dtype=jnp.float32) * s, 'sb2': jax.random.normal(ks[14], (D,), dtype=jnp.float32) * s}
        return inp
    _L1_ffn_in = _L1_ffn_setup()
    _d = {'L0_attn_hidden_states': _L0_attn_in['hidden_states'], 'L0_attn_Wq': _L0_attn_in['Wq'], 'L0_attn_bq': _L0_attn_in['bq'], 'L0_attn_Wk': _L0_attn_in['Wk'], 'L0_attn_bk': _L0_attn_in['bk'], 'L0_attn_Wv': _L0_attn_in['Wv'], 'L0_attn_bv': _L0_attn_in['bv'], 'L0_attn_Wo': _L0_attn_in['Wo'], 'L0_attn_bo': _L0_attn_in['bo'], 'L0_attn_rel_k': _L0_attn_in['rel_k'], 'L0_attn_rel_v': _L0_attn_in['rel_v'], 'L0_ffn_gamma1': _L0_ffn_in['gamma1'], 'L0_ffn_Wq': _L0_ffn_in['Wq'], 'L0_ffn_bq': _L0_ffn_in['bq'], 'L0_ffn_Wdown': _L0_ffn_in['Wdown'], 'L0_ffn_bdown': _L0_ffn_in['bdown'], 'L0_ffn_Wup': _L0_ffn_in['Wup'], 'L0_ffn_bup': _L0_ffn_in['bup'], 'L0_ffn_Wo': _L0_ffn_in['Wo'], 'L0_ffn_bo': _L0_ffn_in['bo'], 'L0_ffn_gamma2': _L0_ffn_in['gamma2'], 'L0_ffn_Wg': _L0_ffn_in['Wg'], 'L0_ffn_bg': _L0_ffn_in['bg'], 'L0_ffn_We': _L0_ffn_in['We'], 'L1_attn_gamma': _L1_attn_in['gamma'], 'L1_attn_w_q': _L1_attn_in['w_q'], 'L1_attn_w_kv': _L1_attn_in['w_kv'], 'L1_attn_w_out': _L1_attn_in['w_out'], 'L1_ffn_gate_w': _L1_ffn_in['gate_w'], 'L1_ffn_gate_b': _L1_ffn_in['gate_b'], 'L1_ffn_w1': _L1_ffn_in['w1'], 'L1_ffn_b1': _L1_ffn_in['b1'], 'L1_ffn_w3': _L1_ffn_in['w3'], 'L1_ffn_b3': _L1_ffn_in['b3'], 'L1_ffn_w2': _L1_ffn_in['w2'], 'L1_ffn_b2': _L1_ffn_in['b2'], 'L1_ffn_sw1': _L1_ffn_in['sw1'], 'L1_ffn_sb1': _L1_ffn_in['sb1'], 'L1_ffn_sw3': _L1_ffn_in['sw3'], 'L1_ffn_sb3': _L1_ffn_in['sb3'], 'L1_ffn_sw2': _L1_ffn_in['sw2'], 'L1_ffn_sb2': _L1_ffn_in['sb2']}
    _x0 = _d['L0_attn_hidden_states']
    _d['L0_attn_hidden_states'] = jax.random.normal(jax.random.fold_in(jax.random.key(seed), 1), (8, 256, 128), dtype=_x0.dtype)
    del _x0
    return _d

def reference(L0_attn_hidden_states, L0_attn_Wq, L0_attn_bq, L0_attn_Wk, L0_attn_bk, L0_attn_Wv, L0_attn_bv, L0_attn_Wo, L0_attn_bo, L0_attn_rel_k, L0_attn_rel_v, L0_ffn_gamma1, L0_ffn_Wq, L0_ffn_bq, L0_ffn_Wdown, L0_ffn_bdown, L0_ffn_Wup, L0_ffn_bup, L0_ffn_Wo, L0_ffn_bo, L0_ffn_gamma2, L0_ffn_Wg, L0_ffn_bg, L0_ffn_We, L1_attn_gamma, L1_attn_w_q, L1_attn_w_kv, L1_attn_w_out, L1_ffn_gate_w, L1_ffn_gate_b, L1_ffn_w1, L1_ffn_b1, L1_ffn_w3, L1_ffn_b3, L1_ffn_w2, L1_ffn_b2, L1_ffn_sw1, L1_ffn_sb1, L1_ffn_sw3, L1_ffn_sb3, L1_ffn_sw2, L1_ffn_sb2):

    def _L0_attn_ref(hidden_states, Wq, bq, Wk, bk, Wv, bv, Wo, bo, rel_k, rel_v):
        import jax, jax.numpy as jnp
        import numpy as np
        E = 128
        H = 16
        HD = E // H
        MAX_REL = 20
        B, S, _ = hidden_states.shape
        scale = jnp.sqrt(jnp.float32(HD))

        def proj(W, b):
            return (hidden_states @ W.T + b).reshape(B, S, H, HD).transpose(0, 2, 1, 3)
        q = proj(Wq, bq)
        k = proj(Wk, bk)
        v = proj(Wv, bv)
        pos = jnp.arange(S)
        idx = jnp.clip(pos[None, :] - pos[:, None], -MAX_REL, MAX_REL) + MAX_REL
        rk2 = rel_k[idx]
        rv2 = rel_v[idx]
        attn1 = jnp.einsum('bhqd,bhkd->bhqk', q, k)
        attn2 = jnp.einsum('bhqd,qkd->bhqk', q, rk2)
        attn = jax.nn.softmax((attn1 + attn2) / scale, axis=-1)
        w1 = jnp.einsum('bhqk,bhkd->bhqd', attn, v)
        w2 = jnp.einsum('bhqk,qkd->bhqd', attn, rv2)
        x = (w1 + w2).transpose(0, 2, 1, 3).reshape(B, S, E)
        out = x @ Wo.T + bo
        return out

    def _L0_ffn_ref(x, gamma1, Wq, bq, Wdown, bdown, Wup, bup, Wo, bo, gamma2, Wg, bg, We):
        import jax, jax.numpy as jnp
        import numpy as np
        D = 128
        H = 16
        HD = D // H
        L = 64
        E = 8
        B, T = (4, 256)
        EPS = 1e-06

        def _glorot(k, shape):
            fan_in, fan_out = (shape[-2], shape[-1])
            lim = np.sqrt(6.0 / (fan_in + fan_out)).astype(np.float32)
            return jax.random.uniform(k, shape, jnp.float32, -lim, lim)

        def _rmsnorm(x, gamma):
            return gamma * x * jax.lax.rsqrt(jnp.mean(x * x, axis=-1, keepdims=True) + EPS)
        b, t = (x.shape[0], x.shape[1])
        h = _rmsnorm(x, gamma1)
        q = (h @ Wq + bq).reshape(b, t, H, HD)
        kv = ((h @ Wdown + bdown) @ Wup + bup).reshape(b, t, H, 2 * HD)
        k, v = jnp.split(kv, 2, axis=-1)
        att = jnp.einsum('bthd,btgd->bthg', q, k) / np.sqrt(HD).astype(np.float32)
        att = jax.nn.softmax(att, axis=-1)
        out = jnp.einsum('bthg,btgd->bthd', att, v).reshape(b, t, D)
        x = x + (out @ Wo + bo)
        h2 = _rmsnorm(x, gamma2)
        gate = jax.nn.softmax(h2 @ Wg + bg, axis=-1)
        combined = jnp.einsum('btd,edf,bte->btf', h2, We, gate)
        return x + combined

    def _L1_attn_ref(x, gamma, w_q, w_kv, w_out):
        import jax, jax.numpy as jnp
        import numpy as np
        DIM = 128
        DIM_HEAD = 16
        HEADS = 8
        EPS = 1e-05

        def rms_norm(x, gamma):
            n = jnp.sqrt(jnp.sum(x * x, axis=-1, keepdims=True))
            return gamma * (x / jnp.maximum(n, 1e-12)) * x.shape[-1] ** 0.5

        def second_taylor_expansion(x):
            d = x.shape[-1]
            x0 = jnp.ones(x.shape[:-1] + (1,), dtype=x.dtype)
            x2 = jnp.einsum('...i,...j->...ij', x, x) * 0.5 ** 0.5
            x2 = x2.reshape(x.shape[:-1] + (d * d,))
            return jnp.concatenate([x0, x, x2], axis=-1)
        b, n, _ = x.shape
        h, dh = (HEADS, DIM_HEAD)
        normed = rms_norm(x, gamma)
        q = (normed @ w_q).reshape(b, n, h, dh).transpose(0, 2, 1, 3)
        kv = (normed @ w_kv).reshape(b, n, 2, h, dh).transpose(2, 0, 3, 1, 4)
        k, v = (kv[0], kv[1])
        q = q * dh ** (-0.5)
        q = second_taylor_expansion(q)
        k = second_taylor_expansion(k)
        kv_state = jnp.einsum('bhnd,bhne->bhde', k, v)
        k_sum = jnp.sum(k, axis=2)
        den = jnp.einsum('bhnd,bhd->bhn', q, k_sum)
        qk_inv = 1.0 / jnp.maximum(den, EPS)
        out = jnp.einsum('bhnd,bhde->bhne', q, kv_state) * qk_inv[..., None]
        out = out.transpose(0, 2, 1, 3).reshape(b, n, h * dh)
        return out @ w_out

    def _L1_ffn_ref(x, gate_w, gate_b, w1, b1, w3, b3, w2, b2, sw1, sb1, sw3, sb3, sw2, sb2):
        import jax, jax.numpy as jnp
        import numpy as np
        from jax import lax
        D = 128
        H = 176
        E = 8
        K = 2
        ROUTER_SCALE = 1.0

        def _expert(x, w1, b1, w3, b3, w2, b2):
            h = jax.nn.silu((x @ w1 + b1) * (x @ w3 + b3))
            return h @ w2 + b2
        shape = x.shape
        xf = x.reshape(-1, D)
        T = xf.shape[0]
        scores = jax.nn.softmax(xf @ gate_w.T, axis=-1)
        biased = scores + gate_b
        _, idx = lax.top_k(biased, K)
        w = jnp.take_along_axis(scores, idx, axis=-1) * ROUTER_SCALE
        rw = jnp.zeros((T, E), dtype=xf.dtype).at[jnp.arange(T)[:, None], idx].add(w)
        h = jax.nn.silu((jnp.einsum('td,edh->teh', xf, w1) + b1) * (jnp.einsum('td,edh->teh', xf, w3) + b3))
        oe = jnp.einsum('teh,ehd->ted', h, w2) + b2
        y = jnp.einsum('te,ted->td', rw, oe)
        z = _expert(xf, sw1, sb1, sw3, sb3, sw2, sb2)
        return (y + z).reshape(shape)
    x = L0_attn_hidden_states
    x = x + _L0_attn_ref(_layernorm(x, axis=-1), L0_attn_Wq, L0_attn_bq, L0_attn_Wk, L0_attn_bk, L0_attn_Wv, L0_attn_bv, L0_attn_Wo, L0_attn_bo, L0_attn_rel_k, L0_attn_rel_v)
    x = x + _L0_ffn_ref(_layernorm(x, axis=-1), L0_ffn_gamma1, L0_ffn_Wq, L0_ffn_bq, L0_ffn_Wdown, L0_ffn_bdown, L0_ffn_Wup, L0_ffn_bup, L0_ffn_Wo, L0_ffn_bo, L0_ffn_gamma2, L0_ffn_Wg, L0_ffn_bg, L0_ffn_We)
    x = x + _L1_attn_ref(_layernorm(x, axis=-1), L1_attn_gamma, L1_attn_w_q, L1_attn_w_kv, L1_attn_w_out)
    x = x + _L1_ffn_ref(_layernorm(x, axis=-1), L1_ffn_gate_w, L1_ffn_gate_b, L1_ffn_w1, L1_ffn_b1, L1_ffn_w3, L1_ffn_b3, L1_ffn_w2, L1_ffn_b2, L1_ffn_sw1, L1_ffn_sb1, L1_ffn_sw3, L1_ffn_sb3, L1_ffn_sw2, L1_ffn_sb2)
    return x

_drawn_inputs = setup_inputs


def setup_inputs(seed=0):
    import zlib

    import numpy as np

    out = dict(_drawn_inputs(seed))
    spreads = {'L0_attn_bq': (0.0, 0.574),
     'L0_attn_bk': (0.0, 2.0),
     'L0_attn_bv': (0.0, 0.1),
     'L0_attn_bo': (0.0, 0.1),
     'L0_ffn_gamma1': (1.0, 0.2),
     'L0_ffn_bq': (0.0, 0.74),
     'L0_ffn_bdown': (0.0, 0.581),
     'L0_ffn_bup': (0.0, 0.303),
     'L0_ffn_bo': (0.0, 0.1),
     'L0_ffn_gamma2': (1.0, 0.2),
     'L0_ffn_bg': (0.0, 0.643),
     'L1_attn_gamma': (1.0, 0.6)}
    factors = {'L0_attn_rel_k': 2.973,
     'L1_ffn_gate_w': 8.0,
     'L1_ffn_gate_b': 8.0,
     'L1_ffn_w1': 8.0,
     'L1_ffn_b1': 8.0,
     'L1_ffn_w3': 8.0,
     'L1_ffn_b3': 8.0,
     'L1_ffn_w2': 8.0,
     'L1_ffn_b2': 29.987,
     'L1_ffn_sw1': 8.0,
     'L1_ffn_sb1': 8.0,
     'L1_ffn_sw3': 8.0,
     'L1_ffn_sb3': 8.0,
     'L1_ffn_sw2': 8.0,
     'L1_ffn_sb2': 17.628}
    for name, (base, spread) in spreads.items():
        noise = np.random.default_rng([zlib.crc32(name.encode()), seed]).standard_normal(out[name].shape)
        drawn = base * np.exp(spread * noise) if base else spread * noise
        out[name] = jnp.asarray(drawn.astype(out[name].dtype))
    for name, factor in factors.items():
        out[name] = (out[name] * factor).astype(out[name].dtype)
    return out
```

```python
from contextlib import ExitStack

import concourse.bass as bass
from concourse import mybir

F32 = mybir.dt.float32
ALU = mybir.AluOpType
ACT = mybir.ActivationFunctionType
AX_X = mybir.AxisListType.X

P = 128
B = 8
S = 256
C = S // P
E = 128
H0, D0 = 16, 8
REL = 20
NREL = 2 * REL + 1
QI = P // H0
RT = S // QI
RTC = RT // C
PAIRS = RT // 2
L = 64
NE = 8
H1, D1 = 8, 16
HID = 176
REM = HID - P
NX = NE + 1
NR = (NX + 1) // 2
NCH = NX + NR
LN_EPS = 1e-5
RMS_EPS = 1e-6
NORM_GUARD = 1e-24 / E
DEN_GUARD = 1e-5
TOP_K = 2

W_COLS = [("ident", P), ("head_mask", H0), ("query_mask", QI), ("parity_mask", 2), ("earlier", NE * NE), ("half", P),
          ("WqT", E), ("WqT_dh", E), ("WkT", E), ("WvT", E), ("WoT", E),
          ("bq", 1), ("bk", 1), ("rk_first", 1), ("rk_last", 1),
          ("gamma1", 1), ("gamma2", 1), ("gamma3", 1), ("bdown", 1), ("b1", NCH), ("b3", NCH),
          ("fWq", E), ("fWdown", L), ("fWo", E), ("fWg", NE), ("fWe", NE * E),
          ("aWq", E), ("aWk", E), ("aWv", E), ("aWo", E), ("gateT", NE),
          ("W1", NCH * P), ("W3", NCH * P), ("W2main", NX * E), ("W2rem", NX * E)]
R_COLS = [("bq_dh", E), ("bv", E), ("bo", E), ("fbq", E), ("fbkv", 2 * E), ("fbo", E),
          ("fbg", NE), ("gate_b", NE)]


def offsets(cols):
    out, at = {}, 0
    for name, n in cols:
        out[name] = (at, n)
        at += n
    return out, at


W_AT, W_N = offsets(W_COLS)
R_AT, R_N = offsets(R_COLS)


def build(nc, x_in, wpack, rpack, fWup, b2, relkT, relv, out):
    ctx = ExitStack()
    with ctx:
        def sb(name, *shape):
            return ctx.enter_context(nc.sbuf_tensor(name, list(shape), F32))

        def sem(name, per):
            return ctx.enter_context(nc.semaphore(name)), per

        def view(t, off, dims, p0=0, np_=P):
            a = t[:]
            row = a.ap[0][0]
            return bass.AP(a.tensor, p0 * row + off, [[row, np_]] + [list(d) for d in dims])

        def wait(eng, signal, t, k):
            s, per = signal
            value = t * per + k
            if isinstance(value, int) and value <= 0:
                return
            eng.wait_ge(s, value)

        w = sb("w", P, W_N)
        r = sb("r", P, R_N)

        def wc(name, a=0, b=None, p0=0, p1=P):
            at, n = W_AT[name]
            return w[p0:p1, at + a:at + (n if b is None else b)]

        def rc(name):
            at, n = R_AT[name]
            return r[:, at:at + n]

        def rbc(name, copies):
            at, n = R_AT[name]
            return view(r, at, [[0, copies], [1, n]])

        ident = wc("ident")
        wup = sb("wup", L, 2 * E)
        b2s = sb("b2s", NX, E)
        expo = sb("expo", P, 8)
        half_root = sb("half_root", P, 1)
        TKN, TKP = 2 * S, 2 * S + QI
        ek = sb("ek", D0, TKP)
        tk = sb("tk", QI * D0, TKN)
        TVN = S + P
        ev = sb("ev", 1, (TVN + P) * D0)
        tv = sb("tv", P, TVN * D0)
        xin = sb("xin", P, C, E)
        xres = sb("xres", P, C, E)
        st_a, mv_a, ve_a, rs_a = sb("st_a", P, C, 6), sb("mv_a", P, C, 2), sb("ve_a", P, C), sb("rs_a", P, C)
        xn = sb("xn", P, C, E)
        xnT = sb("xnT", P, S)
        qT = sb("qT", P, S)
        kT3 = sb("kT3", P, 3, S)
        qdh = sb("qdh", P, C, E)
        v9 = sb("v9", P, C, H0, D0 + 1)
        qbd = sb("qbd", P, RT // 2, P)
        qr = sb("qr", QI * D0, RT, P)
        nmx = sb("nmx", P, RT)
        pm = sb("pm", P, 2, 2, S)
        pT = sb("pT", P, C, RT, P)
        rvm = sb("rvm", P, 512)
        w2 = sb("w2", P, RT, D0)
        relo = sb("relo", P, C, E)
        rden = sb("rden", P, C, H0)
        on = sb("on", P, C, E)
        onT = sb("onT", P, S)
        x1 = sb("x1", P, C, E)
        st_b, mv_b, ve_b, rs_b = sb("st_b", P, C, 6), sb("mv_b", P, C, 2), sb("ve_b", P, 2, C), sb("rs_b", P, 2, C)
        xl = sb("xl", P, C, E)
        hh = sb("hh", P, C, E)
        hT = sb("hT", P, S)
        h2 = h3 = xf = hh
        h2T = h3T = xfT = hT
        dT = sb("dT", L, S)
        q1 = sb("q1", P, C, E)
        kv1 = sb("kv1", P, C, 2 * E)
        prod = sb("prod", P, C, H0 * H0 * D0)
        lg = sb("lg", P, C, H0 * H0)
        lmx = sb("lmx", P, C, H0)
        lsum = sb("lsum", P, C, H0)
        at1 = sb("at1", P, C, E)
        atT = sb("atT", P, S)
        o3, o3T = at1, atT
        y = sb("y", P, C, E)
        ysq = sb("ysq", P, E)
        ss = sb("ss", P, C)
        gl = sb("gl", P, C, NE)
        gmx, gsum = sb("gmx", P, C), sb("gsum", P, C)
        x2 = sb("x2", P, C, E)
        q3 = sb("q3", P, 2, S)
        k3 = sb("k3", P, S)
        v17 = sb("v17", P, C, H1, D1 + 1)
        sq = prod[:].rearrange("p c (h q) -> p (c h) q", q=2 * S).rearrange("p h (c q) -> p h c q", c=C)
        den3 = sb("den3", P, C, H1)
        x3 = sb("x3", P, C, E)
        sc = sb("sc", P, C, NE)
        smx, ssum = sb("smx", P, C), sb("ssum", P, C)
        bi = sb("bi", P, C, NE)
        above, tied = sb("above", P, C, NE, NE), sb("tied", P, C, NE, NE)
        rank = sb("rank", P, C, NE)
        rw = sb("rw", P, C, NX)
        rwT = sb("rwT", NX, S)
        ha = sb("ha", P, 2, S)
        hu = sb("hu", P, NCH, S)
        ht = sb("ht", P, 2, S)
        xo = sb("xo", P, C, E)
        bank = [ctx.enter_context(nc.psum_tensor(f"bank{j}", [P, 512], F32)) for j in range(8)]
        b_s, b_t = bank[0:2], bank[2:4]
        b_rv, b_o = bank[4], bank[5]
        m0, m1 = bank[6], bank[7]
        d_qdh = nc.dram_tensor("d_qdh", [S, D0, H0], F32, kind="Internal").ap()
        d_w2 = nc.dram_tensor("d_w2", [RT, QI, H0, D0], F32, kind="Internal").ap()
        d_ev = nc.dram_tensor("d_ev", [TVN + P, D0], F32, kind="Internal").ap()

        w_in0, w_in1, r_in, small_in = (sem(n, 16) for n in ("w_in0", "w_in1", "r_in", "small_in"))
        rel_in, tk_in, ev_out, tv_in = (sem(n, 16) for n in ("rel_in", "tk_in", "ev_out", "tv_in"))
        zeroed, ones_set, rel_filled, w_folded = (sem(n, 1) for n in ("zeroed", "ones_set", "rel_filled", "w_folded"))
        x_loaded, xres_ready, ln_a, rstd_a, xn_ready = sem("x_loaded", 16), sem("xres_ready", 1), sem("ln_a", 5), sem("rstd_a", 1), sem("xn_ready", 1)
        xnT_ps, xnT_ready, qk_ps, v_ps = sem("xnT_ps", 1), sem("xnT_ready", 1), sem("qk_ps", 1), sem("v_ps", 1)
        qT_ready, kT_ready, kT3_ready, qdh_ready, v_ready = sem("qT_ready", 1), sem("kT_ready", 1), sem("kT3_ready", 1), sem("qdh_ready", 1), sem("v_ready", 1)
        qdh_out, qr_in, qbd_ready = sem("qdh_out", 16), sem("qr_in", 16 * QI), sem("qbd_ready", 4)
        s_ps, max_ready, exp_ready = sem("s_ps", PAIRS), sem("max_ready", PAIRS), sem("exp_ready", PAIRS)
        pT_ps, pT_even, pT_odd = sem("pT_ps", PAIRS), sem("pT_even", PAIRS // 2), sem("pT_odd", PAIRS // 2)
        rv_ps, rv_masked, rv_sum = sem("rv_ps", 4), sem("rv_masked", 4), sem("rv_sum", 4)
        w2_out, relo_in = sem("w2_out", 16), sem("relo_in", 16)
        o_ps, o_steps, on_ready = sem("o_ps", 1), sem("o_steps", 1), sem("on_ready", 1)
        onT_ps, onT_ready, wo_ps, x1_ready = sem("onT_ps", 1), sem("onT_ready", 1), sem("wo_ps", 1), sem("x1_ready", 1)
        ln_b, rstd_b, h_ready, hT_ps, hT_ready = sem("ln_b", 5), sem("rstd_b", 1), sem("h_ready", 1), sem("hT_ps", 1), sem("hT_ready", 1)
        qd_ps, dT_ready, q1_ready, kv_ps, kv_ready = sem("qd_ps", 1), sem("dT_ready", 1), sem("q1_ready", 1), sem("kv_ps", 1), sem("kv_ready", 1)
        xl_ready, res_b = sem("xl_ready", 1), sem("res_b", 1)
        qk_prod, qk_sum, l_max, l_sub, l_exp = sem("qk_prod", 2), sem("qk_sum", 2), sem("l_max", 1), sem("l_sub", 1), sem("l_exp", 1)
        l_sum, l_rec, pv_prod, pv_sum, at_ready = sem("l_sum", 1), sem("l_rec", 1), sem("pv_prod", 2), sem("pv_sum", 2), sem("at_ready", 1)
        atT_ps, atT_ready, fo_ps, y_ready = sem("atT_ps", 1), sem("atT_ready", 1), sem("fo_ps", 1), sem("y_ready", 1)
        y_sq, ss_eps, rstd_y, h2_ready = sem("y_sq", 2), sem("ss_eps", 1), sem("rstd_y", 1), sem("h2_ready", 1)
        h2T_ps, h2T_ready, g_ps = sem("h2T_ps", 1), sem("h2T_ready", 1), sem("g_ps", 1)
        g_steps, g_exp, gate_ready = sem("g_steps", 3), sem("g_exp", 1), sem("gate_ready", 3)
        we_ps, acc_e = sem("we_ps", 4), sem("acc_e", 2 * NE)
        x1_sum, x2_ready = sem("x1_sum", 1), sem("x2_ready", 1)
        ln_c, var_c, rstd_c, h3_ready = sem("ln_c", 5), sem("var_c", 2), sem("rstd_c", 1), sem("h3_ready", 1)
        h3T_ps, h3T_ready, qk3_ps, qk3_ready = sem("h3T_ps", 1), sem("h3T_ready", 1), sem("qk3_ps", 1), sem("qk3_ready", 1)
        v3_ps, v3_ready, s3_ps, sq_ready = sem("v3_ps", 1), sem("v3_ready", 1), sem("s3_ps", H1), sem("sq_ready", H1)
        o3_ps, o3_den, o3_ready, o3T_ps, o3T_ready = sem("o3_ps", 1), sem("o3_den", 2), sem("o3_ready", 1), sem("o3T_ps", 1), sem("o3T_ready", 1)
        ao_ps, x3_ready = sem("ao_ps", 1), sem("x3_ready", 1)
        ln_d, rstd_d, xf_ready, xfT_ps, xfT_ready = sem("ln_d", 5), sem("rstd_d", 1), sem("xf_ready", 1), sem("xfT_ps", 1), sem("xfT_ready", 1)
        r_ps, r_steps, r_exp, sc_steps, rw_ready = sem("r_ps", 1), sem("r_steps", 2), sem("r_exp", 1), sem("sc_steps", 8), sem("rw_ready", 1)
        rwT_ps, rwT_ready = sem("rwT_ps", 1), sem("rwT_ready", 1)
        ab_ps, a_ready, u_ready, tanh_ready, hid_ready = sem("ab_ps", NCH), sem("a_ready", NCH), sem("u_ready", NCH), sem("tanh_ready", NCH), sem("hid_ready", NCH)
        EG = 3
        eo_ps, eo_acc = sem("eo_ps", C * EG), sem("eo_acc", C * NX)
        stored = sem("stored", 16)

        block = ctx.enter_context(nc.Block())

        def turns(eng, body):
            body(0)
            with eng.Fori(1, B) as t:
                body(t)

        @block.sync
        def _(sp):
            n0 = W_AT["fWq"][0]
            sp.dma_start(w[:, 0:n0], wpack[:, 0:n0]).then_inc(w_in0[0], 16)
            sp.dma_start(xin[:], x_in[0].rearrange("(c p) e -> p c e", p=P)).then_inc(x_loaded[0], 16)
            sp.dma_start(w[:, n0:], wpack[:, n0:]).then_inc(w_in1[0], 16)
            sp.wait_ge(rel_filled[0], 1)
            for qi in range(QI):
                sp.dma_start(tk[qi * D0:(qi + 1) * D0, :], ek[:, QI - 1 - qi:QI - 1 - qi + TKN]).then_inc(tk_in[0], 16)
            sp.wait_ge(rel_filled[0], 2)
            sp.dma_start(d_ev.rearrange("m d -> (m d)").rearrange("(a n) -> a n", a=1), ev[:]).then_inc(ev_out[0], 16)
            sp.wait_ge(ev_out[0], 16)
            sp.dma_start(tv[:], bass.AP(d_ev.tensor, 0, [[D0, P], [1, TVN * D0]])).then_inc(tv_in[0], 16)

            def due(signal, t, k):
                value = t * signal[1] + k
                return signal[0], value if isinstance(value, int) else sp.snap(value)

            def met(mark):
                if not isinstance(mark[1], int) or mark[1] > 0:
                    sp.wait_ge(*mark)

            def body(t):
                queries, o_before = due(qdh_ready, t, 1), due(o_ps, t, 0)
                written = due(qdh_out, t, 16)
                rel_sums, rel_written, on_before = due(rv_sum, t, 4), due(w2_out, t, 16), due(on_ready, t, 0)
                if not isinstance(t, int):
                    xn_before, xres_before = due(xn_ready, t, 0), due(xres_ready, t, 0)
                    at = sp.snap(t * (S * E))
                    met(xn_before)
                    met(xres_before)
                    sp.dma_start(xin[:], bass.AP(x_in.tensor, at, [[E, P], [P * E, C], [1, E]])).then_inc(x_loaded[0], 16)
                met(queries)
                met(o_before)
                sp.dma_start(d_qdh.rearrange("(c p) d h -> p c (d h)", p=P), qdh[:]).then_inc(qdh_out[0], 16)
                met(written)
                for qi in range(QI):
                    dst = view(qr, qi * H0, [[P, RT], [1, H0]], qi * D0, D0)
                    src = d_qdh.rearrange("(r q) d h -> q d r h", q=QI)[qi]
                    sp.dma_start(dst, src).then_inc(qr_in[0], 16)
                met(rel_sums)
                met(on_before)
                sp.dma_start(d_w2.rearrange("r q h d -> (q h) r d"), w2[:]).then_inc(w2_out[0], 16)
                met(rel_written)
                sp.dma_start(relo[:], d_w2.rearrange("(c r) q h d -> (r q) c (h d)", c=C)).then_inc(relo_in[0], 16)

            turns(sp, body)
            sp.wait_ge(stored[0], 16 * B)

        @block.scalar
        def _(act):
            copy, idn, exp = ACT.Copy, ACT.Identity, ACT.Exp
            act.dma_start(r[:], rpack.partition_broadcast(P)).then_inc(r_in[0], 16)
            act.dma_start(ek[:, S - REL + QI - 1:S + REL + QI], relkT).then_inc(rel_in[0], 16)
            act.dma_start(ev[:, (S - 1 - REL) * D0:(S + REL) * D0], relv).then_inc(rel_in[0], 16)
            act.dma_start(wup[:], fWup).then_inc(small_in[0], 16)
            act.dma_start(b2s[:], b2).then_inc(small_in[0], 16)

            def evict(t, ps, k, done, src, dst, free=None):
                wait(act, ps, t, k)
                if free:
                    wait(act, *free)
                act.activation(dst, src, copy).then_inc(done[0], 1)

            def body(t):
                evict(t, xnT_ps, 1, xnT_ready, b_t[0][:, 0:S], xnT[:], (v_ps, t, 0))
                wait(act, qk_ps, t, 1)
                wait(act, qbd_ready, t, 0)
                act.activation(qT[:], b_t[1][:, 0:S], idn, bias=wc("bq")).then_inc(qT_ready[0], 1)
                wait(act, s_ps, t, 0)
                act.activation(kT3[:, 1, :], b_t[1][:, S:2 * S], idn, bias=wc("bk")).then_inc(kT_ready[0], 1)
                for p in range(PAIRS + 1):
                    if p < PAIRS:
                        wait(act, max_ready, t, p + 1)
                        wait(act, pT_ps, t, p - 1)
                        for j in range(2):
                            a = act.activation(pm[:, p % 2, j], b_s[p % 2][:, j * S:(j + 1) * S], exp,
                                               bias=nmx[:, 2 * p + j:2 * p + j + 1])
                        a.then_inc(exp_ready[0], 1)
                    if p >= 1 and (p - 1) % 2:
                        move_pT(t, p - 1)
                evict(t, onT_ps, 1, onT_ready, b_o[:, 0:S], onT[:], (wo_ps, t, 0))
                rest(t)

            def move_pT(t, p):
                wait(act, pT_ps, t, p + 1)
                if p < 2:
                    wait(act, o_ps, t, 0)
                src = view(b_t[p % 2], 0, [[P, 2], [2 * P, 2], [1, P]])
                dst = view(pT, 2 * p * P, [[RT * P, 2], [P, 2], [1, P]])
                act.activation(dst, src, copy).then_inc(pT_odd[0], 1)

            def rest(t):
                evict(t, hT_ps, 1, hT_ready, m0[:, 0:S], hT[:], (qd_ps, t, 0))
                wait(act, qd_ps, t, 1)
                wait(act, kv_ps, t, 0)
                act.activation(dT[:], m1[0:L, 0:S], idn, bias=wc("bdown", p1=L)).then_inc(dT_ready[0], 1)
                wait(act, l_sub, t, 1)
                act.activation(lg[:], lg[:], exp, scale=float(D0) ** -0.5).then_inc(l_exp[0], 1)
                evict(t, atT_ps, 1, atT_ready, m0[:, 0:S], atT[:], (fo_ps, t, 0))
                wait(act, y_ready, t, 1)
                for c in range(C):
                    wait(act, y_sq, t, c)
                    act.activation(ysq[:], y[:, c], ACT.Square, accum_out=ss[:, c:c + 1]).then_inc(y_sq[0], 1)
                evict(t, h2T_ps, 1, h2T_ready, m0[:, 0:S], h2T[:], (we_ps, t, 0))
                wait(act, g_steps, t, 3)
                act.activation(gl[:], gl[:], exp).then_inc(g_exp[0], 1)
                evict(t, h3T_ps, 1, h3T_ready, m0[:, 0:S], h3T[:], (v3_ps, t, 0))
                wait(act, qk3_ps, t, 1)
                wait(act, s3_ps, t, 0)
                act.activation(k3[:], m1[:, S:2 * S], copy)
                for j in range(2):
                    a = act.activation(q3[:, j], m1[:, 0:S], copy, scale=wc("parity_mask", j, j + 1))
                a.then_inc(qk3_ready[0], 1)
                wait(act, o3_ps, t, 0)
                for h in range(H1):
                    wait(act, s3_ps, t, h + 1)
                    act.activation(sq[:, h], (m0, m1)[h % 2][:], ACT.Square, scale=0.5 ** 0.5,
                                   bias=half_root[:]).then_inc(sq_ready[0], 1)
                evict(t, o3T_ps, 1, o3T_ready, m1[:, 0:S], o3T[:], (ao_ps, t, 0))
                evict(t, xfT_ps, 1, xfT_ready, m0[:, 0:S], xfT[:], (ab_ps, t, 0))
                wait(act, r_steps, t, 2)
                act.activation(sc[:], sc[:], exp).then_inc(r_exp[0], 1)
                for n in range(NCH + 1):
                    if n < NCH:
                        wait(act, ab_ps, t, n + 1)
                        wait(act, u_ready, t, n - 1)
                        act.activation(ha[:, n % 2], (m0, m1)[n % 2][:, 0:S], idn, scale=0.5,
                                       bias=wc("b1", n, n + 1)).then_inc(a_ready[0], 1)
                    if n:
                        wait(act, u_ready, t, n)
                        wait(act, hid_ready, t, n - 2)
                        act.activation(ht[:, (n - 1) % 2], hu[:, n - 1], ACT.Tanh).then_inc(tanh_ready[0], 1)
                evict(t, rwT_ps, 1, rwT_ready, m0[0:NX, 0:S], rwT[:], (eo_ps, t, 0))

            act.wait_ge(w_folded[0], 2)
            act.wait_ge(ones_set[0], 1)
            turns(act, body)

        @block.gpsimd
        def _(pool):
            g = nc.gpsimd
            g.memset(expo[:], -0.5)
            g.memset(half_root[:], 0.5 ** 0.5)
            g.memset(v9[:], 1.0)
            g.memset(v17[:], 1.0)
            g.memset(rw[:], 1.0)
            g.memset(qr[:], 0.0).then_inc(ones_set[0], 1)

            def body(t):
                wait(pool, x_loaded, t, 16)
                if isinstance(t, int):
                    pool.wait_ge(r_in[0], 16)
                wait(pool, x1_ready, t, 0)
                g.tensor_tensor(xres[:], xin[:], rbc("bo", C), ALU.add).then_inc(xres_ready[0], 1)
                wait(pool, ln_a, t, 5)
                wait(pool, xn_ready, t, 0)
                g.tensor_tensor(rs_a[:], ve_a[:], expo[:, 0:C], ALU.pow).then_inc(rstd_a[0], 1)
                wait(pool, qT_ready, t, 1)
                for k in range(4):
                    wait(pool, s_ps, t, 4 * (k - 1))
                    n = RT // 4
                    g.tensor_tensor(view(qbd, k % 2 * n * P, [[P, n], [H0, QI], [1, H0]]),
                                    view(qT, k * n * QI, [[QI, n], [1, QI], [0, H0]]),
                                    view(w, W_AT["head_mask"][0], [[0, n], [0, QI], [1, H0]]),
                                    ALU.mult).then_inc(qbd_ready[0], 1)
                wait(pool, ln_b, t, 5)
                wait(pool, h_ready, t, 0)
                g.tensor_tensor(rs_b[:], ve_b[:], view(expo, 0, [[0, 2], [1, C]]), ALU.pow).then_inc(rstd_b[0], 1)
                wait(pool, xl_ready, t, 1)
                wait(pool, y_ready, t, 0)
                g.tensor_tensor(xl[:], xl[:], rbc("fbo", C), ALU.add).then_inc(res_b[0], 1)
                wait(pool, ss_eps, t, 1)
                wait(pool, h2_ready, t, 0)
                g.tensor_tensor(rs_b[:, 0], ve_b[:, 0], expo[:, 0:C], ALU.pow).then_inc(rstd_y[0], 1)
                wait(pool, x3_ready, t, 0)
                g.tensor_tensor(x2[:], x1[:], y[:], ALU.add).then_inc(x1_sum[0], 1)
                wait(pool, var_c, t, 2)
                g.tensor_tensor(rs_b[:, 0], ve_b[:, 0], expo[:, 0:C], ALU.pow).then_inc(rstd_c[0], 1)
                wait(pool, ln_d, t, 5)
                g.tensor_tensor(rs_b[:, 0], ve_b[:, 0], expo[:, 0:C], ALU.pow).then_inc(rstd_d[0], 1)
                wait(pool, eo_acc, t, C * NX)
                pool.dma_start(out[t].rearrange("(c p) e -> p c e", p=P), xo[:]).then_inc(stored[0], 16)

            pool.wait_ge(w_in0[0], 16)
            pool.wait_ge(w_folded[0], 1)
            pool.wait_ge(ones_set[0], 1)
            turns(pool, body)

        @block.vector
        def _(dve):
            v = nc.vector
            scale0 = float(D0) ** -0.5
            dve.wait_ge(rel_in[0], 32)
            lo, hi = S - REL + QI - 1, S + REL + QI
            v.tensor_copy(view(ek, 0, [[1, lo]], 0, D0), view(ek, lo, [[0, lo]], 0, D0))
            v.tensor_copy(view(ek, hi, [[1, TKP - hi]], 0, D0), view(ek, hi - 1, [[0, TKP - hi]], 0, D0)).then_inc(rel_filled[0], 1)
            lo, hi = S - 1 - REL, S + REL
            v.tensor_copy(view(ev, 0, [[D0, lo], [1, D0]], 0, 1), view(ev, lo * D0, [[0, lo], [1, D0]], 0, 1))
            v.tensor_copy(view(ev, hi * D0, [[D0, TVN + P - hi], [1, D0]], 0, 1),
                          view(ev, (hi - 1) * D0, [[0, TVN + P - hi], [1, D0]], 0, 1)).then_inc(rel_filled[0], 1)
            dve.wait_ge(w_in0[0], 16)
            dve.wait_ge(r_in[0], 16)
            for n in ("WqT", "WqT_dh", "bq"):
                v.tensor_scalar(wc(n), wc(n), scale0, None, ALU.mult)
            v.tensor_scalar(rc("bq_dh"), rc("bq_dh"), scale0, None, ALU.mult).then_inc(w_folded[0], 1)
            dve.wait_ge(w_in1[0], 16)
            for n, gain in (("fWq", "gamma1"), ("fWdown", "gamma1"), ("fWg", "gamma2"), ("fWe", "gamma2"),
                            ("aWq", "gamma3"), ("aWk", "gamma3"), ("aWv", "gamma3")):
                v.tensor_scalar(wc(n), wc(n), wc(gain), None, ALU.mult)
            v.tensor_scalar(wc("b1"), wc("b1"), 0.5, None, ALU.mult).then_inc(w_folded[0], 1)
            dve.wait_ge(w_folded[0], 2)
            dve.wait_ge(ones_set[0], 1)

            def moments(t, src, st, mv, ve, steps):
                for c in range(C):
                    a = v.bn_stats(st[:, c], src[:, c])
                a.then_inc(steps[0], 1)
                wait(dve, steps, t, 1)
                v.tensor_tensor(mv[:], st[:, :, 1:3], st[:, :, 4:6], ALU.add)
                v.tensor_tensor(st[:, :, 0], st[:, :, 1], st[:, :, 4], ALU.subtract).then_inc(steps[0], 1)
                wait(dve, steps, t, 2)
                v.tensor_scalar(mv[:, :, 0], mv[:, :, 0], 0.5, None, ALU.mult)
                v.scalar_tensor_tensor(st[:, :, 3], st[:, :, 0], E / 4, st[:, :, 0], ALU.mult, ALU.mult).then_inc(steps[0], 1)
                wait(dve, steps, t, 3)
                v.tensor_tensor(mv[:, :, 1], mv[:, :, 1], st[:, :, 3], ALU.add).then_inc(steps[0], 1)
                wait(dve, steps, t, 4)
                return v.tensor_scalar(ve, mv[:, :, 1], 1 / E, LN_EPS, ALU.mult, ALU.add)

            def normed(dst, src, mv, rs):
                for c in range(C):
                    a = v.tensor_scalar(dst[:, c], src[:, c], mv[:, c, 0:1], rs[:, c:c + 1], ALU.subtract, ALU.mult)
                return a

            def body(t):
                wait(dve, x_loaded, t, 16)
                moments(t, xin, st_a, mv_a, ve_a[:], ln_a).then_inc(ln_a[0], 1)
                wait(dve, rstd_a, t, 1)
                wait(dve, xnT_ps, t, 0)
                normed(xn, xin, mv_a, rs_a).then_inc(xn_ready[0], 1)
                wait(dve, kT_ready, t, 1)
                v.tensor_scalar(kT3[:, 0], kT3[:, 1], wc("rk_first"), None, ALU.add)
                v.tensor_scalar(kT3[:, 2], kT3[:, 1], wc("rk_last"), None, ALU.add).then_inc(kT3_ready[0], 1)
                wait(dve, v_ps, t, 1)
                wait(dve, qdh_out, t, 0)
                v.tensor_tensor(qdh[:], b_o[:, 0:C * E].rearrange("p (c e) -> p c e", c=C), rbc("bq_dh", C), ALU.add).then_inc(qdh_ready[0], 1)
                wait(dve, o_ps, t, 0)
                for c in range(C):
                    a = v.tensor_tensor(v9[:, c, :, 0:D0],
                                        view(b_rv, c * E, [[D0, H0], [1, D0]]),
                                        view(r, R_AT["bv"][0], [[D0, H0], [1, D0]]), ALU.add)
                a.then_inc(v_ready[0], 1)
                for p in range(PAIRS + 3):
                    if p < PAIRS:
                        wait(dve, s_ps, t, p + 1)
                        wait(dve, exp_ready, t, 0)
                        v.tensor_reduce(nmx[:, 2 * p:2 * p + 2], b_s[p % 2][:].rearrange("p (j k) -> p j k", j=2),
                                        AX_X, ALU.max, negate=True).then_inc(max_ready[0], 1)
                    if 1 <= p <= PAIRS and (p - 1) % 2 == 0:
                        q = p - 1
                        wait(dve, pT_ps, t, q + 1)
                        if q < 2:
                            wait(dve, o_ps, t, 0)
                            wait(dve, rv_ps, t, 0)
                        v.tensor_copy(view(pT, 2 * q * P, [[RT * P, 2], [P, 2], [1, P]]),
                                      view(b_t[q % 2], 0, [[P, 2], [2 * P, 2], [1, P]])).then_inc(pT_even[0], 1)
                    if p >= 6 and (p - 6) % 4 == 0 or p == PAIRS + 2:
                        rel_values(t, (p - 6) // 4)
                wait(dve, o_ps, t, 1)
                o4 = [view(b_o, c * 256, [[D0 + 1, H0], [1, D0]]) for c in range(C)]
                wait(dve, on_ready, t, 0)
                v.reciprocal(rden[:], view(b_o, D0, [[256, C], [D0 + 1, H0]]))
                wait(dve, relo_in, t, 16)
                for c in range(C):
                    a = v.tensor_tensor(view(on, c * E, [[D0, H0], [1, D0]]), o4[c], view(relo, c * E, [[D0, H0], [1, D0]]), ALU.add)
                a.then_inc(o_steps[0], 1)
                wait(dve, o_steps, t, 1)
                wait(dve, onT_ps, t, 0)
                v.tensor_tensor(view(on, 0, [[E, C], [D0, H0], [1, D0]]), view(on, 0, [[E, C], [D0, H0], [1, D0]]),
                                view(rden, 0, [[H0, C], [1, H0], [0, D0]]), ALU.mult).then_inc(on_ready[0], 1)
                wait(dve, wo_ps, t, 1)
                wait(dve, xres_ready, t, 1)
                wait(dve, x1_sum, t, 0)
                v.tensor_tensor(x1[:], b_rv[:, 0:C * E].rearrange("p (c e) -> p c e", c=C), xres[:], ALU.add).then_inc(x1_ready[0], 1)
                wait(dve, x1_ready, t, 1)
                rest(t)

            def rel_values(t, k):
                wait(dve, rv_ps, t, k + 1)
                wait(dve, rv_sum, t, k)
                v.tensor_tensor(rvm[:].rearrange("p (r q d) -> p r q d", r=8, q=QI),
                                b_rv[:].rearrange("p (r q d) -> p r q d", r=8, q=QI),
                                view(w, W_AT["query_mask"][0], [[0, 8], [1, QI], [0, D0]]), ALU.mult).then_inc(rv_masked[0], 1)
                wait(dve, rv_masked, t, k + 1)
                if k == 0:
                    wait(dve, w2_out, t, 0)
                v.tensor_reduce(w2[:, 8 * k:8 * k + 8, :], view(rvm, 0, [[QI * D0, 8], [1, D0], [D0, QI]]), AX_X, ALU.add).then_inc(rv_sum[0], 1)

            def rest(t):
                moments(t, x1, st_b, mv_b, ve_b[:, 0], ln_b)
                v.tensor_scalar(ve_b[:, 1], mv_b[:, :, 1], (1.0 + RMS_EPS) / E, LN_EPS * RMS_EPS, ALU.mult, ALU.add).then_inc(ln_b[0], 1)
                wait(dve, rstd_b, t, 1)
                normed(xl, x1, mv_b, rs_b[:, 0]).then_inc(xl_ready[0], 1)
                wait(dve, hT_ps, t, 0)
                normed(hh, x1, mv_b, rs_b[:, 1]).then_inc(h_ready[0], 1)
                wait(dve, qd_ps, t, 1)
                v.tensor_tensor(q1[:], m0[:, 0:S].rearrange("p (c e) -> p c e", c=C), rbc("fbq", C), ALU.add).then_inc(q1_ready[0], 1)
                wait(dve, kv_ps, t, 1)
                v.tensor_tensor(kv1[:], m1[:].rearrange("p (c e) -> p c e", c=C), rbc("fbkv", C), ALU.add).then_inc(kv_ready[0], 1)
                wait(dve, kv_ready, t, 1)
                HH = H0 * H0
                for c in range(C):
                    wait(dve, qk_sum, t, c)
                    v.tensor_tensor(view(prod, c * HH * D0, [[H0 * D0, H0], [D0, H0], [1, D0]]),
                                    view(q1, c * E, [[D0, H0], [0, H0], [1, D0]]),
                                    view(kv1, c * 2 * E, [[0, H0], [D0, H0], [1, D0]]), ALU.mult).then_inc(qk_prod[0], 1)
                    wait(dve, qk_prod, t, c + 1)
                    v.tensor_reduce(lg[:, c], view(prod, c * HH * D0, [[D0, HH], [1, D0]]), AX_X, ALU.add).then_inc(qk_sum[0], 1)
                wait(dve, qk_sum, t, C)
                v.tensor_reduce(lmx[:], view(lg, 0, [[H0, C * H0], [1, H0]]), AX_X, ALU.max).then_inc(l_max[0], 1)
                wait(dve, l_max, t, 1)
                v.tensor_tensor(view(lg, 0, [[H0, C * H0], [1, H0]]), view(lg, 0, [[H0, C * H0], [1, H0]]),
                                view(lmx, 0, [[1, C * H0], [0, H0]]), ALU.subtract).then_inc(l_sub[0], 1)
                wait(dve, l_exp, t, 1)
                v.tensor_reduce(lsum[:], view(lg, 0, [[H0, C * H0], [1, H0]]), AX_X, ALU.add).then_inc(l_sum[0], 1)
                wait(dve, l_sum, t, 1)
                v.reciprocal(lsum[:], lsum[:]).then_inc(l_rec[0], 1)
                for c in range(C):
                    v.tensor_tensor(view(prod, c * HH * D0, [[H0 * D0, H0], [H0, D0], [1, H0]]),
                                    view(lg, c * HH, [[H0, H0], [0, D0], [1, H0]]),
                                    view(kv1, c * 2 * E + E, [[0, H0], [H0, D0], [1, H0]]), ALU.mult).then_inc(pv_prod[0], 1)
                    wait(dve, pv_prod, t, c + 1)
                    v.tensor_reduce(at1[:, c], view(prod, c * HH * D0, [[H0, E], [1, H0]]), AX_X, ALU.add).then_inc(pv_sum[0], 1)
                wait(dve, pv_sum, t, C)
                wait(dve, l_rec, t, 1)
                wait(dve, atT_ps, t, 0)
                v.tensor_tensor(view(at1, 0, [[D0, C * H0], [1, D0]]), view(at1, 0, [[D0, C * H0], [1, D0]]),
                                view(lsum, 0, [[1, C * H0], [0, D0]]), ALU.mult).then_inc(at_ready[0], 1)
                wait(dve, fo_ps, t, 1)
                wait(dve, res_b, t, 1)
                v.tensor_tensor(y[:], m1[:, 0:S].rearrange("p (c e) -> p c e", c=C), xl[:], ALU.add).then_inc(y_ready[0], 1)
                wait(dve, y_sq, t, 2)
                v.tensor_scalar(ve_b[:, 0], ss[:], 1.0 / E, RMS_EPS, ALU.mult, ALU.add).then_inc(ss_eps[0], 1)
                wait(dve, rstd_y, t, 1)
                wait(dve, h2T_ps, t, 0)
                for c in range(C):
                    a = v.tensor_scalar(h2[:, c], y[:, c], rs_b[:, 0, c:c + 1], None, ALU.mult)
                a.then_inc(h2_ready[0], 1)
                wait(dve, g_ps, t, 1)
                v.tensor_tensor(gl[:], m1[:, 0:C * NE].rearrange("p (c e) -> p c e", c=C), rbc("fbg", C), ALU.add).then_inc(g_steps[0], 1)
                wait(dve, g_steps, t, 1)
                v.tensor_reduce(gmx[:], gl[:], AX_X, ALU.max).then_inc(g_steps[0], 1)
                wait(dve, g_steps, t, 2)
                v.tensor_tensor(gl[:], gl[:], view(gmx, 0, [[1, C], [0, NE]]), ALU.subtract).then_inc(g_steps[0], 1)
                wait(dve, g_exp, t, 1)
                v.tensor_reduce(gsum[:], gl[:], AX_X, ALU.add).then_inc(gate_ready[0], 1)
                wait(dve, gate_ready, t, 1)
                v.reciprocal(gsum[:], gsum[:]).then_inc(gate_ready[0], 1)
                wait(dve, gate_ready, t, 2)
                v.tensor_tensor(gl[:], gl[:], view(gsum, 0, [[1, C], [0, NE]]), ALU.mult).then_inc(gate_ready[0], 1)
                wait(dve, gate_ready, t, 3)
                wait(dve, x1_sum, t, 1)
                for c in range(C):
                    for half in range(2):
                        wait(dve, we_ps, t, 2 * c + half + 1)
                        for e in range(4):
                            n = (c * 2 + half) * 4 + e
                            ee = half * 4 + e
                            if ee:
                                wait(dve, acc_e, t, n)
                            v.scalar_tensor_tensor(x2[:, c], (m0, m1)[half][:, e * E:(e + 1) * E], gl[:, c, ee:ee + 1], x2[:, c],
                                                   ALU.mult, ALU.add).then_inc(acc_e[0], 1)
                wait(dve, acc_e, t, 2 * NE)
                moments(t, x2, st_b, mv_b, ve_b[:, 0], ln_c).then_inc(ln_c[0], 1)
                wait(dve, ln_c, t, 5)
                v.tensor_scalar(ve_b[:, 1], ve_b[:, 0], NORM_GUARD, None, ALU.mult).then_inc(var_c[0], 1)
                wait(dve, var_c, t, 1)
                v.scalar_tensor_tensor(ve_b[:, 0], mv_b[:, :, 1], 1 / E, ve_b[:, 1], ALU.mult, ALU.max).then_inc(var_c[0], 1)
                wait(dve, rstd_c, t, 1)
                wait(dve, h3T_ps, t, 0)
                normed(h3, x2, mv_b, rs_b[:, 0]).then_inc(h3_ready[0], 1)
                wait(dve, v3_ps, t, 1)
                for c in range(C):
                    a = v.tensor_copy(v17[:, c, :, 0:D1], view(m0, c * E, [[D1, H1], [1, D1]]))
                a.then_inc(v3_ready[0], 1)
                wait(dve, o3_ps, t, 1)
                v.tensor_scalar(den3[:], view(m0, D1, [[256, C], [D1 + 1, H1]]), DEN_GUARD, None, ALU.max).then_inc(o3_den[0], 1)
                wait(dve, o3_den, t, 1)
                v.reciprocal(den3[:], den3[:]).then_inc(o3_den[0], 1)
                wait(dve, o3_den, t, 2)
                wait(dve, o3T_ps, t, 0)
                v.tensor_tensor(view(o3, 0, [[E, C], [D1, H1], [1, D1]]), view(m0, 0, [[256, C], [D1 + 1, H1], [1, D1]]),
                                view(den3, 0, [[H1, C], [1, H1], [0, D1]]), ALU.mult).then_inc(o3_ready[0], 1)
                wait(dve, ao_ps, t, 1)
                v.tensor_tensor(x3[:], m0[:, 0:S].rearrange("p (c e) -> p c e", c=C), x2[:], ALU.add).then_inc(x3_ready[0], 1)
                wait(dve, x3_ready, t, 1)
                moments(t, x3, st_b, mv_b, ve_b[:, 0], ln_d).then_inc(ln_d[0], 1)
                wait(dve, rstd_d, t, 1)
                wait(dve, xfT_ps, t, 0)
                normed(xf, x3, mv_b, rs_b[:, 0]).then_inc(xf_ready[0], 1)
                wait(dve, r_ps, t, 1)
                lgt = m1[:, 0:C * NE].rearrange("p (c e) -> p c e", c=C)
                v.tensor_reduce(smx[:], lgt, AX_X, ALU.max).then_inc(r_steps[0], 1)
                wait(dve, r_steps, t, 1)
                v.tensor_tensor(sc[:], lgt, view(smx, 0, [[1, C], [0, NE]]), ALU.subtract).then_inc(r_steps[0], 1)
                wait(dve, r_exp, t, 1)
                v.tensor_reduce(ssum[:], sc[:], AX_X, ALU.add).then_inc(sc_steps[0], 1)
                wait(dve, sc_steps, t, 1)
                v.reciprocal(ssum[:], ssum[:]).then_inc(sc_steps[0], 1)
                wait(dve, sc_steps, t, 2)
                v.tensor_tensor(sc[:], sc[:], view(ssum, 0, [[1, C], [0, NE]]), ALU.mult).then_inc(sc_steps[0], 1)
                wait(dve, sc_steps, t, 3)
                v.tensor_tensor(bi[:], sc[:], rbc("gate_b", C), ALU.add).then_inc(sc_steps[0], 1)
                wait(dve, sc_steps, t, 4)
                mine = view(bi, 0, [[NE, C], [1, NE], [0, NE]])
                others = view(bi, 0, [[NE, C], [0, NE], [1, NE]])
                v.tensor_tensor(above[:], others, mine, ALU.is_gt)
                v.tensor_tensor(tied[:], others, mine, ALU.is_equal).then_inc(sc_steps[0], 1)
                wait(dve, sc_steps, t, 5)
                v.tensor_tensor(tied[:], tied[:], view(w, W_AT["earlier"][0], [[0, C], [NE, NE], [1, NE]]), ALU.mult).then_inc(sc_steps[0], 1)
                wait(dve, sc_steps, t, 6)
                v.tensor_tensor(above[:], above[:], tied[:], ALU.add).then_inc(sc_steps[0], 1)
                wait(dve, sc_steps, t, 7)
                v.tensor_reduce(rank[:], above[:], AX_X, ALU.add).then_inc(sc_steps[0], 1)
                wait(dve, sc_steps, t, 8)
                wait(dve, rwT_ps, t, 0)
                v.scalar_tensor_tensor(rw[:, :, 0:NE], rank[:], TOP_K - 0.5, sc[:], ALU.is_lt, ALU.mult).then_inc(rw_ready[0], 1)
                wait(dve, eo_ps, t, 0)
                for n in range(NCH + 2):
                    if n < NCH:
                        wait(dve, a_ready, t, n + 1)
                        v.scalar_tensor_tensor(hu[:, n], (m0, m1)[n % 2][:, S:2 * S], wc("b3", n, n + 1), ha[:, n % 2],
                                               ALU.add, ALU.mult).then_inc(u_ready[0], 1)
                    if n >= 2:
                        wait(dve, tanh_ready, t, n - 1)
                        v.scalar_tensor_tensor(hu[:, n - 2], ht[:, n % 2], 1.0, hu[:, n - 2], ALU.add, ALU.mult).then_inc(hid_ready[0], 1)
                wait(dve, rw_ready, t, 1)
                wait(dve, stored, t, 0)
                done = 0
                for c in range(C):
                    for g in range(EG):
                        gi = c * EG + g
                        src = (m1, m0)[gi % 2]
                        wait(dve, eo_ps, t, gi + 1)
                        if g == 0:
                            v.tensor_tensor(xo[:, c], src[:, 0:E], x3[:, c], ALU.add).then_inc(eo_acc[0], 1)
                            done += 1
                            continue
                        for j in range(4):
                            e = (g - 1) * 4 + j
                            wait(dve, eo_acc, t, done)
                            v.scalar_tensor_tensor(xo[:, c], src[:, j * E:(j + 1) * E], rw[:, c, e:e + 1], xo[:, c],
                                                   ALU.mult, ALU.add).then_inc(eo_acc[0], 1)
                            done += 1

            turns(dve, body)

        @block.tensor
        def _(pe):
            mm = nc.tensor.matmul

            def turned(bank_, src):
                for c in range(C):
                    a = nc.tensor.transpose(bank_[:, c * P:(c + 1) * P], src[:, c], ident)
                return a

            def chunk(ap, c):
                return ap[:, c * P:(c + 1) * P]

            def pT_wait(t, p):
                if p % 2:
                    wait(pe, pT_odd, t, p // 2 + 1)
                else:
                    wait(pe, pT_even, t, p // 2 + 1)

            def body(t):
                wait(pe, xn_ready, t, 1)
                pT_wait(t, -2)
                turned(b_t[0], xn).then_inc(xnT_ps[0], 1)
                wait(pe, xnT_ready, t, 1)
                pT_wait(t, -1)
                mm(b_t[1][:, 0:S], wc("WqT"), xnT[:], start=True, stop=True)
                mm(b_t[1][:, S:2 * S], wc("WkT"), xnT[:], start=True, stop=True).then_inc(qk_ps[0], 1)
                wait(pe, onT_ready, t, 0)
                wait(pe, x1_ready, t, 0)
                for c in range(C):
                    mm(chunk(b_o, c), chunk(xnT, c), wc("WqT_dh"), start=True, stop=True)
                    a = mm(chunk(b_rv, c), chunk(xnT, c), wc("WvT"), start=True, stop=True)
                a.then_inc(v_ps[0], 1)
                wait(pe, kT3_ready, t, 1)
                wait(pe, qr_in, t, 16 * QI)
                if isinstance(t, int):
                    pe.wait_ge(tk_in[0], 16 * QI)
                    pe.wait_ge(tv_in[0], 16)
                for p in range(PAIRS + 3):
                    if p < PAIRS:
                        scores(t, p)
                    if 1 <= p <= PAIRS:
                        turn_weights(t, p - 1)
                    if p >= 3:
                        relative_values(t, p - 3)
                wait(pe, qdh_ready, t, 1)
                for c in range(C):
                    for h in range(H0):
                        at = c * 256 + h * (D0 + 1)
                        for kc in range(C):
                            a = mm(b_o[:, at:at + D0 + 1], view(pT, (kc * RT + c * RTC) * P + h, [[H0, P]]),
                                   v9[:, kc, h], start=kc == 0, stop=kc == C - 1)
                a.then_inc(o_ps[0], 1)
                wait(pe, on_ready, t, 1)
                turned(b_o, on).then_inc(onT_ps[0], 1)
                wait(pe, onT_ready, t, 1)
                for c in range(C):
                    a = mm(chunk(b_rv, c), chunk(onT, c), wc("WoT"), start=True, stop=True)
                a.then_inc(wo_ps[0], 1)
                if isinstance(t, int):
                    pe.wait_ge(w_folded[0], 2)
                    pe.wait_ge(small_in[0], 32)
                rest(t)

            def scores(t, p):
                wait(pe, exp_ready, t, p - 1)
                if p % 4 == 0:
                    wait(pe, qbd_ready, t, p // 4 + 1)
                for j in range(2):
                    i = 2 * p + j
                    q0 = i * QI
                    lo, hi = max(0, q0 - REL + 1), min(S, q0 + QI - 1 + REL)
                    first = True
                    for n, (a, b) in enumerate(((0, lo), (lo, hi), (hi, S))):
                        if a < b:
                            mm(b_s[p % 2][:, j * S + a:j * S + b], qbd[:, i % (RT // 2)], kT3[:, n, a:b], start=first,
                               stop=n != 1, skip_group_check=True)
                            first = False
                    a = mm(b_s[p % 2][:, j * S + lo:j * S + hi], qr[:, i],
                           tk[:, S - q0 + lo:S - q0 + hi], start=False, stop=True, skip_group_check=True)
                a.then_inc(s_ps[0], 1)

            def turn_weights(t, p):
                wait(pe, exp_ready, t, p + 1)
                pT_wait(t, p - 2)
                if p == 1:
                    wait(pe, kT_ready, t, 1)
                for j in range(2):
                    for kc in range(C):
                        a = nc.tensor.transpose(b_t[p % 2][:, (j * 2 + kc) * P:(j * 2 + kc + 1) * P],
                                                chunk(pm[:, p % 2, j], kc), ident)
                a.then_inc(pT_ps[0], 1)

            def relative_values(t, p):
                pT_wait(t, p)
                if p % 4 == 0:
                    wait(pe, rv_masked, t, p // 4)
                    wait(pe, v_ready, t, 1)
                for j in range(2):
                    i = 2 * p + j
                    at = i % 8 * QI * D0
                    for kc in range(C):
                        q = (TVN - QI - (i * QI + P - kc * P)) * D0
                        a = mm(b_rv[:, at:at + QI * D0], pT[:, kc, i], tv[:, q:q + QI * D0], start=kc == 0, stop=kc == C - 1)
                if p % 4 == 3:
                    a.then_inc(rv_ps[0], 1)

            def rest(t):
                wait(pe, h_ready, t, 1)
                wait(pe, eo_acc, t, 0)
                turned(m0, hh).then_inc(hT_ps[0], 1)
                wait(pe, hT_ready, t, 1)
                for c in range(C):
                    mm(chunk(m0, c), chunk(hT, c), wc("fWq"), start=True, stop=True)
                mm(m1[0:L, 0:S], wc("fWdown"), hT[:], start=True, stop=True).then_inc(qd_ps[0], 1)
                wait(pe, dT_ready, t, 1)
                for c in range(C):
                    a = mm(m1[:, c * S:(c + 1) * S], chunk(dT, c), wup[:], start=True, stop=True)
                a.then_inc(kv_ps[0], 1)
                wait(pe, at_ready, t, 1)
                turned(m0, at1).then_inc(atT_ps[0], 1)
                wait(pe, atT_ready, t, 1)
                for c in range(C):
                    a = mm(chunk(m1, c), chunk(atT, c), wc("fWo"), start=True, stop=True)
                a.then_inc(fo_ps[0], 1)
                wait(pe, h2_ready, t, 1)
                turned(m0, h2).then_inc(h2T_ps[0], 1)
                wait(pe, h2T_ready, t, 1)
                for c in range(C):
                    a = mm(m1[:, c * NE:(c + 1) * NE], chunk(h2T, c), wc("fWg"), start=True, stop=True)
                a.then_inc(g_ps[0], 1)
                for n in range(2 * C):
                    c, half = n // 2, n % 2
                    if n == 1:
                        wait(pe, g_steps, t, 1)
                    if n >= 2:
                        wait(pe, acc_e, t, 4 * (n - 1))
                    mm((m0, m1)[half][:], chunk(h2T, c), wc("fWe", half * 512, half * 512 + 512), start=True, stop=True).then_inc(we_ps[0], 1)
                wait(pe, h3_ready, t, 1)
                turned(m0, h3).then_inc(h3T_ps[0], 1)
                wait(pe, h3T_ready, t, 1)
                mm(m1[:, 0:S], wc("aWq"), h3T[:], start=True, stop=True)
                mm(m1[:, S:2 * S], wc("aWk"), h3T[:], start=True, stop=True).then_inc(qk3_ps[0], 1)
                for c in range(C):
                    a = mm(chunk(m0, c), chunk(h3T, c), wc("aWv"), start=True, stop=True)
                a.then_inc(v3_ps[0], 1)
                wait(pe, v3_ready, t, 1)
                wait(pe, qk3_ready, t, 1)
                for h in range(H1):
                    wait(pe, sq_ready, t, h - 1)
                    p0 = 2 * D1 * (h // 2)
                    for kc in range(C):
                        a = mm((m0, m1)[h % 2][:, kc * S:(kc + 1) * S], k3[p0:p0 + 2 * D1, kc * P:(kc + 1) * P],
                               q3[p0:p0 + 2 * D1, h % 2], start=True, stop=True)
                    a.then_inc(s3_ps[0], 1)
                wait(pe, sq_ready, t, H1)
                for c in range(C):
                    for kc in range(C):
                        mm(m0[:, c * 256:c * 256 + H1 * (D1 + 1)], wc("half"), v17[:, kc], start=c == 0 and kc == 0,
                           stop=False, skip_group_check=True)
                    for h in range(H1):
                        at = c * 256 + h * (D1 + 1)
                        for kc in range(C):
                            a = mm(m0[:, at:at + D1 + 1], chunk(sq[:, h, kc], c), v17[:, kc, h], start=False,
                                   stop=kc == C - 1, skip_group_check=True)
                a.then_inc(o3_ps[0], 1)
                wait(pe, o3_ready, t, 1)
                turned(m1, o3).then_inc(o3T_ps[0], 1)
                wait(pe, o3T_ready, t, 1)
                for c in range(C):
                    a = mm(chunk(m0, c), chunk(o3T, c), wc("aWo"), start=True, stop=True)
                a.then_inc(ao_ps[0], 1)
                wait(pe, xf_ready, t, 1)
                turned(m0, xf).then_inc(xfT_ps[0], 1)
                wait(pe, xfT_ready, t, 1)
                for c in range(C):
                    a = mm(m1[:, c * NE:(c + 1) * NE], chunk(xfT, c), wc("gateT"), start=True, stop=True)
                a.then_inc(r_ps[0], 1)
                for n in range(NCH):
                    if n == 1:
                        wait(pe, r_steps, t, 2)
                    wait(pe, u_ready, t, n - 1)
                    bk = (m0, m1)[n % 2]
                    mm(bk[:, 0:S], wc("W1", n * P, n * P + P), xfT[:], start=True, stop=True)
                    mm(bk[:, S:2 * S], wc("W3", n * P, n * P + P), xfT[:], start=True, stop=True).then_inc(ab_ps[0], 1)
                wait(pe, rw_ready, t, 1)
                wait(pe, u_ready, t, NCH - 1)
                for c in range(C):
                    a = nc.tensor.transpose(m0[0:NX, c * P:(c + 1) * P], rw[:, c], ident)
                a.then_inc(rwT_ps[0], 1)
                wait(pe, hid_ready, t, NCH)
                for gi in range(C * EG):
                    c, g = gi // EG, gi % EG
                    dst = (m1, m0)[gi % 2]
                    if gi == 0:
                        wait(pe, u_ready, t, NCH)
                    if gi <= 1:
                        wait(pe, rwT_ready, t, 1)
                    if gi >= 2:
                        done = sum((1, 4, 4)[x % EG] for x in range(gi - 1))
                        wait(pe, eo_acc, t, done)
                    for j, e in enumerate([NE] if g == 0 else range((g - 1) * 4, g * 4)):
                        o = dst[:, j * E:(j + 1) * E]
                        if g == 0:
                            mm(o, chunk(rwT, c), b2s[:], start=True, stop=False)
                        mm(o, chunk(hu[:, e], c), wc("W2main", e * E, e * E + E), start=g != 0, stop=False)
                        a = mm(o, chunk(hu[:, NX + e // 2], c), wc("W2rem", e * E, e * E + E), start=False, stop=True)
                    a.then_inc(eo_ps[0], 1)

            pe.wait_ge(w_in0[0], 16)
            pe.wait_ge(w_folded[0], 1)
            turns(pe, body)


def kernel(**inputs):
    import numpy as np
    import concourse.bacc as bacc
    from concourse.bass_utils import run_bass_kernel_spmd

    a = {k: np.asarray(x) for k, x in inputs.items()}
    f = np.float32
    col = lambda x: x.reshape(-1, 1)

    def tall(x):
        return np.concatenate([x, np.zeros((P - x.shape[0], x.shape[1]), f)])

    def by_chunk(first, last):
        allx = np.concatenate([first, last[..., None, :]], -2)
        out = np.zeros((*allx.shape[:-2], NCH, P), f)
        out[..., :NX, :] = allx[..., :P]
        for e in range(NX):
            out[..., NX + e // 2, e % 2 * 64:e % 2 * 64 + REM] = allx[..., e, P:]
        return out

    i = np.arange(P)
    w2_all = np.concatenate([a["L1_ffn_w2"], a["L1_ffn_sw2"][None]])
    w2_rem = np.zeros((P, NX, E), f)
    for e in range(NX):
        w2_rem[e % 2 * 64:e % 2 * 64 + REM, e] = w2_all[e, P:]
    kvf = a["L0_ffn_Wup"].reshape(L, H0, 2, D0)
    bkv = a["L0_ffn_bup"].reshape(H0, 2, D0)
    WqT = a["L0_attn_Wq"].T
    dh = lambda x: x.reshape(-1, H0, D0).transpose(0, 2, 1).reshape(-1, E)
    parts = {
        "ident": np.eye(P, dtype=f),
        "head_mask": (i[:, None] // D0 == np.arange(H0)).astype(f),
        "query_mask": (i[:, None] // H0 == QI - 1 - np.arange(QI)).astype(f),
        "parity_mask": (i[:, None] // D1 % 2 == np.arange(2)).astype(f) * f(D1 ** -0.5),
        "earlier": np.broadcast_to(np.tril(np.ones((NE, NE), f), -1).reshape(1, -1), (P, NE * NE)),
        "half": np.full((P, P), 0.5, f),
        "WqT": WqT, "WqT_dh": dh(WqT), "WkT": a["L0_attn_Wk"].T, "WvT": a["L0_attn_Wv"].T, "WoT": a["L0_attn_Wo"].T,
        "bq": col(a["L0_attn_bq"]), "bk": col(a["L0_attn_bk"]),
        "rk_first": col(np.tile(a["L0_attn_rel_k"][0], H0)), "rk_last": col(np.tile(a["L0_attn_rel_k"][-1], H0)),
        "gamma1": col(a["L0_ffn_gamma1"]), "gamma2": col(a["L0_ffn_gamma2"]), "gamma3": col(a["L1_attn_gamma"]),
        "bdown": tall(col(a["L0_ffn_bdown"])),
        "b1": by_chunk(a["L1_ffn_b1"], a["L1_ffn_sb1"]).T, "b3": by_chunk(a["L1_ffn_b3"], a["L1_ffn_sb3"]).T,
        "fWq": a["L0_ffn_Wq"], "fWdown": a["L0_ffn_Wdown"], "fWo": a["L0_ffn_Wo"], "fWg": a["L0_ffn_Wg"],
        "fWe": a["L0_ffn_We"].transpose(1, 0, 2).reshape(E, NE * E),
        "aWq": a["L1_attn_w_q"], "aWk": a["L1_attn_w_kv"][:, :E], "aWv": a["L1_attn_w_kv"][:, E:], "aWo": a["L1_attn_w_out"],
        "gateT": a["L1_ffn_gate_w"].T,
        "W1": by_chunk(a["L1_ffn_w1"].transpose(1, 0, 2), a["L1_ffn_sw1"]).reshape(E, -1),
        "W3": by_chunk(a["L1_ffn_w3"].transpose(1, 0, 2), a["L1_ffn_sw3"]).reshape(E, -1),
        "W2main": w2_all[:, :P].transpose(1, 0, 2).reshape(P, -1), "W2rem": w2_rem.reshape(P, -1),
    }
    rows = {
        "bq_dh": dh(a["L0_attn_bq"][None]), "bv": a["L0_attn_bv"], "bo": a["L0_attn_bo"], "fbq": a["L0_ffn_bq"],
        "fbkv": np.concatenate([bkv[:, 0].reshape(-1), bkv[:, 1].T.reshape(-1)]), "fbo": a["L0_ffn_bo"],
        "fbg": a["L0_ffn_bg"], "gate_b": a["L1_ffn_gate_b"],
    }
    arrays = {
        "x_in": a["L0_attn_hidden_states"],
        "wpack": np.concatenate([parts[n] for n, _ in W_COLS], 1),
        "rpack": np.concatenate([rows[n].reshape(-1) for n, _ in R_COLS]),
        "fWup": np.concatenate([kvf[:, :, 0].reshape(L, E), kvf[:, :, 1].transpose(0, 2, 1).reshape(L, E)], 1),
        "b2": np.concatenate([a["L1_ffn_b2"], a["L1_ffn_sb2"][None]]),
        "relkT": a["L0_attn_rel_k"].T,
        "relv": a["L0_attn_rel_v"].reshape(1, -1),
    }
    nc = bacc.Bacc("TRN2", target_bir_lowering=False, num_devices=1)
    args, maps = [], {}
    for name, x in arrays.items():
        x = np.ascontiguousarray(x)
        maps[name + "_dram"] = x
        args.append(nc.dram_tensor(name + "_dram", x.shape, F32, kind="ExternalInput").ap())
    args.append(nc.dram_tensor("out_dram", (B, S, E), F32, kind="ExternalOutput").ap())
    build(nc, *args)
    got = run_bass_kernel_spmd(nc, [maps], core_ids=[0])
    return got.results[0]["out_dram"]
```

```python
from contextlib import ExitStack

import concourse.bass as bass
from concourse import mybir

F32 = mybir.dt.float32
ALU = mybir.AluOpType
ACT = mybir.ActivationFunctionType
AX_X = mybir.AxisListType.X

P = 128
B = 8
S = 256
C = S // P
E = 128
H0, D0 = 16, 8
REL = 20
NREL = 2 * REL + 1
QI = P // H0
RT = S // QI
RTC = RT // C
PAIRS = RT // 2
L = 64
NE = 8
H1, D1 = 8, 16
HID = 176
REM = HID - P
NX = NE + 1
NR = (NX + 1) // 2
NCH = NX + NR
LN_EPS = 1e-5
RMS_EPS = 1e-6
NORM_GUARD = 1e-24 / E
DEN_GUARD = 1e-5
TOP_K = 2
NMM = 96

KB = 64
NKB = S // KB
NEAR = 32
WIN = KB + 2 * NEAR
TV0, TV1 = S - P - (REL // QI + 1) * QI, S + NEAR
TV = TV1 - TV0
CORNER = REL // QI + 1
TVC = (CORNER + 1) * QI
EG = 3

NORM, SCALE, TURN, PROJECT, SPLIT, PAIR0 = 0, 1, 2, 3, 4, 8
STEPS_PER_PAIR = 3
LAG_TURN, LAG_REL = 2, 4
WEIGH = PAIR0 + STEPS_PER_PAIR * (PAIRS + LAG_REL)
PV_STEPS = 4
DIVIDE = WEIGH + PV_STEPS
TURN_OUT, PROJECT_OUT = DIVIDE + 1, DIVIDE + 2
STEPS = PROJECT_OUT + 1


def counted(name, n):
    return [(name, k) for k in range(n)]


def once(*names):
    return [(name, 0) for name in names]


EARLY = (once("norm1", "root1", "scale1", "turn1", "down", "up")
         + [("dot", 0), ("dot", 1), ("dot_sum", 1), ("dot_sum", 0), ("soft", 0), ("soft_sum", 0),
            ("mix", 0), ("mix", 1), ("mix_sum", 1), ("mix_sum", 0), ("mix_scale", 0)]
         + once("turn_mix", "out1", "root2", "scale2", "turn2", "gate", "gate_norm") + counted("experts", 2 * C)
         + once("norm3", "scale3", "turn3", "qkv3", "sum3") + counted("taylor", H1) + counted("weigh3", C)
         + once("divide3", "turn_o3", "out3", "norm4", "scale4", "turn4"))
LATE = once("route", "rank") + counted("chunk", NCH + 2) + once("turn_rw") + counted("join", C * EG) + once("store")


LATE_STEPS = [0, 0, 0, 0, 1, 1, 1, 1, 1, 1, 2, 2, 2, 2, 2, 2, 2, 2, 2, 3, 3, 3, 3, 4, 4, 6]
EARLY_STEPS = [6, 6, 9, 13, 15, 16, 16, 16, 19, 19, 22, 26, 29, 31, 32, 37, 38, 43, 46, 48, 48, 51, 53, 54,
               54, 55, 57, 58, 60, 60, 65, 67, 69, 69, 69, 69, 69, 69, 69, 69, 69, 70, 70, 71, 71, 72, 72,
               74, 74]
PIECE_STEP = {**dict(zip(LATE, LATE_STEPS)), **dict(zip(EARLY, EARLY_STEPS))}
PIECES_AT = [[x for x in LATE + EARLY if PIECE_STEP[x] == step] for step in range(STEPS)]

W_COLS = [("ident", P), ("head_mask", H0), ("query_mask", QI), ("head_mask3", H1), ("earlier", NE * NE), ("half", P),
          ("WqT", E), ("WqT_dh", E), ("WkT", E), ("WvT", E), ("WoT", E),
          ("bq", 1), ("bk", 1), ("rk_first", 1), ("rk_last", 1),
          ("gamma1", 1), ("gamma2", 1), ("gamma3", 1), ("bdown", 1), ("b1", NCH), ("b3", NCH),
          ("fWq", E), ("fWdown", L), ("fWup", 2 * E), ("fWo", E), ("fWg", NE), ("fWe", NE * E),
          ("aWq", E), ("aWk", E), ("aWv", E), ("aWo", E), ("gateT", NE),
          ("W1", NCH * P), ("W3", NCH * P), ("W2main", NX * E), ("W2rem", NX * E)]
R_COLS = [("bq_dh", E), ("bv", E), ("rv_first", D0), ("rv_last", D0), ("bo", E), ("fbq", E), ("fbkv", 2 * E), ("fbo", E),
          ("fbg", NE), ("gate_b", NE)]


def offsets(cols):
    out, at = {}, 0
    for name, n in cols:
        out[name] = (at, n)
        at += n
    return out, at


W_AT, W_N = offsets(W_COLS)
R_AT, R_N = offsets(R_COLS)


def build(nc, x_in, wpack, rpack, b2, relkT, relv, out):
    ctx = ExitStack()
    with ctx:
        def sb(name, *shape):
            return ctx.enter_context(nc.sbuf_tensor(name, list(shape), F32))

        def sem(name, per):
            return ctx.enter_context(nc.semaphore(name)), per

        def view(t, off, dims, p0=0, np_=P):
            a = t[:]
            row = a.ap[0][0]
            return bass.AP(a.tensor, p0 * row + off, [[row, np_]] + [list(d) for d in dims])

        def wait(eng, signal, t, k):
            s, per = signal
            value = t * per + max(k, 0)
            if isinstance(value, int) and value <= 0:
                return
            eng.wait_ge(s, value)

        w = sb("w", P, W_N)
        r = sb("r", P, R_N)

        def wc(name, a=0, b=None, p0=0, p1=P):
            at, n = W_AT[name]
            return w[p0:p1, at + a:at + (n if b is None else b)]

        def rc(name):
            at, n = R_AT[name]
            return r[:, at:at + n]

        def rbc(name, copies):
            at, n = R_AT[name]
            return view(r, at, [[0, copies], [1, n]])

        ident = wc("ident")
        HH = H0 * H0
        b2s = sb("b2s", NX, E)
        expo = sb("expo", P, 8)
        half_root = sb("half_root", P, 1)
        TKN = 2 * S
        tk = sb("tk", QI * D0, TKN)
        tkw = sb("tkw", P, KB // QI, WIN)
        tv = sb("tv", P, TV * D0)
        tv_right, tv_left = sb("tv_right", P, TVC * D0), sb("tv_left", P, TVC * D0)
        xin = sb("xin", P, C, E)
        xres = sb("xres", P, C, E)
        st_a, mv_a, ve_a, rs_a = sb("st_a", P, C, 6), sb("mv_a", P, C, 2), sb("ve_a", P, C), sb("rs_a", P, C)
        xn = sb("xn", P, C, E)
        xnT = sb("xnT", P, S)
        qT = sb("qT", P, S)
        kT = sb("kT", P, NKB, S)
        bkf, bkl = sb("bkf", P, 1), sb("bkl", P, 1)
        qdh = sb("qdh", P, C, E)
        V9 = H0 * (D0 + 1)
        v9 = sb("v9", P, 2 * C * V9 + NMM)
        qbd = sb("qbd", P, RT // 2, P)
        qr = sb("qr", P, RT, P)
        nmx = sb("nmx", P, RT)
        pm = sb("pm", P, 3, 2, S)
        pT = sb("pT", P, C, RT, P)
        rvm = sb("rvm", P, 512)
        w2 = sb("w2", P, RT, D0)
        relo = sb("relo", P, C, E)
        rden = sb("rden", P, C, H0)
        on = sb("on", P, C, E)
        onT = sb("onT", P, S)
        x1 = sb("x1", P, C, E)
        st_b, mv_b, ve_b, rs_b = sb("st_b", P, C, 6), sb("mv_b", P, C, 2), sb("ve_b", P, 2, C), sb("rs_b", P, 2, C)
        xl = sb("xl", P, C, E)
        hh = sb("hh", P, C, E)
        hT = sb("hT", P, S)
        h2 = h3 = xf = hh
        h2T = h3T = xfT = hT
        dT = sb("dT", P, S)
        q1 = sb("q1", P, C, E)
        kv1 = sb("kv1", P, C, 2 * E)
        prod = sb("prod", P, C, H0 * H0 * D0)
        lg = sb("lg", P, C, H0 * H0)
        lmx = sb("lmx", P, C, H0)
        lsum = sb("lsum", P, C, H0)
        at1 = sb("at1", P, C, E)
        atT = sb("atT", P, S)
        o3, o3T = at1, atT
        y = sb("y", P, C, E)
        ysq = sb("ysq", P, E)
        ss = sb("ss", P, C)
        gl = sb("gl", P, C, NE)
        gmx, gsum = sb("gmx", P, C), sb("gsum", P, C)
        x2 = sb("x2", P, C, E)
        q3 = sb("q3", P, S)
        q3h = sb("q3h", P, H1, S)
        k3 = sb("k3", P, S)
        V17 = H1 * (D1 + 1)
        v17 = sb("v17", P, C * V17 + NMM)
        vsum = sb("vsum", P, V17)
        o17 = sb("o17", P, C, V17)
        sq = prod[:].rearrange("p c (h q) -> p (c h) q", q=2 * S).rearrange("p h (c q) -> p h c q", c=C)
        den3 = sb("den3", P, C, H1)
        x3 = sb("x3", P, C, E)
        sc = sb("sc", P, C, NE)
        smx, ssum = sb("smx", P, C), sb("ssum", P, C)
        bi = sb("bi", P, C, NE)
        above, tied = sb("above", P, C, NE, NE), sb("tied", P, C, NE, NE)
        rank = sb("rank", P, C, NE)
        rw = sb("rw", P, C, NX)
        rwT = sb("rwT", NX, S)
        ha = sb("ha", P, 2, S)
        hu = sb("hu", P, NCH, S)
        EK, EV = 2 * S + QI, S + NEAR + P
        ek, ev = hu[:].rearrange("p n s -> p (n s)")[:, 0:EK], prod[:].rearrange("p c n -> p (c n)")[:, 0:EV * D0]
        ht = sb("ht", P, 2, S)
        xo = sb("xo", P, C, E)
        bank = [ctx.enter_context(nc.psum_tensor(f"bank{j}", [P, 512], F32)) for j in range(8)]
        b_t = bank[2:4]
        b_rv, b_o = bank[4], bank[5]
        b_s = [bank[0], bank[1], b_o]
        m0, m1 = bank[6], bank[7]
        d_qdh = nc.dram_tensor("d_qdh", [S, D0, H0], F32, kind="Internal").ap()
        d_w2 = nc.dram_tensor("d_w2", [RT, QI, H0, D0], F32, kind="Internal").ap()
        d_ev = nc.dram_tensor("d_ev", [EV, D0], F32, kind="Internal").ap()

        w_in0, w_in1, r_in, small_in = (sem(n, 16) for n in ("w_in0", "w_in1", "r_in", "small_in"))
        rel_in, tk_in, ev_out, tv_in = (sem(n, 16) for n in ("rel_in", "tk_in", "ev_out", "tv_in"))
        tables_ready = sem("tables_ready", 1)
        zeroed, ones_set, rel_filled, w_folded = (sem(n, 1) for n in ("zeroed", "ones_set", "rel_filled", "w_folded"))
        x_loaded, xres_ready, ln_a, rstd_a, xn_ready = sem("x_loaded", 16), sem("xres_ready", 1), sem("ln_a", 5), sem("rstd_a", 1), sem("xn_ready", 1)
        xnT_ps, xnT_ready, qk_ps, v_ps = sem("xnT_ps", 1), sem("xnT_ready", 1), sem("qk_ps", 1), sem("v_ps", 1)
        qT_ready, kT_ready, qdh_ready, v_ready = sem("qT_ready", 1), sem("kT_ready", NKB), sem("qdh_ready", 1), sem("v_ready", 2)
        qdh_out, qr_in, qbd_ready = sem("qdh_out", 16), sem("qr_in", 16 * QI), sem("qbd_ready", 4)
        s_ps, max_ready, exp_ready = sem("s_ps", PAIRS), sem("max_ready", PAIRS), sem("exp_ready", PAIRS)
        pT_ps, pT_even, pT_odd = sem("pT_ps", PAIRS), sem("pT_even", PAIRS // 2), sem("pT_odd", PAIRS // 2)
        rv_ps, rv_masked, rv_sum = sem("rv_ps", 4), sem("rv_masked", 4), sem("rv_sum", 4)
        w2_out, relo_in = sem("w2_out", 16), sem("relo_in", 16)
        o_ps, o_steps, on_ready = sem("o_ps", 1), sem("o_steps", 1), sem("on_ready", 1)
        onT_ps, onT_ready, wo_ps, x1_ready = sem("onT_ps", 1), sem("onT_ready", 1), sem("wo_ps", 1), sem("x1_ready", 1)
        ln_b, rstd_b, h_ready, hT_ps, hT_ready = sem("ln_b", 5), sem("rstd_b", 1), sem("h_ready", 1), sem("hT_ps", 1), sem("hT_ready", 1)
        qd_ps, dT_ready, q1_ready, kv_ps, kv_ready = sem("qd_ps", 1), sem("dT_ready", 1), sem("q1_ready", 1), sem("kv_ps", 1), sem("kv_ready", 1)
        xl_ready, res_b = sem("xl_ready", 1), sem("res_b", 1)
        qk_prod, qk_prod1, qk_sum, l_max, l_sub, l_exp = sem("qk_prod", 1), sem("qk_prod1", 1), sem("qk_sum", 2), sem("l_max", 1), sem("l_sub", 1), sem("l_exp", 1)
        l_sum, l_rec, pv_prod, pv_prod1, pv_sum, at_ready = sem("l_sum", 1), sem("l_rec", 1), sem("pv_prod", 1), sem("pv_prod1", 1), sem("pv_sum", 2), sem("at_ready", 1)
        atT_ps, atT_ready, fo_ps, y_ready = sem("atT_ps", 1), sem("atT_ready", 1), sem("fo_ps", 1), sem("y_ready", 1)
        y_sq, ss_eps, rstd_y, h2_ready = sem("y_sq", 2), sem("ss_eps", 1), sem("rstd_y", 1), sem("h2_ready", 1)
        h2T_ps, h2T_ready, g_ps = sem("h2T_ps", 1), sem("h2T_ready", 1), sem("g_ps", 1)
        g_steps, g_exp, gate_ready = sem("g_steps", 3), sem("g_exp", 1), sem("gate_ready", 3)
        we_ps, acc_e = sem("we_ps", 4), sem("acc_e", 2 * NE)
        x1_sum, x2_ready = sem("x1_sum", 1), sem("x2_ready", 1)
        ln_c, var_c, rstd_c, h3_ready = sem("ln_c", 5), sem("var_c", 2), sem("rstd_c", 1), sem("h3_ready", 1)
        h3T_ps, h3T_ready, qk3_ps, qk3_ready = sem("h3T_ps", 1), sem("h3T_ready", 1), sem("qk3_ps", 1), sem("qk3_ready", 1)
        q3h_ready, vsum_ps, vsum_ready = sem("q3h_ready", 1), sem("vsum_ps", 1), sem("vsum_ready", 1)
        v3_ps, v3_ready, s3_ps, sq_ready = sem("v3_ps", 1), sem("v3_ready", 1), sem("s3_ps", H1), sem("sq_ready", H1)
        o3_ps, o3_den, o3_ready, o3T_ps, o3T_ready = sem("o3_ps", 1), sem("o3_den", 3), sem("o3_ready", 1), sem("o3T_ps", 1), sem("o3T_ready", 1)
        ao_ps, x3_ready = sem("ao_ps", 1), sem("x3_ready", 1)
        ln_d, rstd_d, xf_ready, xfT_ps, xfT_ready = sem("ln_d", 5), sem("rstd_d", 1), sem("xf_ready", 1), sem("xfT_ps", 1), sem("xfT_ready", 1)
        r_ps, r_steps, r_exp, sc_steps, rw_ready = sem("r_ps", 1), sem("r_steps", 2), sem("r_exp", 1), sem("sc_steps", 8), sem("rw_ready", 1)
        rwT_ps, rwT_ready = sem("rwT_ps", 1), sem("rwT_ready", 1)
        ab_ps, a_ready, u_ready, tanh_ready, hid_ready = sem("ab_ps", NCH), sem("a_ready", NCH), sem("u_ready", NCH), sem("tanh_ready", NCH), sem("hid_ready", NCH)
        eo_ps, eo_acc = sem("eo_ps", C * EG), sem("eo_acc", C * NX)
        stored = sem("stored", 16)

        block = ctx.enter_context(nc.Block())

        def turns(eng, attention, rest):
            def body(ta, tb, tc):
                for step in range(STEPS):
                    if ta is not None:
                        attention(ta, step)
                    for name, n in PIECES_AT[step]:
                        t = tc if (name, n) in LATE else tb
                        if t is not None:
                            rest(t, name, n)

            body(0, None, None)
            body(1, 0, None)
            body(2, 1, 0)
            with eng.Fori(3, B) as t:
                body(t, t - 1, t - 2)
            body(None, B - 1, B - 2)
            body(None, None, B - 1)

        @block.sync
        def _(sp):
            n0 = W_AT["fWq"][0]
            sp.dma_start(w[:, 0:n0], wpack[:, 0:n0]).then_inc(w_in0[0], 16)
            sp.dma_start(xin[:], x_in[0].rearrange("(c p) e -> p c e", p=P)).then_inc(x_loaded[0], 16)
            sp.wait_ge(rel_filled[0], 1)
            for qi in range(QI):
                sp.dma_start(tk[qi * D0:(qi + 1) * D0, :], ek[0:D0, QI - 1 - qi:QI - 1 - qi + TKN]).then_inc(tk_in[0], 16)
            sp.wait_ge(rel_filled[0], 2)
            sp.dma_start(d_ev.rearrange("m d -> (m d)").rearrange("(a n) -> a n", a=1), ev[0:1]).then_inc(ev_out[0], 16)
            sp.wait_ge(ev_out[0], 16)
            sp.dma_start(tv[:], bass.AP(d_ev.tensor, TV0 * D0, [[D0, P], [1, TV * D0]])).then_inc(tv_in[0], 16)
            sp.dma_start(w[:, n0:], wpack[:, n0:]).then_inc(w_in1[0], 16)

            def due(signal, t, k):
                value = t * signal[1] + k
                return signal[0], value if isinstance(value, int) else sp.snap(value)

            def met(mark):
                if not isinstance(mark[1], int) or mark[1] > 0:
                    sp.wait_ge(*mark)

            def body(t):
                queries, o_before = due(qdh_ready, t, 1), due(o_ps, t, 0)
                written = due(qdh_out, t, 16)
                rel_sums, rel_written, on_before = due(rv_sum, t, 4), due(w2_out, t, 16), due(on_ready, t, 0)
                if not isinstance(t, int) or t > 0:
                    xn_before, xres_before = due(xn_ready, t, 0), due(xres_ready, t, 0)
                    at = t * (S * E) if isinstance(t, int) else sp.snap(t * (S * E))
                    met(xn_before)
                    met(xres_before)
                    sp.dma_start(xin[:], bass.AP(x_in.tensor, at, [[E, P], [P * E, C], [1, E]])).then_inc(x_loaded[0], 16)
                met(queries)
                met(o_before)
                sp.dma_start(d_qdh.rearrange("(c p) d h -> p c (d h)", p=P), qdh[:]).then_inc(qdh_out[0], 16)
                met(written)
                for qi in range(QI):
                    dst = view(qr, qi * H0, [[P, RT], [1, H0]], qi * D0, D0)
                    src = d_qdh.rearrange("(r q) d h -> q d r h", q=QI)[qi]
                    sp.dma_start(dst, src).then_inc(qr_in[0], 16)
                met(rel_sums)
                met(on_before)
                sp.dma_start(d_w2.rearrange("r q h d -> (q h) r d"), w2[:]).then_inc(w2_out[0], 16)
                met(rel_written)
                sp.dma_start(relo[:], d_w2.rearrange("(c r) q h d -> (r q) c (h d)", c=C)).then_inc(relo_in[0], 16)

            body(0)
            body(1)
            with sp.Fori(2, B) as t:
                body(t)
            sp.wait_ge(stored[0], 16 * B)

        @block.scalar
        def _(act):
            copy, idn, exp = ACT.Copy, ACT.Identity, ACT.Exp
            act.dma_start(r[:], rpack.partition_broadcast(P)).then_inc(r_in[0], 16)
            act.dma_start(ek[0:D0, S - REL + QI - 1:S + REL + QI], relkT).then_inc(rel_in[0], 16)
            act.dma_start(ev[0:1, (S - 1 - REL) * D0:(S + REL) * D0], relv).then_inc(rel_in[0], 16)
            act.dma_start(b2s[:], b2).then_inc(small_in[0], 16)

            def evict(t, ps, k, done, src, dst, free=None):
                wait(act, ps, t, k)
                if free:
                    wait(act, *free)
                act.activation(dst, src, copy).then_inc(done[0], 1)

            def attention(t, step):
                if step == TURN:
                    evict(t, xnT_ps, 1, xnT_ready, b_t[0][:, 0:S], xnT[:], (v_ps, t, 0))
                elif step == PROJECT:
                    wait(act, qk_ps, t, 1)
                    wait(act, qbd_ready, t, 0)
                    act.activation(qT[:], b_t[1][:, 0:S], idn, bias=wc("bq")).then_inc(qT_ready[0], 1)
                    wait(act, s_ps, t, 0)
                    for u in range(NKB):
                        if u:
                            act.activation(kT[:, u, 0:u * KB], b_t[1][:, S:S + u * KB], idn, bias=bkf[:])
                        act.activation(kT[:, u, u * KB:], b_t[1][:, S + u * KB:2 * S], idn, bias=bkl[:]).then_inc(kT_ready[0], 1)
                elif PAIR0 <= step < WEIGH:
                    p, part = divmod(step - PAIR0, STEPS_PER_PAIR)
                    if part == 0 and p < PAIRS:
                        weights(t, p)
                    elif part == 2 and 0 <= p - LAG_TURN < PAIRS and (p - LAG_TURN) % 2:
                        move_pT(t, p - LAG_TURN)
                elif step == TURN_OUT:
                    evict(t, onT_ps, 1, onT_ready, b_o[:, 0:S], onT[:], (wo_ps, t, 0))

            def weights(t, p):
                wait(act, max_ready, t, p + 1)
                wait(act, pT_ps, t, p - 2)
                for j in range(2):
                    a = act.activation(pm[:, p % 3, j], b_s[p % 3][:, j * S:(j + 1) * S], exp,
                                       bias=nmx[:, 2 * p + j:2 * p + j + 1])
                a.then_inc(exp_ready[0], 1)

            def move_pT(t, p):
                wait(act, pT_ps, t, p + 1)
                if p < 2:
                    wait(act, o_ps, t, 0)
                src = view(b_t[p % 2], 0, [[P, 2], [2 * P, 2], [1, P]])
                dst = view(pT, 2 * p * P, [[RT * P, 2], [P, 2], [1, P]])
                act.activation(dst, src, copy).then_inc(pT_odd[0], 1)

            def rest(t, name, n):
                if name == "turn1":
                    if isinstance(t, int):
                        act.wait_ge(w_folded[0], 2)
                    evict(t, hT_ps, 1, hT_ready, m0[:, 0:S], hT[:], (qd_ps, t, 0))
                elif name == "down":
                    wait(act, qd_ps, t, 1)
                    wait(act, kv_ps, t, 0)
                    act.activation(dT[0:L], m1[0:L, 0:S], idn, bias=wc("bdown", p1=L)).then_inc(dT_ready[0], 1)
                elif name == "soft":
                    wait(act, l_sub, t, 1)
                    act.activation(lg[:], lg[:], exp, scale=float(D0) ** -0.5).then_inc(l_exp[0], 1)
                elif name == "turn_mix":
                    evict(t, atT_ps, 1, atT_ready, m0[:, 0:S], atT[:], (fo_ps, t, 0))
                elif name == "out1":
                    wait(act, y_ready, t, 1)
                    for c in range(C):
                        wait(act, y_sq, t, c)
                        act.activation(ysq[:], y[:, c], ACT.Square, accum_out=ss[:, c:c + 1]).then_inc(y_sq[0], 1)
                elif name == "turn2":
                    evict(t, h2T_ps, 1, h2T_ready, m0[:, 0:S], h2T[:], (we_ps, t, 0))
                elif name == "gate":
                    wait(act, g_steps, t, 3)
                    act.activation(gl[:], gl[:], exp).then_inc(g_exp[0], 1)
                elif name == "turn3":
                    evict(t, h3T_ps, 1, h3T_ready, m0[:, 0:S], h3T[:], (v3_ps, t, 0))
                elif name == "qkv3":
                    wait(act, qk3_ps, t, 1)
                    wait(act, s3_ps, t, 0)
                    wait(act, q3h_ready, t, 0)
                    act.activation(q3[:], m1[:, 0:S], copy)
                    act.activation(k3[:], m1[:, S:2 * S], copy).then_inc(qk3_ready[0], 1)
                elif name == "sum3":
                    wait(act, vsum_ps, t, 1)
                    wait(act, o3_den, t, 0)
                    act.activation(vsum[:], m1[:, 0:V17], copy).then_inc(vsum_ready[0], 1)
                elif name == "taylor":
                    wait(act, o3_ps, t, 0)
                    wait(act, s3_ps, t, n + 1)
                    act.activation(sq[:, n], (m0, m1)[n % 2][:], ACT.Square, scale=0.5 ** 0.5,
                                   bias=half_root[:]).then_inc(sq_ready[0], 1)
                elif name == "turn_o3":
                    evict(t, o3T_ps, 1, o3T_ready, m1[:, 0:S], o3T[:], (ao_ps, t, 0))
                elif name == "turn4":
                    evict(t, xfT_ps, 1, xfT_ready, m0[:, 0:S], xfT[:], (ab_ps, t, 0))
                elif name == "route":
                    wait(act, r_steps, t, 2)
                    act.activation(sc[:], sc[:], exp).then_inc(r_exp[0], 1)
                elif name == "chunk":
                    if n < NCH:
                        wait(act, ab_ps, t, n + 1)
                        wait(act, u_ready, t, n - 1)
                        act.activation(ha[:, n % 2], (m0, m1)[n % 2][:, 0:S], idn, scale=0.5,
                                       bias=wc("b1", n, n + 1)).then_inc(a_ready[0], 1)
                    if 1 <= n <= NCH:
                        wait(act, u_ready, t, n)
                        wait(act, hid_ready, t, n - 2)
                        act.activation(ht[:, (n - 1) % 2], hu[:, n - 1], ACT.Tanh).then_inc(tanh_ready[0], 1)
                elif name == "turn_rw":
                    evict(t, rwT_ps, 1, rwT_ready, m0[0:NX, 0:S], rwT[:], (eo_ps, t, 0))

            act.wait_ge(w_folded[0], 1)
            act.wait_ge(ones_set[0], 1)
            turns(act, attention, rest)

        @block.gpsimd
        def _(pool):
            g = nc.gpsimd
            g.memset(expo[:], -0.5)
            g.memset(half_root[:], 0.5 ** 0.5)
            g.memset(v9[:], 1.0)
            g.memset(v17[:], 1.0)
            g.memset(rw[:], 1.0)
            g.memset(dT[:], 0.0)
            g.memset(tkw[:], 0.0)
            g.memset(qr[:], 0.0).then_inc(ones_set[0], 1)

            def attention(t, step):
                if step == NORM:
                    wait(pool, x_loaded, t, 16)
                    if isinstance(t, int):
                        pool.wait_ge(r_in[0], 16)
                    wait(pool, x1_ready, t, 0)
                    g.tensor_tensor(xres[:], xin[:], rbc("bo", C), ALU.add).then_inc(xres_ready[0], 1)
                    wait(pool, ln_a, t, 5)
                    wait(pool, xn_ready, t, 0)
                    g.tensor_tensor(rs_a[:], ve_a[:], expo[:, 0:C], ALU.pow).then_inc(rstd_a[0], 1)
                elif step == SPLIT:
                    wait(pool, qT_ready, t, 1)
                    block_queries(t, 0)
                    block_queries(t, 1)
                elif step in (PAIR0 + 4 * STEPS_PER_PAIR, PAIR0 + 8 * STEPS_PER_PAIR):
                    block_queries(t, 1 + (step - PAIR0) // (4 * STEPS_PER_PAIR))

            def block_queries(t, k):
                wait(pool, s_ps, t, 4 * (k - 1))
                n = RT // 4
                g.tensor_tensor(view(qbd, k % 2 * n * P, [[P, n], [H0, QI], [1, H0]]),
                                view(qT, k * n * QI, [[QI, n], [1, QI], [0, H0]]),
                                view(w, W_AT["head_mask"][0], [[0, n], [0, QI], [1, H0]]),
                                ALU.mult).then_inc(qbd_ready[0], 1)

            def rest(t, name, n):
                if name == "root1":
                    wait(pool, ln_b, t, 5)
                    wait(pool, h_ready, t, 0)
                    g.tensor_tensor(rs_b[:], ve_b[:], view(expo, 0, [[0, 2], [1, C]]), ALU.pow).then_inc(rstd_b[0], 1)
                elif name == "scale1":
                    wait(pool, xl_ready, t, 1)
                    wait(pool, y_ready, t, 0)
                    g.tensor_tensor(xl[:], xl[:], rbc("fbo", C), ALU.add).then_inc(res_b[0], 1)
                elif name == "dot" and n == 0:
                    wait(pool, kv_ready, t, 1)
                    wait(pool, o3_ps, t, 0)
                    g.tensor_tensor(view(prod, n * HH * D0, [[H0 * D0, H0], [D0, H0], [1, D0]]),
                                    view(q1, n * E, [[D0, H0], [0, H0], [1, D0]]),
                                    view(kv1, n * 2 * E, [[0, H0], [D0, H0], [1, D0]]), ALU.mult).then_inc(qk_prod[0], 1)
                elif name == "mix" and n == 0:
                    wait(pool, l_exp, t, 1)
                    g.tensor_tensor(view(prod, n * HH * D0, [[H0 * D0, H0], [H0, D0], [1, H0]]),
                                    view(lg, n * HH, [[H0, H0], [0, D0], [1, H0]]),
                                    view(kv1, n * 2 * E + E, [[0, H0], [H0, D0], [1, H0]]), ALU.mult).then_inc(pv_prod[0], 1)
                elif name == "root2":
                    wait(pool, ss_eps, t, 1)
                    wait(pool, h2_ready, t, 0)
                    g.tensor_tensor(rs_b[:, 0], ve_b[:, 0], expo[:, 0:C], ALU.pow).then_inc(rstd_y[0], 1)
                elif name == "turn2":
                    wait(pool, y_ready, t, 1)
                    wait(pool, x3_ready, t, 0)
                    g.tensor_tensor(x2[:], x1[:], y[:], ALU.add).then_inc(x1_sum[0], 1)
                elif name == "norm3":
                    wait(pool, var_c, t, 2)
                    g.tensor_tensor(rs_b[:, 0], ve_b[:, 0], expo[:, 0:C], ALU.pow).then_inc(rstd_c[0], 1)
                elif name == "qkv3":
                    wait(pool, qk3_ready, t, 1)
                    wait(pool, s3_ps, t, 0)
                    g.tensor_tensor(q3h[:], view(q3, 0, [[0, H1], [1, S]]),
                                    view(w, W_AT["head_mask3"][0], [[1, H1], [0, S]]), ALU.mult).then_inc(q3h_ready[0], 1)
                elif name == "norm4":
                    wait(pool, ln_d, t, 5)
                    g.tensor_tensor(rs_b[:, 0], ve_b[:, 0], expo[:, 0:C], ALU.pow).then_inc(rstd_d[0], 1)
                elif name == "store":
                    wait(pool, eo_acc, t, C * NX)
                    pool.dma_start(out[t].rearrange("(c p) e -> p c e", p=P), xo[:]).then_inc(stored[0], 16)

            pool.wait_ge(w_in0[0], 16)
            pool.wait_ge(w_folded[0], 1)
            pool.wait_ge(ones_set[0], 1)
            turns(pool, attention, rest)

        @block.vector
        def _(dve):
            v = nc.vector
            scale0 = float(D0) ** -0.5
            dve.wait_ge(rel_in[0], 32)
            lo, hi = S - REL + QI - 1, S + REL + QI
            v.tensor_copy(view(hu, 0, [[1, lo]], 0, D0), view(hu, lo, [[0, lo]], 0, D0))
            v.tensor_copy(view(hu, hi, [[1, EK - hi]], 0, D0), view(hu, hi - 1, [[0, EK - hi]], 0, D0)).then_inc(rel_filled[0], 1)
            lo, hi = S - 1 - REL, S + REL
            v.tensor_copy(view(prod, 0, [[D0, lo], [1, D0]], 0, 1), view(prod, lo * D0, [[0, lo], [1, D0]], 0, 1))
            v.tensor_copy(view(prod, hi * D0, [[D0, EV - hi], [1, D0]], 0, 1),
                          view(prod, (hi - 1) * D0, [[0, EV - hi], [1, D0]], 0, 1)).then_inc(rel_filled[0], 1)
            dve.wait_ge(w_in0[0], 16)
            dve.wait_ge(r_in[0], 16)
            for n in ("WqT", "WqT_dh", "bq"):
                v.tensor_scalar(wc(n), wc(n), scale0, None, ALU.mult)
            v.tensor_tensor(bkf[:], wc("bk"), wc("rk_first"), ALU.add)
            v.tensor_tensor(bkl[:], wc("bk"), wc("rk_last"), ALU.add)
            v.tensor_scalar(rc("bq_dh"), rc("bq_dh"), scale0, None, ALU.mult).then_inc(w_folded[0], 1)
            dve.wait_ge(w_folded[0], 1)
            dve.wait_ge(ones_set[0], 1)

            def rel_tables():
                dve.wait_ge(tk_in[0], 16 * QI)
                dve.wait_ge(tv_in[0], 16)
                at, n = S - KB + QI - NEAR, KB // QI
                k = QI * D0
                v.tensor_scalar(view(tkw, 0, [[WIN, n], [1, NEAR]], 0, k), view(tk, at, [[QI, n], [1, NEAR]], 0, k),
                                tk[:, 0:1], None, ALU.subtract)
                v.tensor_scalar(view(tkw, NEAR, [[WIN, n], [1, WIN - NEAR]], 0, k), view(tk, at + NEAR, [[QI, n], [1, WIN - NEAR]], 0, k),
                                tk[:, TKN - 1:TKN], None, ALU.subtract)
                for dst, x, end in ((tv_right, S, "rv_last"), (tv_left, TV0, "rv_first")):
                    a = v.tensor_tensor(view(dst, 0, [[D0, TVC], [1, D0]]), view(tv, (x - TV0) * D0, [[D0, TVC], [1, D0]]),
                                        view(r, R_AT[end][0], [[0, TVC], [1, D0]]), ALU.subtract)
                a.then_inc(tables_ready[0], 1)

            def fold_gains():
                dve.wait_ge(w_in1[0], 16)
                for n, gain in (("fWq", "gamma1"), ("fWdown", "gamma1"), ("fWg", "gamma2"), ("fWe", "gamma2"),
                                ("aWq", "gamma3"), ("aWk", "gamma3"), ("aWv", "gamma3")):
                    v.tensor_scalar(wc(n), wc(n), wc(gain), None, ALU.mult)
                v.tensor_scalar(wc("b1"), wc("b1"), 0.5, None, ALU.mult).then_inc(w_folded[0], 1)
                dve.wait_ge(w_folded[0], 2)

            def moments(t, src, st, mv, ve, steps):
                for c in range(C):
                    a = v.bn_stats(st[:, c], src[:, c])
                a.then_inc(steps[0], 1)
                wait(dve, steps, t, 1)
                v.tensor_tensor(mv[:], st[:, :, 1:3], st[:, :, 4:6], ALU.add)
                v.tensor_tensor(st[:, :, 0], st[:, :, 1], st[:, :, 4], ALU.subtract).then_inc(steps[0], 1)
                wait(dve, steps, t, 2)
                v.tensor_scalar(mv[:, :, 0], mv[:, :, 0], 0.5, None, ALU.mult)
                v.scalar_tensor_tensor(st[:, :, 3], st[:, :, 0], E / 4, st[:, :, 0], ALU.mult, ALU.mult).then_inc(steps[0], 1)
                wait(dve, steps, t, 3)
                v.tensor_tensor(mv[:, :, 1], mv[:, :, 1], st[:, :, 3], ALU.add).then_inc(steps[0], 1)
                wait(dve, steps, t, 4)
                return v.tensor_scalar(ve, mv[:, :, 1], 1 / E, LN_EPS, ALU.mult, ALU.add)

            def normed(dst, src, mv, rs):
                for c in range(C):
                    a = v.tensor_scalar(dst[:, c], src[:, c], mv[:, c, 0:1], rs[:, c:c + 1], ALU.subtract, ALU.mult)
                return a

            def attention(t, step):
                if step == NORM:
                    wait(dve, x_loaded, t, 16)
                    moments(t, xin, st_a, mv_a, ve_a[:], ln_a).then_inc(ln_a[0], 1)
                elif step == SCALE:
                    wait(dve, rstd_a, t, 1)
                    wait(dve, xnT_ps, t, 0)
                    normed(xn, xin, mv_a, rs_a).then_inc(xn_ready[0], 1)
                elif step == SPLIT:
                    wait(dve, v_ps, t, 1)
                    wait(dve, qdh_out, t, 0)
                    v.tensor_tensor(qdh[:], b_o[:, 0:C * E].rearrange("p (c e) -> p c e", c=C), rbc("bq_dh", C), ALU.add).then_inc(qdh_ready[0], 1)
                    if isinstance(t, int) and t == 0:
                        rel_tables()
                    wait(dve, o_ps, t, 0)
                    for c in range(C):
                        a = v.tensor_tensor(view(v9, c * V9, [[D0 + 1, H0], [1, D0]]),
                                            view(b_rv, c * E, [[D0, H0], [1, D0]]),
                                            view(r, R_AT["bv"][0], [[D0, H0], [1, D0]]), ALU.add)
                    a.then_inc(v_ready[0], 1)
                    wait(dve, v_ready, t, 1)
                    for c, end in enumerate(("rv_first", "rv_last")):
                        a = v.tensor_tensor(view(v9, (C + c) * V9, [[D0 + 1, H0], [1, D0]]),
                                            view(v9, c * V9, [[D0 + 1, H0], [1, D0]]),
                                            view(r, R_AT[end][0], [[0, H0], [1, D0]]), ALU.add)
                    a.then_inc(v_ready[0], 1)
                elif PAIR0 <= step < WEIGH:
                    p, part = divmod(step - PAIR0, STEPS_PER_PAIR)
                    if part == 0 and p < PAIRS:
                        wait(dve, s_ps, t, p + 1)
                        wait(dve, exp_ready, t, 0)
                        v.tensor_reduce(nmx[:, 2 * p:2 * p + 2], b_s[p % 3][:].rearrange("p (j k) -> p j k", j=2),
                                        AX_X, ALU.max, negate=True).then_inc(max_ready[0], 1)
                    elif part == 1 and p >= LAG_REL and (p - LAG_REL) % 4 == 3:
                        rel_values(t, (p - LAG_REL) // 4)
                    elif part == 2 and 0 <= p - LAG_TURN < PAIRS and (p - LAG_TURN) % 2 == 0:
                        move_pT(t, p - LAG_TURN)
                elif step == DIVIDE:
                    wait(dve, o_ps, t, 1)
                    o4 = [view(b_o, c * 256, [[D0 + 1, H0], [1, D0]]) for c in range(C)]
                    wait(dve, on_ready, t, 0)
                    v.reciprocal(rden[:], view(b_o, D0, [[256, C], [D0 + 1, H0]]))
                    wait(dve, relo_in, t, 16)
                    for c in range(C):
                        a = v.tensor_tensor(view(on, c * E, [[D0, H0], [1, D0]]), o4[c], view(relo, c * E, [[D0, H0], [1, D0]]), ALU.add)
                    a.then_inc(o_steps[0], 1)
                    wait(dve, o_steps, t, 1)
                    wait(dve, onT_ps, t, 0)
                    v.tensor_tensor(view(on, 0, [[E, C], [D0, H0], [1, D0]]), view(on, 0, [[E, C], [D0, H0], [1, D0]]),
                                    view(rden, 0, [[H0, C], [1, H0], [0, D0]]), ALU.mult).then_inc(on_ready[0], 1)
                elif step == PROJECT_OUT:
                    wait(dve, wo_ps, t, 1)
                    wait(dve, xres_ready, t, 1)
                    wait(dve, x1_sum, t, 0)
                    v.tensor_tensor(x1[:], b_rv[:, 0:C * E].rearrange("p (c e) -> p c e", c=C), xres[:], ALU.add).then_inc(x1_ready[0], 1)

            def move_pT(t, q):
                wait(dve, pT_ps, t, q + 1)
                if q < 2:
                    wait(dve, o_ps, t, 0)
                    wait(dve, rv_ps, t, 0)
                v.tensor_copy(view(pT, 2 * q * P, [[RT * P, 2], [P, 2], [1, P]]),
                              view(b_t[q % 2], 0, [[P, 2], [2 * P, 2], [1, P]])).then_inc(pT_even[0], 1)

            def rel_values(t, k):
                wait(dve, rv_ps, t, k + 1)
                wait(dve, rv_sum, t, k)
                v.tensor_tensor(rvm[:].rearrange("p (r q d) -> p r q d", r=8, q=QI),
                                b_rv[:].rearrange("p (r q d) -> p r q d", r=8, q=QI),
                                view(w, W_AT["query_mask"][0], [[0, 8], [1, QI], [0, D0]]), ALU.mult).then_inc(rv_masked[0], 1)
                wait(dve, rv_masked, t, k + 1)
                if k == 0:
                    wait(dve, w2_out, t, 0)
                v.tensor_reduce(w2[:, 8 * k:8 * k + 8, :], view(rvm, 0, [[QI * D0, 8], [1, D0], [D0, QI]]), AX_X, ALU.add).then_inc(rv_sum[0], 1)

            def rest(t, name, n):
                if name == "norm1":
                    if isinstance(t, int) and t == 0:
                        fold_gains()
                    wait(dve, x1_ready, t, 1)
                    moments(t, x1, st_b, mv_b, ve_b[:, 0], ln_b)
                    v.tensor_scalar(ve_b[:, 1], mv_b[:, :, 1], (1.0 + RMS_EPS) / E, LN_EPS * RMS_EPS, ALU.mult, ALU.add).then_inc(ln_b[0], 1)
                elif name == "scale1":
                    wait(dve, rstd_b, t, 1)
                    normed(xl, x1, mv_b, rs_b[:, 0]).then_inc(xl_ready[0], 1)
                    wait(dve, hT_ps, t, 0)
                    normed(hh, x1, mv_b, rs_b[:, 1]).then_inc(h_ready[0], 1)
                elif name == "down":
                    wait(dve, qd_ps, t, 1)
                    wait(dve, qk_prod, t, 0)
                    v.tensor_tensor(q1[:], m0[:, 0:S].rearrange("p (c e) -> p c e", c=C), rbc("fbq", C), ALU.add).then_inc(q1_ready[0], 1)
                elif name == "up":
                    wait(dve, kv_ps, t, 1)
                    wait(dve, pv_prod, t, 0)
                    v.tensor_tensor(kv1[:], m1[:].rearrange("p (c e) -> p c e", c=C), rbc("fbkv", C), ALU.add).then_inc(kv_ready[0], 1)
                elif name == "dot" and n == 1:
                    wait(dve, kv_ready, t, 1)
                    wait(dve, o3_ps, t, 0)
                    v.tensor_tensor(view(prod, n * HH * D0, [[H0 * D0, H0], [D0, H0], [1, D0]]),
                                    view(q1, n * E, [[D0, H0], [0, H0], [1, D0]]),
                                    view(kv1, n * 2 * E, [[0, H0], [D0, H0], [1, D0]]), ALU.mult).then_inc(qk_prod1[0], 1)
                elif name == "dot_sum":
                    wait(dve, (qk_prod, qk_prod1)[n], t, 1)
                    v.tensor_reduce(lg[:, n], view(prod, n * HH * D0, [[D0, HH], [1, D0]]), AX_X, ALU.add).then_inc(qk_sum[0], 1)
                elif name == "soft":
                    wait(dve, qk_sum, t, C)
                    v.tensor_reduce(lmx[:], view(lg, 0, [[H0, C * H0], [1, H0]]), AX_X, ALU.max).then_inc(l_max[0], 1)
                    wait(dve, l_max, t, 1)
                    v.tensor_tensor(view(lg, 0, [[H0, C * H0], [1, H0]]), view(lg, 0, [[H0, C * H0], [1, H0]]),
                                    view(lmx, 0, [[1, C * H0], [0, H0]]), ALU.subtract).then_inc(l_sub[0], 1)
                elif name == "soft_sum":
                    wait(dve, l_exp, t, 1)
                    v.tensor_reduce(lsum[:], view(lg, 0, [[H0, C * H0], [1, H0]]), AX_X, ALU.add).then_inc(l_sum[0], 1)
                    wait(dve, l_sum, t, 1)
                    v.reciprocal(lsum[:], lsum[:]).then_inc(l_rec[0], 1)
                elif name == "mix" and n == 1:
                    wait(dve, l_exp, t, 1)
                    v.tensor_tensor(view(prod, n * HH * D0, [[H0 * D0, H0], [H0, D0], [1, H0]]),
                                    view(lg, n * HH, [[H0, H0], [0, D0], [1, H0]]),
                                    view(kv1, n * 2 * E + E, [[0, H0], [H0, D0], [1, H0]]), ALU.mult).then_inc(pv_prod1[0], 1)
                elif name == "mix_sum":
                    wait(dve, (pv_prod, pv_prod1)[n], t, 1)
                    v.tensor_reduce(at1[:, n], view(prod, n * HH * D0, [[H0, E], [1, H0]]), AX_X, ALU.add).then_inc(pv_sum[0], 1)
                elif name == "mix_scale":
                    wait(dve, pv_sum, t, C)
                    wait(dve, l_rec, t, 1)
                    wait(dve, atT_ps, t, 0)
                    v.tensor_tensor(view(at1, 0, [[D0, C * H0], [1, D0]]), view(at1, 0, [[D0, C * H0], [1, D0]]),
                                    view(lsum, 0, [[1, C * H0], [0, D0]]), ALU.mult).then_inc(at_ready[0], 1)
                elif name == "out1":
                    wait(dve, fo_ps, t, 1)
                    wait(dve, res_b, t, 1)
                    v.tensor_tensor(y[:], m1[:, 0:S].rearrange("p (c e) -> p c e", c=C), xl[:], ALU.add).then_inc(y_ready[0], 1)
                elif name == "root2":
                    wait(dve, y_sq, t, 2)
                    v.tensor_scalar(ve_b[:, 0], ss[:], 1.0 / E, RMS_EPS, ALU.mult, ALU.add).then_inc(ss_eps[0], 1)
                elif name == "scale2":
                    wait(dve, rstd_y, t, 1)
                    wait(dve, h2T_ps, t, 0)
                    for c in range(C):
                        a = v.tensor_scalar(h2[:, c], y[:, c], rs_b[:, 0, c:c + 1], None, ALU.mult)
                    a.then_inc(h2_ready[0], 1)
                elif name == "gate":
                    wait(dve, g_ps, t, 1)
                    v.tensor_tensor(gl[:], m1[:, 0:C * NE].rearrange("p (c e) -> p c e", c=C), rbc("fbg", C), ALU.add).then_inc(g_steps[0], 1)
                    wait(dve, g_steps, t, 1)
                    v.tensor_reduce(gmx[:], gl[:], AX_X, ALU.max).then_inc(g_steps[0], 1)
                    wait(dve, g_steps, t, 2)
                    v.tensor_tensor(gl[:], gl[:], view(gmx, 0, [[1, C], [0, NE]]), ALU.subtract).then_inc(g_steps[0], 1)
                elif name == "gate_norm":
                    wait(dve, g_exp, t, 1)
                    v.tensor_reduce(gsum[:], gl[:], AX_X, ALU.add).then_inc(gate_ready[0], 1)
                    wait(dve, gate_ready, t, 1)
                    v.reciprocal(gsum[:], gsum[:]).then_inc(gate_ready[0], 1)
                    wait(dve, gate_ready, t, 2)
                    v.tensor_tensor(gl[:], gl[:], view(gsum, 0, [[1, C], [0, NE]]), ALU.mult).then_inc(gate_ready[0], 1)
                elif name == "experts":
                    c, half = n // 2, n % 2
                    if n == 0:
                        wait(dve, gate_ready, t, 3)
                        wait(dve, x1_sum, t, 1)
                    wait(dve, we_ps, t, n + 1)
                    for e in range(4):
                        ee = half * 4 + e
                        if ee:
                            wait(dve, acc_e, t, n * 4 + e)
                        v.scalar_tensor_tensor(x2[:, c], (m0, m1)[half][:, e * E:(e + 1) * E], gl[:, c, ee:ee + 1], x2[:, c],
                                               ALU.mult, ALU.add).then_inc(acc_e[0], 1)
                elif name == "norm3":
                    wait(dve, acc_e, t, 2 * NE)
                    moments(t, x2, st_b, mv_b, ve_b[:, 0], ln_c).then_inc(ln_c[0], 1)
                    wait(dve, ln_c, t, 5)
                    v.tensor_scalar(ve_b[:, 1], ve_b[:, 0], NORM_GUARD, None, ALU.mult).then_inc(var_c[0], 1)
                    wait(dve, var_c, t, 1)
                    v.scalar_tensor_tensor(ve_b[:, 0], mv_b[:, :, 1], 1 / E, ve_b[:, 1], ALU.mult, ALU.max).then_inc(var_c[0], 1)
                elif name == "scale3":
                    wait(dve, rstd_c, t, 1)
                    wait(dve, h3T_ps, t, 0)
                    normed(h3, x2, mv_b, rs_b[:, 0]).then_inc(h3_ready[0], 1)
                elif name == "qkv3":
                    wait(dve, v3_ps, t, 1)
                    for c in range(C):
                        a = v.tensor_copy(view(v17, c * V17, [[D1 + 1, H1], [1, D1]]), view(m0, c * E, [[D1, H1], [1, D1]]))
                    a.then_inc(v3_ready[0], 1)
                elif name == "divide3":
                    wait(dve, o3_ps, t, 1)
                    wait(dve, vsum_ready, t, 1)
                    v.tensor_tensor(o17[:], view(m0, 0, [[256, C], [1, V17]]), view(vsum, 0, [[0, C], [1, V17]]), ALU.add).then_inc(o3_den[0], 1)
                    wait(dve, o3_den, t, 1)
                    v.tensor_scalar(den3[:], view(o17, D1, [[V17, C], [D1 + 1, H1]]), DEN_GUARD, None, ALU.max).then_inc(o3_den[0], 1)
                    wait(dve, o3_den, t, 2)
                    v.reciprocal(den3[:], den3[:]).then_inc(o3_den[0], 1)
                    wait(dve, o3_den, t, 3)
                    wait(dve, o3T_ps, t, 0)
                    v.tensor_tensor(view(o3, 0, [[E, C], [D1, H1], [1, D1]]), view(o17, 0, [[V17, C], [D1 + 1, H1], [1, D1]]),
                                    view(den3, 0, [[H1, C], [1, H1], [0, D1]]), ALU.mult).then_inc(o3_ready[0], 1)
                elif name == "out3":
                    wait(dve, ao_ps, t, 1)
                    v.tensor_tensor(x3[:], m0[:, 0:S].rearrange("p (c e) -> p c e", c=C), x2[:], ALU.add).then_inc(x3_ready[0], 1)
                elif name == "norm4":
                    wait(dve, x3_ready, t, 1)
                    moments(t, x3, st_b, mv_b, ve_b[:, 0], ln_d).then_inc(ln_d[0], 1)
                elif name == "scale4":
                    wait(dve, rstd_d, t, 1)
                    wait(dve, xfT_ps, t, 0)
                    normed(xf, x3, mv_b, rs_b[:, 0]).then_inc(xf_ready[0], 1)
                elif name == "route":
                    wait(dve, r_ps, t, 1)
                    lgt = m1[:, 0:C * NE].rearrange("p (c e) -> p c e", c=C)
                    v.tensor_reduce(smx[:], lgt, AX_X, ALU.max).then_inc(r_steps[0], 1)
                    wait(dve, r_steps, t, 1)
                    v.tensor_tensor(sc[:], lgt, view(smx, 0, [[1, C], [0, NE]]), ALU.subtract).then_inc(r_steps[0], 1)
                elif name == "rank":
                    wait(dve, r_exp, t, 1)
                    v.tensor_reduce(ssum[:], sc[:], AX_X, ALU.add).then_inc(sc_steps[0], 1)
                    wait(dve, sc_steps, t, 1)
                    v.reciprocal(ssum[:], ssum[:]).then_inc(sc_steps[0], 1)
                    wait(dve, sc_steps, t, 2)
                    v.tensor_tensor(sc[:], sc[:], view(ssum, 0, [[1, C], [0, NE]]), ALU.mult).then_inc(sc_steps[0], 1)
                    wait(dve, sc_steps, t, 3)
                    v.tensor_tensor(bi[:], sc[:], rbc("gate_b", C), ALU.add).then_inc(sc_steps[0], 1)
                    wait(dve, sc_steps, t, 4)
                    mine = view(bi, 0, [[NE, C], [1, NE], [0, NE]])
                    others = view(bi, 0, [[NE, C], [0, NE], [1, NE]])
                    v.tensor_tensor(above[:], others, mine, ALU.is_gt)
                    v.tensor_tensor(tied[:], others, mine, ALU.is_equal).then_inc(sc_steps[0], 1)
                    wait(dve, sc_steps, t, 5)
                    v.tensor_tensor(tied[:], tied[:], view(w, W_AT["earlier"][0], [[0, C], [NE, NE], [1, NE]]), ALU.mult).then_inc(sc_steps[0], 1)
                    wait(dve, sc_steps, t, 6)
                    v.tensor_tensor(above[:], above[:], tied[:], ALU.add).then_inc(sc_steps[0], 1)
                    wait(dve, sc_steps, t, 7)
                    v.tensor_reduce(rank[:], above[:], AX_X, ALU.add).then_inc(sc_steps[0], 1)
                    wait(dve, sc_steps, t, 8)
                    wait(dve, rwT_ps, t, 0)
                    v.scalar_tensor_tensor(rw[:, :, 0:NE], rank[:], TOP_K - 0.5, sc[:], ALU.is_lt, ALU.mult).then_inc(rw_ready[0], 1)
                elif name == "chunk":
                    if n == 0:
                        wait(dve, eo_ps, t, 0)
                    if n < NCH:
                        wait(dve, a_ready, t, n + 1)
                        v.scalar_tensor_tensor(hu[:, n], (m0, m1)[n % 2][:, S:2 * S], wc("b3", n, n + 1), ha[:, n % 2],
                                               ALU.add, ALU.mult).then_inc(u_ready[0], 1)
                    if n >= 2:
                        wait(dve, tanh_ready, t, n - 1)
                        v.scalar_tensor_tensor(hu[:, n - 2], ht[:, n % 2], 1.0, hu[:, n - 2], ALU.add, ALU.mult).then_inc(hid_ready[0], 1)
                elif name == "join":
                    c, group = n // EG, n % EG
                    done = c * NX + (0, 1, 5)[group]
                    src = (m1, m0)[n % 2]
                    wait(dve, eo_ps, t, n + 1)
                    if group == 0:
                        if n == 0:
                            wait(dve, rw_ready, t, 1)
                            wait(dve, stored, t, 0)
                        v.tensor_tensor(xo[:, c], src[:, 0:E], x3[:, c], ALU.add).then_inc(eo_acc[0], 1)
                    else:
                        for j in range(4):
                            e = (group - 1) * 4 + j
                            wait(dve, eo_acc, t, done + j)
                            v.scalar_tensor_tensor(xo[:, c], src[:, j * E:(j + 1) * E], rw[:, c, e:e + 1], xo[:, c],
                                                   ALU.mult, ALU.add).then_inc(eo_acc[0], 1)

            turns(dve, attention, rest)

        @block.tensor
        def _(pe):
            mm = nc.tensor.matmul

            def turned(bank_, src):
                for c in range(C):
                    a = nc.tensor.transpose(bank_[:, c * P:(c + 1) * P], src[:, c], ident)
                return a

            def chunk(ap, c):
                return ap[:, c * P:(c + 1) * P]

            def pT_wait(t, p):
                if p % 2:
                    wait(pe, pT_odd, t, p // 2 + 1)
                else:
                    wait(pe, pT_even, t, p // 2 + 1)

            def attention(t, step):
                if step == TURN:
                    wait(pe, xn_ready, t, 1)
                    pT_wait(t, -2)
                    turned(b_t[0], xn).then_inc(xnT_ps[0], 1)
                elif step == PROJECT:
                    wait(pe, xnT_ready, t, 1)
                    pT_wait(t, -1)
                    mm(b_t[1][:, 0:S], wc("WqT"), xnT[:], start=True, stop=True)
                    mm(b_t[1][:, S:2 * S], wc("WkT"), xnT[:], start=True, stop=True).then_inc(qk_ps[0], 1)
                    wait(pe, onT_ready, t, 0)
                    wait(pe, x1_ready, t, 0)
                    for c in range(C):
                        mm(chunk(b_o, c), chunk(xnT, c), wc("WqT_dh"), start=True, stop=True)
                        a = mm(chunk(b_rv, c), chunk(xnT, c), wc("WvT"), start=True, stop=True)
                    a.then_inc(v_ps[0], 1)
                elif PAIR0 <= step < WEIGH:
                    p, part = divmod(step - PAIR0, STEPS_PER_PAIR)
                    if part == 0 and p < PAIRS:
                        if p == 0:
                            wait(pe, qr_in, t, 16 * QI)
                            if isinstance(t, int):
                                pe.wait_ge(tables_ready[0], 1)
                        scores(t, p)
                    elif part == 0:
                        weigh(t, 0, p - PAIRS)
                    elif part == 1 and p >= LAG_REL:
                        relative_values(t, p - LAG_REL)
                    elif part == 2 and 0 <= p - LAG_TURN < PAIRS:
                        turn_weights(t, p - LAG_TURN)
                elif WEIGH <= step < DIVIDE:
                    weigh(t, 1, step - WEIGH)
                elif step == TURN_OUT:
                    wait(pe, on_ready, t, 1)
                    turned(b_o, on).then_inc(onT_ps[0], 1)
                elif step == PROJECT_OUT:
                    wait(pe, onT_ready, t, 1)
                    for c in range(C):
                        a = mm(chunk(b_rv, c), chunk(onT, c), wc("WoT"), start=True, stop=True)
                    a.then_inc(wo_ps[0], 1)

            def weigh(t, c, part):
                if c == 0 and part == 0:
                    wait(pe, exp_ready, t, PAIRS)
                    wait(pe, v_ready, t, 2)
                n = H0 // PV_STEPS
                for h in range(part * n, part * n + n):
                    at = c * 256 + h * (D0 + 1)
                    for kc in range(C):
                        v0 = (kc + C * (kc != c)) * V9 + h * (D0 + 1)
                        a = mm(b_o[:, at:at + NMM], view(pT, (kc * RT + c * RTC) * P + h, [[H0, P]]),
                               v9[:, v0:v0 + NMM], start=kc == 0, stop=kc == C - 1)
                if c == C - 1 and h == H0 - 1:
                    a.then_inc(o_ps[0], 1)

            def scores(t, p):
                wait(pe, exp_ready, t, p - 2)
                if p == 2:
                    wait(pe, qdh_ready, t, 1)
                if p % 4 == 0:
                    wait(pe, qbd_ready, t, p // 4 + 1)
                    wait(pe, kT_ready, t, p // 4 + 1)
                u = 2 * p * QI // KB
                at = u * KB - NEAR
                lo, hi = max(0, at), min(S, at + WIN)
                for j in range(2):
                    i = 2 * p + j
                    mm(b_s[p % 3][:, j * S:(j + 1) * S], qbd[:, i % (RT // 2)], kT[:, u], start=True, stop=False, skip_group_check=True)
                    a = mm(b_s[p % 3][:, j * S + lo:j * S + hi], qr[:, i], tkw[:, KB // QI - 1 - i % (KB // QI), lo - at:hi - at],
                           start=False, stop=True, skip_group_check=True)
                a.then_inc(s_ps[0], 1)

            def turn_weights(t, p):
                wait(pe, exp_ready, t, p + 1)
                pT_wait(t, p - 2)
                if p == 1:
                    wait(pe, kT_ready, t, NKB)
                for j in range(2):
                    for kc in range(C):
                        a = nc.tensor.transpose(b_t[p % 2][:, (j * 2 + kc) * P:(j * 2 + kc + 1) * P],
                                                chunk(pm[:, p % 3, j], kc), ident)
                a.then_inc(pT_ps[0], 1)

            def relative_values(t, p):
                pT_wait(t, p)
                if p % 4 == 0:
                    wait(pe, rv_masked, t, p // 4)
                    wait(pe, v_ready, t, 1)
                for j in range(2):
                    i = 2 * p + j
                    c = i // RTC
                    at = i % 8 * QI * D0
                    n = QI * D0 * (2 if i % 8 < 7 else 1)
                    x = S - QI - i % RTC * QI - TV0
                    corner = RTC - CORNER <= i < RTC + CORNER
                    a = mm(b_rv[:, at:at + n], pT[:, c, i], tv[:, x * D0:x * D0 + n], start=True, stop=not corner)
                    if corner:
                        other = (RTC - 1 - i if c == 0 else RTC + CORNER - 1 - i) * QI * D0
                        a = mm(b_rv[:, at:at + n], pT[:, 1 - c, i], (tv_right, tv_left)[c][:, other:other + n], start=False, stop=True)
                if p % 4 == 3:
                    a.then_inc(rv_ps[0], 1)

            def rest(t, name, n):
                if name == "turn1":
                    wait(pe, h_ready, t, 1)
                    if isinstance(t, int):
                        pe.wait_ge(w_folded[0], 2)
                        pe.wait_ge(small_in[0], 16)
                    wait(pe, eo_acc, t, 0)
                    turned(m0, hh).then_inc(hT_ps[0], 1)
                elif name == "down":
                    wait(pe, hT_ready, t, 1)
                    for c in range(C):
                        mm(chunk(m0, c), chunk(hT, c), wc("fWq"), start=True, stop=True)
                    mm(m1[0:L, 0:S], wc("fWdown"), hT[:], start=True, stop=True).then_inc(qd_ps[0], 1)
                elif name == "up":
                    wait(pe, dT_ready, t, 1)
                    for c in range(C):
                        a = mm(m1[:, c * S:(c + 1) * S], chunk(dT, c), wc("fWup"), start=True, stop=True)
                    a.then_inc(kv_ps[0], 1)
                elif name == "turn_mix":
                    wait(pe, at_ready, t, 1)
                    turned(m0, at1).then_inc(atT_ps[0], 1)
                elif name == "out1":
                    wait(pe, atT_ready, t, 1)
                    for c in range(C):
                        a = mm(chunk(m1, c), chunk(atT, c), wc("fWo"), start=True, stop=True)
                    a.then_inc(fo_ps[0], 1)
                elif name == "turn2":
                    wait(pe, h2_ready, t, 1)
                    turned(m0, h2).then_inc(h2T_ps[0], 1)
                elif name == "gate":
                    wait(pe, h2T_ready, t, 1)
                    for c in range(C):
                        a = mm(m1[:, c * NE:(c + 1) * NE], chunk(h2T, c), wc("fWg"), start=True, stop=True)
                    a.then_inc(g_ps[0], 1)
                elif name == "experts":
                    c, half = n // 2, n % 2
                    if n == 1:
                        wait(pe, g_steps, t, 1)
                    if n >= 2:
                        wait(pe, acc_e, t, 4 * (n - 1))
                    mm((m0, m1)[half][:], chunk(h2T, c), wc("fWe", half * 512, half * 512 + 512), start=True, stop=True).then_inc(we_ps[0], 1)
                elif name == "turn3":
                    wait(pe, h3_ready, t, 1)
                    turned(m0, h3).then_inc(h3T_ps[0], 1)
                elif name == "qkv3":
                    wait(pe, h3T_ready, t, 1)
                    mm(m1[:, 0:S], wc("aWq"), h3T[:], start=True, stop=True)
                    mm(m1[:, S:2 * S], wc("aWk"), h3T[:], start=True, stop=True).then_inc(qk3_ps[0], 1)
                    for c in range(C):
                        a = mm(chunk(m0, c), chunk(h3T, c), wc("aWv"), start=True, stop=True)
                    a.then_inc(v3_ps[0], 1)
                elif name == "sum3":
                    wait(pe, v3_ready, t, 1)
                    wait(pe, qk3_ready, t, 1)
                    for kc in range(C):
                        a = mm(m1[:, 0:V17], wc("half"), v17[:, kc * V17:(kc + 1) * V17], start=kc == 0, stop=kc == C - 1)
                    a.then_inc(vsum_ps[0], 1)
                elif name == "taylor":
                    if n == 0:
                        wait(pe, q3h_ready, t, 1)
                    if n == 1:
                        wait(pe, vsum_ready, t, 1)
                    wait(pe, sq_ready, t, n - 1)
                    for kc in range(C):
                        a = mm((m0, m1)[n % 2][:, kc * S:(kc + 1) * S], chunk(k3, kc), q3h[:, n], start=True, stop=True)
                    a.then_inc(s3_ps[0], 1)
                elif name == "weigh3":
                    if n == 0:
                        wait(pe, sq_ready, t, H1)
                    for h in range(H1):
                        at = h * (D1 + 1)
                        for kc in range(C):
                            a = mm(m0[:, n * 256 + at:n * 256 + at + NMM], chunk(sq[:, h, kc], n),
                                   v17[:, kc * V17 + at:kc * V17 + at + NMM], start=kc == 0, stop=kc == C - 1)
                    if n == C - 1:
                        a.then_inc(o3_ps[0], 1)
                elif name == "turn_o3":
                    wait(pe, o3_ready, t, 1)
                    turned(m1, o3).then_inc(o3T_ps[0], 1)
                elif name == "out3":
                    wait(pe, o3T_ready, t, 1)
                    for c in range(C):
                        a = mm(chunk(m0, c), chunk(o3T, c), wc("aWo"), start=True, stop=True)
                    a.then_inc(ao_ps[0], 1)
                elif name == "turn4":
                    wait(pe, xf_ready, t, 1)
                    turned(m0, xf).then_inc(xfT_ps[0], 1)
                elif name == "route":
                    wait(pe, xfT_ready, t, 1)
                    for c in range(C):
                        a = mm(m1[:, c * NE:(c + 1) * NE], chunk(xfT, c), wc("gateT"), start=True, stop=True)
                    a.then_inc(r_ps[0], 1)
                elif name == "chunk":
                    if n < NCH:
                        if n == 1:
                            wait(pe, r_steps, t, 2)
                        wait(pe, u_ready, t, n - 1)
                        bk = (m0, m1)[n % 2]
                        mm(bk[:, 0:S], wc("W1", n * P, n * P + P), xfT[:], start=True, stop=True)
                        mm(bk[:, S:2 * S], wc("W3", n * P, n * P + P), xfT[:], start=True, stop=True).then_inc(ab_ps[0], 1)
                elif name == "turn_rw":
                    wait(pe, rw_ready, t, 1)
                    wait(pe, u_ready, t, NCH - 1)
                    for c in range(C):
                        a = nc.tensor.transpose(m0[0:NX, c * P:(c + 1) * P], rw[:, c], ident)
                    a.then_inc(rwT_ps[0], 1)
                elif name == "join":
                    c, group = n // EG, n % EG
                    dst = (m1, m0)[n % 2]
                    if n == 0:
                        wait(pe, hid_ready, t, NCH)
                    if n <= 1:
                        wait(pe, rwT_ready, t, 1)
                    if n >= 2:
                        before = n - 2
                        wait(pe, eo_acc, t, before // EG * NX + (1, 5, 9)[before % EG])
                    for j, e in enumerate([NE] if group == 0 else range((group - 1) * 4, group * 4)):
                        o = dst[:, j * E:(j + 1) * E]
                        if group == 0:
                            mm(o, chunk(rwT, c), b2s[:], start=True, stop=False)
                        mm(o, chunk(hu[:, e], c), wc("W2main", e * E, e * E + E), start=group != 0, stop=False)
                        a = mm(o, chunk(hu[:, NX + e // 2], c), wc("W2rem", e * E, e * E + E), start=False, stop=True)
                    a.then_inc(eo_ps[0], 1)

            pe.wait_ge(w_in0[0], 16)
            pe.wait_ge(w_folded[0], 1)
            turns(pe, attention, rest)


def kernel(**inputs):
    import numpy as np
    import concourse.bacc as bacc
    from concourse.bass_utils import run_bass_kernel_spmd

    a = {k: np.asarray(x) for k, x in inputs.items()}
    f = np.float32
    col = lambda x: x.reshape(-1, 1)

    def tall(x):
        return np.concatenate([x, np.zeros((P - x.shape[0], x.shape[1]), f)])

    def by_chunk(first, last):
        allx = np.concatenate([first, last[..., None, :]], -2)
        out = np.zeros((*allx.shape[:-2], NCH, P), f)
        out[..., :NX, :] = allx[..., :P]
        for e in range(NX):
            out[..., NX + e // 2, e % 2 * 64:e % 2 * 64 + REM] = allx[..., e, P:]
        return out

    i = np.arange(P)
    w2_all = np.concatenate([a["L1_ffn_w2"], a["L1_ffn_sw2"][None]])
    w2_rem = np.zeros((P, NX, E), f)
    for e in range(NX):
        w2_rem[e % 2 * 64:e % 2 * 64 + REM, e] = w2_all[e, P:]
    kvf = a["L0_ffn_Wup"].reshape(L, H0, 2, D0)
    bkv = a["L0_ffn_bup"].reshape(H0, 2, D0)
    WqT = a["L0_attn_Wq"].T
    dh = lambda x: x.reshape(-1, H0, D0).transpose(0, 2, 1).reshape(-1, E)
    parts = {
        "ident": np.eye(P, dtype=f),
        "head_mask": (i[:, None] // D0 == np.arange(H0)).astype(f),
        "query_mask": (i[:, None] // H0 == QI - 1 - np.arange(QI)).astype(f),
        "head_mask3": (i[:, None] // D1 == np.arange(H1)).astype(f) * f(D1 ** -0.5),
        "earlier": np.broadcast_to(np.tril(np.ones((NE, NE), f), -1).reshape(1, -1), (P, NE * NE)),
        "half": np.full((P, P), 0.5, f),
        "WqT": WqT, "WqT_dh": dh(WqT), "WkT": a["L0_attn_Wk"].T, "WvT": a["L0_attn_Wv"].T, "WoT": a["L0_attn_Wo"].T,
        "bq": col(a["L0_attn_bq"]), "bk": col(a["L0_attn_bk"]),
        "rk_first": col(np.tile(a["L0_attn_rel_k"][0], H0)), "rk_last": col(np.tile(a["L0_attn_rel_k"][-1], H0)),
        "gamma1": col(a["L0_ffn_gamma1"]), "gamma2": col(a["L0_ffn_gamma2"]), "gamma3": col(a["L1_attn_gamma"]),
        "bdown": tall(col(a["L0_ffn_bdown"])),
        "b1": by_chunk(a["L1_ffn_b1"], a["L1_ffn_sb1"]).T, "b3": by_chunk(a["L1_ffn_b3"], a["L1_ffn_sb3"]).T,
        "fWq": a["L0_ffn_Wq"], "fWdown": a["L0_ffn_Wdown"], "fWo": a["L0_ffn_Wo"],
        "fWup": tall(np.concatenate([kvf[:, :, 0].reshape(L, E), kvf[:, :, 1].transpose(0, 2, 1).reshape(L, E)], 1)), "fWg": a["L0_ffn_Wg"],
        "fWe": a["L0_ffn_We"].transpose(1, 0, 2).reshape(E, NE * E),
        "aWq": a["L1_attn_w_q"], "aWk": a["L1_attn_w_kv"][:, :E], "aWv": a["L1_attn_w_kv"][:, E:], "aWo": a["L1_attn_w_out"],
        "gateT": a["L1_ffn_gate_w"].T,
        "W1": by_chunk(a["L1_ffn_w1"].transpose(1, 0, 2), a["L1_ffn_sw1"]).reshape(E, -1),
        "W3": by_chunk(a["L1_ffn_w3"].transpose(1, 0, 2), a["L1_ffn_sw3"]).reshape(E, -1),
        "W2main": w2_all[:, :P].transpose(1, 0, 2).reshape(P, -1), "W2rem": w2_rem.reshape(P, -1),
    }
    rows = {
        "bq_dh": dh(a["L0_attn_bq"][None]), "bv": a["L0_attn_bv"],
        "rv_first": a["L0_attn_rel_v"][0], "rv_last": a["L0_attn_rel_v"][-1], "bo": a["L0_attn_bo"], "fbq": a["L0_ffn_bq"],
        "fbkv": np.concatenate([bkv[:, 0].reshape(-1), bkv[:, 1].T.reshape(-1)]), "fbo": a["L0_ffn_bo"],
        "fbg": a["L0_ffn_bg"], "gate_b": a["L1_ffn_gate_b"],
    }
    arrays = {
        "x_in": a["L0_attn_hidden_states"],
        "wpack": np.concatenate([parts[n] for n, _ in W_COLS], 1),
        "rpack": np.concatenate([rows[n].reshape(-1) for n, _ in R_COLS]),
        "b2": np.concatenate([a["L1_ffn_b2"], a["L1_ffn_sb2"][None]]),
        "relkT": a["L0_attn_rel_k"].T,
        "relv": a["L0_attn_rel_v"].reshape(1, -1),
    }
    nc = bacc.Bacc("TRN2", target_bir_lowering=False, num_devices=1)
    args, maps = [], {}
    for name, x in arrays.items():
        x = np.ascontiguousarray(x)
        maps[name + "_dram"] = x
        args.append(nc.dram_tensor(name + "_dram", x.shape, F32, kind="ExternalInput").ap())
    args.append(nc.dram_tensor("out_dram", (B, S, E), F32, kind="ExternalOutput").ap())
    build(nc, *args)
    got = run_bass_kernel_spmd(nc, [maps], core_ids=[0])
    return got.results[0]["out_dram"]
```

```python
from contextlib import ExitStack

import concourse.bass as bass
from concourse import mybir

F32 = mybir.dt.float32
ALU = mybir.AluOpType
ACT = mybir.ActivationFunctionType
AX_X = mybir.AxisListType.X

P = 128
B = 8
S = 256
C = S // P
E = 128
H0, D0 = 16, 8
REL = 20
NREL = 2 * REL + 1
QI = P // H0
RT = S // QI
RTC = RT // C
PAIRS = RT // 2
L = 64
NE = 8
H1, D1 = 8, 16
HID = 176
REM = HID - P
NX = NE + 1
NR = NE // 2
SPARE = P - 2 * REM
NSH = -(-REM // SPARE)
NCH = NX + NR
LN_EPS = 1e-5
RMS_EPS = 1e-6
NORM_GUARD = 1e-24 / E
DEN_GUARD = 1e-5
TOP_K = 2
NMM = 96

KB = 64
NKB = S // KB
NEAR = 32
WIN = KB + 2 * NEAR
TV0, TV1 = S - P - (REL // QI + 1) * QI, S + NEAR
TV = TV1 - TV0
CORNER = REL // QI + 1
TVC = (CORNER + 1) * QI
NP = NE // 2

START, PAIR0 = 0, 1
RESIDUAL = PAIR0 + 8
STEPS_PER_PAIR = 3
DVE_MOVES = 8
LAG_TURN, LAG_REL = 2, 4
WEIGH = PAIR0 + STEPS_PER_PAIR * (PAIRS + LAG_REL)
PV_STEPS = 4
DIVIDE = WEIGH + PV_STEPS
TURN_OUT, PROJECT_OUT = DIVIDE + 1, DIVIDE + 2
STEPS = PROJECT_OUT + 1


def counted(name, n):
    return [(name, k) for k in range(n)]


def once(*names):
    return [(name, 0) for name in names]


PREPARE = ["norm0", "scale0", "turn0", "project0", "split0", "blocks0"]

EARLY = (once("norm1", "root1", "scale1", "turn1", "down", "up")
         + [("dot", 2), ("dot", 0), ("dot", 3), ("dot_sum", 3), ("dot_sum", 2), ("dot_sum", 0), ("dot_sum", 1),
            ("soft", 0), ("soft_sum", 0), ("mix", 2), ("mix", 0), ("mix", 3), ("mix_sum", 3),
            ("mix_sum", 2), ("mix_sum", 0), ("mix_sum", 1), ("mix_scale", 0)]
         + once("turn_mix", "out1", "root2", "scale2", "turn2", "gate", "gate_norm") + counted("experts", NP)
         + once("norm3", "scale3", "turn3", "qkv3", "sum3") + counted("taylor", H1) + counted("weigh3", 2 * C)
         + once("divide3", "turn_o3", "out3", "norm4", "scale4", "turn4"))
LATE = once("route", "rank") + counted("chunk", NCH + 2) + once("turn_rw") + counted("join", 1 + NP) + once("store")


PREPARE_STEPS = [50, 51, 52, 52, 55, 62]
LATE_STEPS = [2, 4, 4, 9, 12, 18, 20, 24, 33, 36, 39, 44, 48, 50, 51, 52, 52, 52, 56, 59, 61, 65, 66, 67]
EARLY_STEPS = [0, 0, 3, 5, 7, 10, 10, 10, 10, 13, 16, 19, 23, 25, 29, 31, 31, 32, 34, 38, 38, 41, 41, 44, 46,
               47, 47, 49, 50, 50, 50, 51, 52, 54, 54, 55, 58, 60, 61, 61, 61, 61, 61, 61, 61, 62, 62, 63,
               63, 63, 63, 64, 65, 65, 65, 66, 67]
PIECE_STEP = {**dict(zip(LATE, LATE_STEPS)), **dict(zip(EARLY, EARLY_STEPS))}
PREPARE_AT = [[x for x, at in zip(PREPARE, PREPARE_STEPS) if at == step] for step in range(STEPS)]
PIECES_AT = [[x for x in LATE + EARLY if PIECE_STEP[x] == step] for step in range(STEPS)]
assert PIECE_STEP[("join", 0)] <= PIECE_STEP[("out3", 0)]
LATE_SPAN = 41

W_COLS = [("ident", P), ("head_mask", H0), ("query_mask", QI), ("head_mask3", H1), ("earlier", NE * NE), ("half", P),
          ("WqT", E), ("WqT_dh", E), ("WkT", E), ("WvT", E), ("WoT", E),
          ("bq", 1), ("bk", 1), ("rk_first", 1), ("rk_last", 1),
          ("gamma1", 1), ("gamma2", 1), ("gamma3", 1), ("bdown", 1), ("b1", NCH), ("b3", NCH),
          ("fWq", E), ("fWdown", L), ("fWup", 2 * E), ("fWo", E), ("fWg", NE), ("fWe", NE * E),
          ("aWq", E), ("aWk", E), ("aWv", E), ("aWo", E), ("gateT", NE),
          ("W1", NCH * P), ("W3", NCH * P), ("W2main", NX * E), ("W2rem", (NE + NSH) * E)]
R_COLS = [("bq_dh", E), ("bv", E), ("rv_first", D0), ("rv_last", D0), ("bo", E), ("fbq", E), ("fbkv", 2 * E), ("fbo", E),
          ("fbg", NE), ("gate_b", NE)]


def offsets(cols):
    out, at = {}, 0
    for name, n in cols:
        out[name] = (at, n)
        at += n
    return out, at


W_AT, W_N = offsets(W_COLS)
R_AT, R_N = offsets(R_COLS)


def build(nc, x_in, wpack, rpack, b2, relkT, relv, out):
    ctx = ExitStack()
    with ctx:
        def sb(name, *shape):
            return ctx.enter_context(nc.sbuf_tensor(name, list(shape), F32))

        def sem(name, per):
            return ctx.enter_context(nc.semaphore(name)), per

        def view(t, off, dims, p0=0, np_=P):
            a = t[:]
            row = a.ap[0][0]
            return bass.AP(a.tensor, p0 * row + off, [[row, np_]] + [list(d) for d in dims])

        def raised(signal, t, k):
            s, per = signal
            if isinstance(t, int):
                return s, max(t * per + k, 0)
            return s, t * per + max(k, 0)

        w = sb("w", P, W_N)
        r = sb("r", P, R_N)

        def wc(name, a=0, b=None, p0=0, p1=P):
            at, n = W_AT[name]
            return w[p0:p1, at + a:at + (n if b is None else b)]

        def rc(name):
            at, n = R_AT[name]
            return r[:, at:at + n]

        def rbc(name, copies):
            at, n = R_AT[name]
            return view(r, at, [[0, copies], [1, n]])

        ident = wc("ident")
        HH = H0 * H0
        b2s = sb("b2s", NX, E)
        expo = sb("expo", P, 8)
        half_root = sb("half_root", P, 1)
        TKN = 2 * S
        tk = sb("tk", QI * D0, TKN)
        tkw = sb("tkw", P, KB // QI, WIN)
        tv = sb("tv", P, TV * D0)
        tv_right, tv_left = sb("tv_right", P, TVC * D0), sb("tv_left", P, TVC * D0)
        xin = sb("xin", P, C, E)
        xres = sb("xres", P, C, E)
        st_a, mv_a, ve_a, rs_a = sb("st_a", P, C, 6), sb("mv_a", P, C, 2), sb("ve_a", P, C), sb("rs_a", P, C)
        xn = sb("xn", P, C, E)
        xnT = sb("xnT", P, S)
        qT = sb("qT", P, S)
        kT = sb("kT", P, NKB, S)
        bkf, bkl = sb("bkf", P, 1), sb("bkl", P, 1)
        qdh = sb("qdh", P, C, E)
        vraw = sb("vraw", P, C, E)
        V9 = H0 * (D0 + 1)
        v9 = sb("v9", P, 2 * C * V9 + NMM)
        qbd = sb("qbd", P, RT // 2, P)
        qr = sb("qr", P, RT, P)
        nmx = sb("nmx", P, RT)
        pm = sb("pm", P, 3, 2, S)
        pT = sb("pT", P, C, RT, P)
        rvm = sb("rvm", P, 512)
        w2 = sb("w2", P, RT, D0)
        relo = sb("relo", P, C, E)
        rden = sb("rden", P, C, H0)
        on = sb("on", P, C, E)
        onT = sb("onT", P, S)
        x1 = sb("x1", P, C, E)
        st_b, mv_b, ve_b, rs_b = sb("st_b", P, C, 6), sb("mv_b", P, C, 2), sb("ve_b", P, 2, C), sb("rs_b", P, 2, C)
        xl = sb("xl", P, C, E)
        hh = sb("hh", P, C, E)
        hT = sb("hT", P, S)
        h2 = h3 = xf = hh
        h2T = h3T = hT
        xfT = sb("xfT", P, S)
        dT = sb("dT", P, S)
        q1 = sb("q1", P, C, E)
        kv1 = sb("kv1", P, C, 2 * E)
        prod = sb("prod", P, C, H0 * H0 * D0)
        lg = sb("lg", P, C, H0 * H0)
        lmx = sb("lmx", P, C, H0)
        lsum = sb("lsum", P, C, H0)
        at1 = sb("at1", P, C, E)
        atT = sb("atT", P, S)
        o3, o3T = at1, atT
        y = sb("y", P, C, E)
        ysq = sb("ysq", P, E)
        ss = sb("ss", P, C)
        gl = sb("gl", P, C, NE)
        gmx, gsum = sb("gmx", P, C), sb("gsum", P, C)
        x2 = sb("x2", P, C, E)
        q3 = sb("q3", P, S)
        q3h = sb("q3h", P, H1, S)
        k3 = sb("k3", P, S)
        V17 = H1 * (D1 + 1)
        v17 = sb("v17", P, C * V17 + NMM)
        vsum = sb("vsum", P, V17)
        o17 = sb("o17", P, C, V17)
        sq = prod[:].rearrange("p c (h q) -> p (c h) q", q=2 * S).rearrange("p h (c q) -> p h c q", c=C)
        den3 = sb("den3", P, C, H1)
        x3 = sb("x3", P, C, E)
        sc = sb("sc", P, C, NE)
        smx, ssum = sb("smx", P, C), sb("ssum", P, C)
        bi = sb("bi", P, C, NE)
        above, tied = sb("above", P, C, NE, NE), sb("tied", P, C, NE, NE)
        rank = sb("rank", P, C, NE)
        rw = sb("rw", P, C, NX)
        rwT = sb("rwT", NX, S)
        ha = sb("ha", P, 2, S)
        hu = sb("hu", P, NCH, S)
        EK, EV = 2 * S + QI, S + NEAR + P
        ek, ev = hu[:].rearrange("p n s -> p (n s)")[:, 0:EK], prod[:].rearrange("p c n -> p (c n)")[:, 0:EV * D0]
        ht = sb("ht", P, 2, S)
        xo = sb("xo", P, C, E)
        bank = [ctx.enter_context(nc.psum_tensor(f"bank{j}", [P, 512], F32)) for j in range(8)]
        b_t = bank[2:4]
        b_rv, b_o = bank[4], bank[5]
        b_s = [bank[0], b_o]
        b_p = bank[0]
        m0, m1 = bank[6], bank[7]
        d_qdh = nc.dram_tensor("d_qdh", [S, D0, H0], F32, kind="Internal").ap()
        d_w2 = nc.dram_tensor("d_w2", [RT, QI, H0, D0], F32, kind="Internal").ap()
        d_ev = nc.dram_tensor("d_ev", [EV, D0], F32, kind="Internal").ap()

        w_in0, w_in1, r_in, small_in = (sem(n, 16) for n in ("w_in0", "w_in1", "r_in", "small_in"))
        rel_in, tk_in, ev_out, tv_in = (sem(n, 16) for n in ("rel_in", "tk_in", "ev_out", "tv_in"))
        tables_ready = sem("tables_ready", 1)
        ones_set, rel_filled, w_folded = (sem(n, 1) for n in ("ones_set", "rel_filled", "w_folded"))
        x_loaded, xres_ready, ln_a, rstd_a, xn_ready = sem("x_loaded", 16), sem("xres_ready", 1), sem("ln_a", 5), sem("rstd_a", 1), sem("xn_ready", 1)
        xnT_ps, xnT_ready, qk_ps, v_ps = sem("xnT_ps", 1), sem("xnT_ready", 1), sem("qk_ps", 1), sem("v_ps", 1)
        qT_ready, kT_ready, qdh_ready, v_ready = sem("qT_ready", 1), sem("kT_ready", NKB), sem("qdh_ready", 1), sem("v_ready", 1)
        vraw_ready, v_off_ready = sem("vraw_ready", 1), sem("v_off_ready", 1)
        qdh_out, qr_in, qbd_ready = sem("qdh_out", 16), sem("qr_in", 16 * QI), sem("qbd_ready", 4)
        s_ps, max_ready, exp_ready = sem("s_ps", PAIRS), sem("max_ready", PAIRS), sem("exp_ready", PAIRS)
        pT_ps, pT_dve, pT_act = sem("pT_ps", PAIRS), sem("pT_dve", PAIRS // DVE_MOVES), sem("pT_act", PAIRS - PAIRS // DVE_MOVES)
        rv_ps, rv_masked, rv_sum = sem("rv_ps", 4), sem("rv_masked", 4), sem("rv_sum", 4)
        w2_out, relo_in = sem("w2_out", 16), sem("relo_in", 16)
        o_ps, o_steps, on_ready = sem("o_ps", 1), sem("o_steps", 1), sem("on_ready", 1)
        onT_ps, onT_ready, wo_ps, x1_ready = sem("onT_ps", 1), sem("onT_ready", 1), sem("wo_ps", 1), sem("x1_ready", 1)
        ln_b, rstd_b, h_ready, hT_ps, hT_ready = sem("ln_b", 5), sem("rstd_b", 1), sem("h_ready", 1), sem("hT_ps", 1), sem("hT_ready", 1)
        qd_ps, dT_ready, q1_ready, kv_ps, kv_ready = sem("qd_ps", 1), sem("dT_ready", 1), sem("q1_ready", 1), sem("kv_ps", 1), sem("kv_ready", 1)
        xl_ready, res_b = sem("xl_ready", 1), sem("res_b", 1)
        qk_prod, qk_prod1, qk_sum, l_max, l_sub, l_exp = sem("qk_prod", 2), sem("qk_prod1", 1), sem("qk_sum", 4), sem("l_max", 1), sem("l_sub", 1), sem("l_exp", 1)
        l_sum, l_rec, pv_prod, pv_prod1, pv_sum, at_ready = sem("l_sum", 1), sem("l_rec", 1), sem("pv_prod", 2), sem("pv_prod1", 1), sem("pv_sum", 4), sem("at_ready", 1)
        atT_ps, atT_ready, fo_ps, y_ready = sem("atT_ps", 1), sem("atT_ready", 1), sem("fo_ps", 1), sem("y_ready", 1)
        y_sq, ss_eps, rstd_y, h2_ready = sem("y_sq", 2), sem("ss_eps", 1), sem("rstd_y", 1), sem("h2_ready", 1)
        h2T_ps, h2T_ready, g_ps = sem("h2T_ps", 1), sem("h2T_ready", 1), sem("g_ps", 1)
        g_steps, g_exp, gate_ready = sem("g_steps", 3), sem("g_exp", 1), sem("gate_ready", 3)
        we_ps, acc_e = sem("we_ps", NP), sem("acc_e", 2 * NE)
        x1_sum, x2_ready = sem("x1_sum", 1), sem("x2_ready", 1)
        ln_c, var_c, rstd_c, h3_ready = sem("ln_c", 5), sem("var_c", 2), sem("rstd_c", 1), sem("h3_ready", 1)
        h3T_ps, h3T_ready, qk3_ps, qk3_ready = sem("h3T_ps", 1), sem("h3T_ready", 1), sem("qk3_ps", 1), sem("qk3_ready", 1)
        q3h_ready, vsum_ps, vsum_ready = sem("q3h_ready", H1 // 2), sem("vsum_ps", 1), sem("vsum_ready", 1)
        v3_ps, v3_ready, s3_ps, sq_ready = sem("v3_ps", 1), sem("v3_ready", 1), sem("s3_ps", H1), sem("sq_ready", H1)
        o3_ps, o3_den, o3_ready, o3T_ps, o3T_ready = sem("o3_ps", 1), sem("o3_den", 3), sem("o3_ready", 1), sem("o3T_ps", 1), sem("o3T_ready", 1)
        ao_ps, x3_ready = sem("ao_ps", 1), sem("x3_ready", 1)
        ln_d, rstd_d, xf_ready, xfT_ps, xfT_ready = sem("ln_d", 5), sem("rstd_d", 1), sem("xf_ready", 1), sem("xfT_ps", 1), sem("xfT_ready", 1)
        r_ps, r_steps, r_exp, sc_steps, rw_ready = sem("r_ps", 1), sem("r_steps", 2), sem("r_exp", 1), sem("sc_steps", 8), sem("rw_ready", 1)
        rwT_ps, rwT_ready = sem("rwT_ps", 1), sem("rwT_ready", 1)
        ab_ps, a_ready, u_ready, tanh_ready, hid_ready = sem("ab_ps", NCH), sem("a_ready", NCH), sem("u_ready", NCH), sem("tanh_ready", NCH), sem("hid_ready", NCH)
        eo_ps, eo_acc = sem("eo_ps", 1 + NP), sem("eo_acc", C * NX)
        stored = sem("stored", 16)

        block = ctx.enter_context(nc.Block())

        def late_bank(t, n):
            return bank[0] if late_banks(t) == 2 and n % 2 == 0 else bank[1]

        def late_banks(t):
            return 2 if isinstance(t, int) and t >= B - 2 else 1

        def turns(eng, prepare, attention, rest):
            def body(ta, tb, tc, more=True):
                for step in range(STEPS):
                    attention(ta, step)
                    if more:
                        for name in PREPARE_AT[step]:
                            prepare(ta + 1, name)
                    for name, n in PIECES_AT[step]:
                        t = tc if (name, n) in LATE else tb
                        if t is not None:
                            rest(t, name, n)

            for name in PREPARE:
                prepare(0, name)
            body(0, None, None)
            body(1, 0, None)
            body(2, 1, 0)
            with eng.Fori(3, B - 1) as t:
                body(t, t - 1, t - 2)
            body(B - 1, B - 2, B - 3, more=False)
            for n, piece in enumerate(EARLY):
                rest(B - 1, *piece)
                for late in LATE[n * len(LATE) // LATE_SPAN:(n + 1) * len(LATE) // LATE_SPAN]:
                    rest(B - 2, *late)
            for late in LATE:
                rest(B - 1, *late)

        @block.sync
        def _(sp):
            n0 = W_AT["fWq"][0]
            sp.dma_start(xin[:], x_in[0].rearrange("(c p) e -> p c e", p=P)).then_inc(x_loaded[0], 16)
            sp.dma_start(w[:, 0:n0], wpack[:, 0:n0]).then_inc(w_in0[0], 16)
            sp.wait_ge(rel_filled[0], 1)
            for qi in range(QI):
                sp.dma_start(tk[qi * D0:(qi + 1) * D0, :], ek[0:D0, QI - 1 - qi:QI - 1 - qi + TKN]).then_inc(tk_in[0], 16)
            sp.wait_ge(rel_filled[0], 2)
            sp.dma_start(d_ev.rearrange("m d -> (m d)").rearrange("(a n) -> a n", a=1)[:, TV0 * D0:], ev[0:1, TV0 * D0:]).then_inc(ev_out[0], 16)
            sp.wait_ge(ev_out[0], 16)
            sp.dma_start(tv[:], bass.AP(d_ev.tensor, TV0 * D0, [[D0, P], [1, TV * D0]])).then_inc(tv_in[0], 16)

            def due(signal, t, k):
                value = t * signal[1] + k
                return signal[0], value if isinstance(value, int) else sp.snap(value)

            def met(mark):
                if not isinstance(mark[1], int) or mark[1] > 0:
                    sp.wait_ge(*mark)

            def rows(t, queries, scored, written):
                met(queries)
                met(scored)
                sp.dma_start(d_qdh.rearrange("(c p) d h -> p c (d h)", p=P), qdh[:]).then_inc(qdh_out[0], 16)
                met(written)
                for qi in range(QI):
                    dst = view(qr, qi * H0, [[P, RT], [1, H0]], qi * D0, D0)
                    src = d_qdh.rearrange("(r q) d h -> q d r h", q=QI)[qi]
                    sp.dma_start(dst, src).then_inc(qr_in[0], 16)

            def body(t, more=True):
                rel_sums, rel_written, on_before = due(rv_sum, t, 4), due(w2_out, t, 16), due(on_ready, t, 0)
                if more:
                    xn_before, xres_before = due(xn_ready, t, 1), due(xres_ready, t, 1)
                    marks = due(qdh_ready, t, 2), due(s_ps, t, PAIRS), due(qdh_out, t, 32)
                    at = (t + 1) * (S * E) if isinstance(t, int) else sp.snap((t + 1) * (S * E))
                    met(xn_before)
                    met(xres_before)
                    sp.dma_start(xin[:], bass.AP(x_in.tensor, at, [[E, P], [P * E, C], [1, E]])).then_inc(x_loaded[0], 16)
                    rows(t, *marks)
                met(rel_sums)
                met(on_before)
                sp.dma_start(d_w2.rearrange("r q h d -> (q h) r d"), w2[:]).then_inc(w2_out[0], 16)
                met(rel_written)
                sp.dma_start(relo[:], d_w2.rearrange("(c r) q h d -> (r q) c (h d)", c=C)).then_inc(relo_in[0], 16)

            rows(0, due(qdh_ready, 0, 1), due(s_ps, 0, 0), due(qdh_out, 0, 16))
            sp.dma_start(w[:, n0:], wpack[:, n0:]).then_inc(w_in1[0], 16)
            body(0)
            body(1)
            body(2)
            with sp.Fori(3, B - 1) as t:
                body(t)
            body(B - 1, more=False)
            sp.wait_ge(stored[0], 16 * B)

        @block.scalar
        def _(act):
            copy, idn, exp = ACT.Copy, ACT.Identity, ACT.Exp
            act.dma_start(r[:], rpack.partition_broadcast(P)).then_inc(r_in[0], 16)
            act.dma_start(ek[0:D0, S - REL + QI - 1:S + REL + QI], relkT).then_inc(rel_in[0], 16)
            act.dma_start(ev[0:1, (S - 1 - REL) * D0:(S + REL) * D0], relv).then_inc(rel_in[0], 16)
            act.dma_start(b2s[:], b2).then_inc(small_in[0], 16)

            def evict(t, ps, k, done, src, dst, free=None):
                act.wait_ge(*raised(ps, t, k))
                if free:
                    act.wait_ge(*raised(*free))
                act.activation(dst, src, copy).then_inc(done[0], 1)

            def prepare(t, name):
                if name == "turn0":
                    evict(t, xnT_ps, 1, xnT_ready, b_p[:, 0:S], xnT[:], (v_ps, t, 0))
                elif name == "project0":
                    if isinstance(t, int):
                        act.wait_ge(w_folded[0], 1)
                    act.wait_ge(*raised(qk_ps, t, 1))
                    act.wait_ge(*raised(qbd_ready, t, 0))
                    act.activation(qT[:], b_p[:, 0:S], idn, bias=wc("bq")).then_inc(qT_ready[0], 1)
                    act.wait_ge(*raised(s_ps, t, 0))
                    for u in range(NKB):
                        if u:
                            act.activation(kT[:, u, 0:u * KB], b_p[:, S:S + u * KB], idn, bias=bkf[:])
                        act.activation(kT[:, u, u * KB:], b_p[:, S + u * KB:2 * S], idn, bias=bkl[:]).then_inc(kT_ready[0], 1)

            def attention(t, step):
                if step == START:
                    act.wait_ge(*raised(vraw_ready, t, 1))
                    act.wait_ge(*raised(o_ps, t, 0))
                    act.activation(view(v9, 0, [[V9, C], [D0 + 1, H0], [1, D0]]), view(vraw, 0, [[E, C], [D0, H0], [1, D0]]),
                                   copy).then_inc(v_ready[0], 1)
                elif PAIR0 <= step < WEIGH:
                    p, part = divmod(step - PAIR0, STEPS_PER_PAIR)
                    if part == 0 and p < PAIRS:
                        weights(t, p)
                    elif part == 2 and 0 <= p - LAG_TURN < PAIRS and (p - LAG_TURN) % DVE_MOVES:
                        move_pT(t, p - LAG_TURN)
                elif step == TURN_OUT:
                    evict(t, onT_ps, 1, onT_ready, b_o[:, 0:S], onT[:], (wo_ps, t, 0))

            def weights(t, p):
                act.wait_ge(*raised(max_ready, t, p + 1))
                act.wait_ge(*raised(pT_ps, t, p - 2))
                for j in range(2):
                    a = act.activation(pm[:, p % 3, j], b_s[p % 2][:, j * S:(j + 1) * S], exp,
                                       bias=nmx[:, 2 * p + j:2 * p + j + 1])
                a.then_inc(exp_ready[0], 1)

            def move_pT(t, p):
                act.wait_ge(*raised(pT_ps, t, p + 1))
                if p <= DVE_MOVES:
                    act.wait_ge(*raised(o_ps, t, 0))
                src = view(b_t[p % 2], 0, [[P, 2], [2 * P, 2], [1, P]])
                dst = view(pT, 2 * p * P, [[RT * P, 2], [P, 2], [1, P]])
                act.activation(dst, src, copy).then_inc(pT_act[0], 1)

            def rest(t, name, n):
                if name == "turn1":
                    if isinstance(t, int):
                        act.wait_ge(w_folded[0], 2)
                    evict(t, hT_ps, 1, hT_ready, m0[:, 0:S], hT[:], (v3_ps, t, 0))
                elif name == "down":
                    act.wait_ge(*raised(qd_ps, t, 1))
                    act.wait_ge(*raised(kv_ps, t, 0))
                    act.activation(dT[0:L], m1[0:L, 0:S], idn, bias=wc("bdown", p1=L)).then_inc(dT_ready[0], 1)
                elif name == "soft":
                    act.wait_ge(*raised(l_sub, t, 1))
                    act.activation(lg[:], lg[:], exp, scale=float(D0) ** -0.5).then_inc(l_exp[0], 1)
                elif name == "turn_mix":
                    evict(t, atT_ps, 1, atT_ready, m0[:, 0:S], atT[:], (fo_ps, t, 0))
                elif name == "out1":
                    act.wait_ge(*raised(y_ready, t, 1))
                    for c in range(C):
                        act.wait_ge(*raised(y_sq, t, c))
                        act.activation(ysq[:], y[:, c], ACT.Square, accum_out=ss[:, c:c + 1]).then_inc(y_sq[0], 1)
                elif name == "turn2":
                    evict(t, h2T_ps, 1, h2T_ready, m0[:, 0:S], h2T[:], (we_ps, t, 0))
                elif name == "gate":
                    act.wait_ge(*raised(g_steps, t, 3))
                    act.activation(gl[:], gl[:], exp).then_inc(g_exp[0], 1)
                elif name == "turn3":
                    evict(t, h3T_ps, 1, h3T_ready, m0[:, 0:S], h3T[:], (v3_ps, t, 0))
                elif name == "qkv3":
                    act.wait_ge(*raised(qk3_ps, t, 1))
                    act.wait_ge(*raised(s3_ps, t, 0))
                    act.wait_ge(*raised(q3h_ready, t, 0))
                    act.activation(q3[:], m1[:, 0:S], copy)
                    act.activation(k3[:], m1[:, S:2 * S], copy).then_inc(qk3_ready[0], 1)
                elif name == "sum3":
                    act.wait_ge(*raised(vsum_ps, t, 1))
                    act.wait_ge(*raised(o3_den, t, 0))
                    act.activation(vsum[:], m1[:, 0:V17], copy).then_inc(vsum_ready[0], 1)
                elif name == "taylor":
                    act.wait_ge(*raised(o3_ps, t, 0))
                    act.wait_ge(*raised(s3_ps, t, n + 1))
                    act.activation(sq[:, n], (m0, m1)[n % 2][:], ACT.Square, scale=0.5 ** 0.5,
                                   bias=half_root[:]).then_inc(sq_ready[0], 1)
                elif name == "turn_o3":
                    evict(t, o3T_ps, 1, o3T_ready, m1[:, 0:S], o3T[:], (ao_ps, t, 0))
                elif name == "turn4":
                    evict(t, xfT_ps, 1, xfT_ready, m0[:, 0:S], xfT[:], (ab_ps, t, 0))
                elif name == "route":
                    act.wait_ge(*raised(r_steps, t, 2))
                    act.activation(sc[:], sc[:], exp).then_inc(r_exp[0], 1)
                elif name == "chunk":
                    if n < NCH:
                        act.wait_ge(*raised(ab_ps, t, n + 1))
                        act.wait_ge(*raised(u_ready, t, n - 1))
                        act.activation(ha[:, n % 2], late_bank(t, n)[:, 0:S], idn, scale=0.5,
                                       bias=wc("b1", n, n + 1)).then_inc(a_ready[0], 1)
                    if 1 <= n <= NCH:
                        act.wait_ge(*raised(u_ready, t, n))
                        act.wait_ge(*raised(hid_ready, t, n - 2))
                        act.activation(ht[:, (n - 1) % 2], hu[:, n - 1], ACT.Tanh).then_inc(tanh_ready[0], 1)
                elif name == "turn_rw":
                    evict(t, rwT_ps, 1, rwT_ready, late_bank(t, NCH)[0:NX, 0:S], rwT[:], (eo_ps, t, 0))

            act.wait_ge(ones_set[0], 1)
            turns(act, prepare, attention, rest)

        @block.gpsimd
        def _(pool):
            g = nc.gpsimd
            g.memset(expo[:], -0.5)
            g.memset(half_root[:], 0.5 ** 0.5)
            g.memset(v9[:], 1.0)
            g.memset(v17[:], 1.0)
            g.memset(rw[:], 1.0)
            g.memset(dT[:], 0.0)
            g.memset(tkw[:], 0.0)
            g.memset(qr[:], 0.0).then_inc(ones_set[0], 1)

            def prepare(t, name):
                if name == "norm0":
                    pool.wait_ge(*raised(ln_a, t, 5))
                    pool.wait_ge(*raised(xn_ready, t, 0))
                    g.tensor_tensor(rs_a[:], ve_a[:], expo[:, 0:C], ALU.pow).then_inc(rstd_a[0], 1)
                elif name == "blocks0":
                    if isinstance(t, int):
                        pool.wait_ge(w_in0[0], 16)
                    pool.wait_ge(*raised(qT_ready, t, 1))
                    block_queries(t, 0)
                    block_queries(t, 1)

            def attention(t, step):
                if step == RESIDUAL:
                    pool.wait_ge(*raised(x_loaded, t, 16))
                    if isinstance(t, int):
                        pool.wait_ge(r_in[0], 16)
                    pool.wait_ge(*raised(x1_ready, t, 0))
                    g.tensor_tensor(xres[:], xin[:], rbc("bo", C), ALU.add).then_inc(xres_ready[0], 1)
                    pool.wait_ge(*raised(vraw_ready, t, 1))
                    pool.wait_ge(*raised(o_ps, t, 0))
                    for c, end in enumerate(("rv_first", "rv_last")):
                        a = g.tensor_tensor(view(v9, (C + c) * V9, [[D0 + 1, H0], [1, D0]]), view(vraw, c * E, [[D0, H0], [1, D0]]),
                                            view(r, R_AT[end][0], [[0, H0], [1, D0]]), ALU.add)
                    a.then_inc(v_off_ready[0], 1)
                elif step in (PAIR0 + 4 * STEPS_PER_PAIR, PAIR0 + 8 * STEPS_PER_PAIR):
                    block_queries(t, 1 + (step - PAIR0) // (4 * STEPS_PER_PAIR))

            def block_queries(t, k):
                pool.wait_ge(*raised(s_ps, t, 4 * (k - 1)))
                n = RT // 4
                g.tensor_tensor(view(qbd, k % 2 * n * P, [[P, n], [H0, QI], [1, H0]]),
                                view(qT, k * n * QI, [[QI, n], [1, QI], [0, H0]]),
                                view(w, W_AT["head_mask"][0], [[0, n], [0, QI], [1, H0]]),
                                ALU.mult).then_inc(qbd_ready[0], 1)

            def rest(t, name, n):
                if name == "root1":
                    pool.wait_ge(*raised(ln_b, t, 5))
                    pool.wait_ge(*raised(h_ready, t, 0))
                    g.tensor_tensor(rs_b[:], ve_b[:], view(expo, 0, [[0, 2], [1, C]]), ALU.pow).then_inc(rstd_b[0], 1)
                elif name == "scale1":
                    pool.wait_ge(*raised(xl_ready, t, 1))
                    pool.wait_ge(*raised(y_ready, t, 0))
                    g.tensor_tensor(xl[:], xl[:], rbc("fbo", C), ALU.add).then_inc(res_b[0], 1)
                elif name == "dot" and n != 3:
                    c, heads = n // 2, H0 if n == 0 else H0 // 2
                    pool.wait_ge(*raised(kv_ready, t, 1))
                    pool.wait_ge(*raised(o3_ps, t, 0))
                    g.tensor_tensor(view(prod, c * HH * D0, [[H0 * D0, heads], [D0, H0], [1, D0]]),
                                    view(q1, c * E, [[D0, heads], [0, H0], [1, D0]]),
                                    view(kv1, c * 2 * E, [[0, heads], [D0, H0], [1, D0]]), ALU.mult).then_inc(qk_prod[0], 1)
                elif name == "mix" and n != 3:
                    c, heads = n // 2, H0 if n == 0 else H0 // 2
                    pool.wait_ge(*raised(l_exp, t, 1))
                    g.tensor_tensor(view(prod, c * HH * D0, [[H0 * D0, heads], [H0, D0], [1, H0]]),
                                    view(lg, c * HH, [[H0, heads], [0, D0], [1, H0]]),
                                    view(kv1, c * 2 * E + E, [[0, heads], [H0, D0], [1, H0]]), ALU.mult).then_inc(pv_prod[0], 1)
                elif name == "root2":
                    pool.wait_ge(*raised(ss_eps, t, 1))
                    pool.wait_ge(*raised(h2_ready, t, 0))
                    g.tensor_tensor(rs_b[:, 0], ve_b[:, 0], expo[:, 0:C], ALU.pow).then_inc(rstd_y[0], 1)
                elif name == "turn2":
                    pool.wait_ge(*raised(y_ready, t, 1))
                    pool.wait_ge(*raised(x3_ready, t, 0))
                    g.tensor_tensor(x2[:], x1[:], y[:], ALU.add).then_inc(x1_sum[0], 1)
                elif name == "norm3":
                    pool.wait_ge(*raised(var_c, t, 2))
                    g.tensor_tensor(rs_b[:, 0], ve_b[:, 0], expo[:, 0:C], ALU.pow).then_inc(rstd_c[0], 1)
                elif name == "qkv3":
                    pool.wait_ge(*raised(qk3_ready, t, 1))
                    pool.wait_ge(*raised(s3_ps, t, 0))
                    for h in range(0, H1, 2):
                        g.tensor_tensor(q3h[:, h:h + 2], view(q3, 0, [[0, 2], [1, S]]),
                                        view(w, W_AT["head_mask3"][0] + h, [[1, 2], [0, S]]), ALU.mult).then_inc(q3h_ready[0], 1)
                elif name == "norm4":
                    pool.wait_ge(*raised(ln_d, t, 5))
                    g.tensor_tensor(rs_b[:, 0], ve_b[:, 0], expo[:, 0:C], ALU.pow).then_inc(rstd_d[0], 1)
                elif name == "store":
                    pool.wait_ge(*raised(eo_acc, t, C * NX))
                    pool.dma_start(out[t].rearrange("(c p) e -> p c e", p=P), xo[:]).then_inc(stored[0], 16)

            pool.wait_ge(ones_set[0], 1)
            turns(pool, prepare, attention, rest)

        @block.vector
        def _(dve):
            v = nc.vector
            scale0 = float(D0) ** -0.5

            def fill_ends():
                dve.wait_ge(rel_in[0], 32)
                lo, hi = S - REL + QI - 1, S + REL + QI
                v.tensor_copy(view(hu, 0, [[1, lo]], 0, D0), view(hu, lo, [[0, lo]], 0, D0))
                v.tensor_copy(view(hu, hi, [[1, EK - hi]], 0, D0), view(hu, hi - 1, [[0, EK - hi]], 0, D0)).then_inc(rel_filled[0], 1)
                lo, hi = S - 1 - REL, S + REL
                v.tensor_copy(view(prod, TV0 * D0, [[D0, lo - TV0], [1, D0]], 0, 1), view(prod, lo * D0, [[0, lo - TV0], [1, D0]], 0, 1))
                v.tensor_copy(view(prod, hi * D0, [[D0, EV - hi], [1, D0]], 0, 1),
                              view(prod, (hi - 1) * D0, [[0, EV - hi], [1, D0]], 0, 1)).then_inc(rel_filled[0], 1)

            def fold_scales():
                dve.wait_ge(w_in0[0], 16)
                dve.wait_ge(r_in[0], 16)
                for n in ("WqT", "WqT_dh", "bq"):
                    v.tensor_scalar(wc(n), wc(n), scale0, None, ALU.mult)
                v.tensor_tensor(bkf[:], wc("bk"), wc("rk_first"), ALU.add)
                v.tensor_tensor(bkl[:], wc("bk"), wc("rk_last"), ALU.add)
                v.tensor_scalar(rc("bq_dh"), rc("bq_dh"), scale0, None, ALU.mult).then_inc(w_folded[0], 1)
                dve.wait_ge(w_folded[0], 1)
                dve.wait_ge(ones_set[0], 1)

            def rel_tables():
                dve.wait_ge(tk_in[0], 16 * QI)
                dve.wait_ge(tv_in[0], 16)
                at, n = S - KB + QI - NEAR, KB // QI
                k = QI * D0
                v.tensor_scalar(view(tkw, 0, [[WIN, n], [1, NEAR]], 0, k), view(tk, at, [[QI, n], [1, NEAR]], 0, k),
                                tk[:, 0:1], None, ALU.subtract)
                v.tensor_scalar(view(tkw, NEAR, [[WIN, n], [1, WIN - NEAR]], 0, k), view(tk, at + NEAR, [[QI, n], [1, WIN - NEAR]], 0, k),
                                tk[:, TKN - 1:TKN], None, ALU.subtract)
                for dst, x, end in ((tv_right, S, "rv_last"), (tv_left, TV0, "rv_first")):
                    a = v.tensor_tensor(view(dst, 0, [[D0, TVC], [1, D0]]), view(tv, (x - TV0) * D0, [[D0, TVC], [1, D0]]),
                                        view(r, R_AT[end][0], [[0, TVC], [1, D0]]), ALU.subtract)
                a.then_inc(tables_ready[0], 1)

            def fold_gains():
                dve.wait_ge(w_in1[0], 16)
                for n, gain in (("fWq", "gamma1"), ("fWdown", "gamma1"), ("fWg", "gamma2"), ("fWe", "gamma2"),
                                ("aWq", "gamma3"), ("aWk", "gamma3"), ("aWv", "gamma3")):
                    v.tensor_scalar(wc(n), wc(n), wc(gain), None, ALU.mult)
                v.tensor_scalar(wc("b1"), wc("b1"), 0.5, None, ALU.mult).then_inc(w_folded[0], 1)
                dve.wait_ge(w_folded[0], 2)

            def moments(t, src, st, mv, ve, steps):
                for c in range(C):
                    a = v.bn_stats(st[:, c], src[:, c])
                a.then_inc(steps[0], 1)
                dve.wait_ge(*raised(steps, t, 1))
                v.tensor_tensor(mv[:], st[:, :, 1:3], st[:, :, 4:6], ALU.add)
                v.tensor_tensor(st[:, :, 0], st[:, :, 1], st[:, :, 4], ALU.subtract).then_inc(steps[0], 1)
                dve.wait_ge(*raised(steps, t, 2))
                v.tensor_scalar(mv[:, :, 0], mv[:, :, 0], 0.5, None, ALU.mult)
                v.scalar_tensor_tensor(st[:, :, 3], st[:, :, 0], E / 4, st[:, :, 0], ALU.mult, ALU.mult).then_inc(steps[0], 1)
                dve.wait_ge(*raised(steps, t, 3))
                v.tensor_tensor(mv[:, :, 1], mv[:, :, 1], st[:, :, 3], ALU.add).then_inc(steps[0], 1)
                dve.wait_ge(*raised(steps, t, 4))
                return v.tensor_scalar(ve, mv[:, :, 1], 1 / E, LN_EPS, ALU.mult, ALU.add)

            def normed(dst, src, mv, rs):
                for c in range(C):
                    a = v.tensor_scalar(dst[:, c], src[:, c], mv[:, c, 0:1], rs[:, c:c + 1], ALU.subtract, ALU.mult)
                return a

            def prepare(t, name):
                if name == "norm0":
                    dve.wait_ge(*raised(x_loaded, t, 16))
                    moments(t, xin, st_a, mv_a, ve_a[:], ln_a).then_inc(ln_a[0], 1)
                    if isinstance(t, int) and t == 0:
                        fill_ends()
                elif name == "scale0":
                    dve.wait_ge(*raised(rstd_a, t, 1))
                    dve.wait_ge(*raised(xnT_ps, t, 0))
                    normed(xn, xin, mv_a, rs_a).then_inc(xn_ready[0], 1)
                    if isinstance(t, int) and t == 0:
                        fold_scales()
                elif name == "split0":
                    dve.wait_ge(*raised(v_ps, t, 1))
                    dve.wait_ge(*raised(qdh_out, t, 0))
                    v.tensor_tensor(qdh[:], b_p[:, 0:C * E].rearrange("p (c e) -> p c e", c=C), rbc("bq_dh", C), ALU.add).then_inc(qdh_ready[0], 1)
                    dve.wait_ge(*raised(v_ready, t, 0))
                    dve.wait_ge(*raised(v_off_ready, t, 0))
                    v.tensor_tensor(vraw[:], b_p[:, C * E:2 * C * E].rearrange("p (c e) -> p c e", c=C), rbc("bv", C), ALU.add).then_inc(vraw_ready[0], 1)

            def attention(t, step):
                if step == START:
                    if isinstance(t, int) and t == 0:
                        rel_tables()
                elif PAIR0 <= step < WEIGH:
                    p, part = divmod(step - PAIR0, STEPS_PER_PAIR)
                    if part == 0 and p < PAIRS:
                        dve.wait_ge(*raised(s_ps, t, p + 1))
                        dve.wait_ge(*raised(exp_ready, t, 0))
                        v.tensor_reduce(nmx[:, 2 * p:2 * p + 2], b_s[p % 2][:].rearrange("p (j k) -> p j k", j=2),
                                        AX_X, ALU.max, negate=True).then_inc(max_ready[0], 1)
                    elif part == 1 and p >= LAG_REL and (p - LAG_REL) % 4 == 3:
                        rel_values(t, (p - LAG_REL) // 4)
                    elif part == 2 and 0 <= p - LAG_TURN < PAIRS and (p - LAG_TURN) % DVE_MOVES == 0:
                        move_pT(t, p - LAG_TURN)
                elif step == DIVIDE:
                    dve.wait_ge(*raised(o_ps, t, 1))
                    o4 = [view(b_o, c * 256, [[D0 + 1, H0], [1, D0]]) for c in range(C)]
                    dve.wait_ge(*raised(on_ready, t, 0))
                    v.reciprocal(rden[:], view(b_o, D0, [[256, C], [D0 + 1, H0]]))
                    dve.wait_ge(*raised(relo_in, t, 16))
                    for c in range(C):
                        a = v.tensor_tensor(view(on, c * E, [[D0, H0], [1, D0]]), o4[c], view(relo, c * E, [[D0, H0], [1, D0]]), ALU.add)
                    a.then_inc(o_steps[0], 1)
                    dve.wait_ge(*raised(o_steps, t, 1))
                    dve.wait_ge(*raised(onT_ps, t, 0))
                    v.tensor_tensor(view(on, 0, [[E, C], [D0, H0], [1, D0]]), view(on, 0, [[E, C], [D0, H0], [1, D0]]),
                                    view(rden, 0, [[H0, C], [1, H0], [0, D0]]), ALU.mult).then_inc(on_ready[0], 1)
                elif step == PROJECT_OUT:
                    dve.wait_ge(*raised(wo_ps, t, 1))
                    dve.wait_ge(*raised(xres_ready, t, 1))
                    dve.wait_ge(*raised(x1_sum, t, 0))
                    v.tensor_tensor(x1[:], b_rv[:, 0:C * E].rearrange("p (c e) -> p c e", c=C), xres[:], ALU.add).then_inc(x1_ready[0], 1)

            def move_pT(t, q):
                dve.wait_ge(*raised(pT_ps, t, q + 1))
                if q == 0:
                    dve.wait_ge(*raised(o_ps, t, 0))
                    dve.wait_ge(*raised(rv_ps, t, 0))
                v.tensor_copy(view(pT, 2 * q * P, [[RT * P, 2], [P, 2], [1, P]]),
                              view(b_t[q % 2], 0, [[P, 2], [2 * P, 2], [1, P]])).then_inc(pT_dve[0], 1)

            def rel_values(t, k):
                dve.wait_ge(*raised(rv_ps, t, k + 1))
                dve.wait_ge(*raised(rv_sum, t, k))
                v.tensor_tensor(rvm[:].rearrange("p (r q d) -> p r q d", r=8, q=QI),
                                b_rv[:].rearrange("p (r q d) -> p r q d", r=8, q=QI),
                                view(w, W_AT["query_mask"][0], [[0, 8], [1, QI], [0, D0]]), ALU.mult).then_inc(rv_masked[0], 1)
                dve.wait_ge(*raised(rv_masked, t, k + 1))
                if k == 0:
                    dve.wait_ge(*raised(w2_out, t, 0))
                v.tensor_reduce(w2[:, 8 * k:8 * k + 8, :], view(rvm, 0, [[QI * D0, 8], [1, D0], [D0, QI]]), AX_X, ALU.add).then_inc(rv_sum[0], 1)

            def rest(t, name, n):
                if name == "norm1":
                    if isinstance(t, int) and t == 0:
                        fold_gains()
                    dve.wait_ge(*raised(x1_ready, t, 1))
                    moments(t, x1, st_b, mv_b, ve_b[:, 0], ln_b)
                    v.tensor_scalar(ve_b[:, 1], mv_b[:, :, 1], (1.0 + RMS_EPS) / E, LN_EPS * RMS_EPS, ALU.mult, ALU.add).then_inc(ln_b[0], 1)
                elif name == "scale1":
                    dve.wait_ge(*raised(rstd_b, t, 1))
                    dve.wait_ge(*raised(xfT_ps, t, 0))
                    normed(xl, x1, mv_b, rs_b[:, 0]).then_inc(xl_ready[0], 1)
                    dve.wait_ge(*raised(hT_ps, t, 0))
                    normed(hh, x1, mv_b, rs_b[:, 1]).then_inc(h_ready[0], 1)
                elif name == "down":
                    dve.wait_ge(*raised(qd_ps, t, 1))
                    dve.wait_ge(*raised(qk_prod, t, 0))
                    v.tensor_tensor(q1[:], m0[:, 0:S].rearrange("p (c e) -> p c e", c=C), rbc("fbq", C), ALU.add).then_inc(q1_ready[0], 1)
                elif name == "up":
                    dve.wait_ge(*raised(kv_ps, t, 1))
                    dve.wait_ge(*raised(pv_prod, t, 0))
                    v.tensor_tensor(kv1[:], m1[:].rearrange("p (c e) -> p c e", c=C), rbc("fbkv", C), ALU.add).then_inc(kv_ready[0], 1)
                elif name == "dot" and n == 3:
                    c, at = n // 2, n % 2 * HH // 2
                    dve.wait_ge(*raised(kv_ready, t, 1))
                    dve.wait_ge(*raised(o3_ps, t, 0))
                    v.tensor_tensor(view(prod, (c * HH + at) * D0, [[H0 * D0, H0 // 2], [D0, H0], [1, D0]]),
                                    view(q1, c * E + n % 2 * E // 2, [[D0, H0 // 2], [0, H0], [1, D0]]),
                                    view(kv1, c * 2 * E, [[0, H0 // 2], [D0, H0], [1, D0]]), ALU.mult).then_inc(qk_prod1[0], 1)
                elif name == "dot_sum":
                    c, at = n // 2, n % 2 * HH // 2
                    if n == 3:
                        dve.wait_ge(*raised(qk_prod1, t, 1))
                    else:
                        dve.wait_ge(*raised(qk_prod, t, 2 - c))
                    v.tensor_reduce(lg[:, c, at:at + HH // 2], view(prod, (c * HH + at) * D0, [[D0, HH // 2], [1, D0]]),
                                    AX_X, ALU.add).then_inc(qk_sum[0], 1)
                elif name == "soft":
                    dve.wait_ge(*raised(qk_sum, t, 2 * C))
                    v.tensor_reduce(lmx[:], view(lg, 0, [[H0, C * H0], [1, H0]]), AX_X, ALU.max).then_inc(l_max[0], 1)
                    dve.wait_ge(*raised(l_max, t, 1))
                    v.tensor_tensor(view(lg, 0, [[H0, C * H0], [1, H0]]), view(lg, 0, [[H0, C * H0], [1, H0]]),
                                    view(lmx, 0, [[1, C * H0], [0, H0]]), ALU.subtract).then_inc(l_sub[0], 1)
                elif name == "soft_sum":
                    dve.wait_ge(*raised(l_exp, t, 1))
                    v.tensor_reduce(lsum[:], view(lg, 0, [[H0, C * H0], [1, H0]]), AX_X, ALU.add).then_inc(l_sum[0], 1)
                    dve.wait_ge(*raised(l_sum, t, 1))
                    v.reciprocal(lsum[:], lsum[:]).then_inc(l_rec[0], 1)
                elif name == "mix" and n == 3:
                    c, at = n // 2, n % 2 * HH // 2
                    dve.wait_ge(*raised(l_exp, t, 1))
                    v.tensor_tensor(view(prod, (c * HH + at) * D0, [[H0 * D0, H0 // 2], [H0, D0], [1, H0]]),
                                    view(lg, c * HH + at, [[H0, H0 // 2], [0, D0], [1, H0]]),
                                    view(kv1, c * 2 * E + E, [[0, H0 // 2], [H0, D0], [1, H0]]), ALU.mult).then_inc(pv_prod1[0], 1)
                elif name == "mix_sum":
                    c, at = n // 2, n % 2 * HH // 2
                    if n == 3:
                        dve.wait_ge(*raised(pv_prod1, t, 1))
                    else:
                        dve.wait_ge(*raised(pv_prod, t, 2 - c))
                    v.tensor_reduce(at1[:, c, n % 2 * E // 2:(n % 2 + 1) * E // 2], view(prod, (c * HH + at) * D0, [[H0, E // 2], [1, H0]]),
                                    AX_X, ALU.add).then_inc(pv_sum[0], 1)
                elif name == "mix_scale":
                    dve.wait_ge(*raised(pv_sum, t, 2 * C))
                    dve.wait_ge(*raised(l_rec, t, 1))
                    dve.wait_ge(*raised(atT_ps, t, 0))
                    v.tensor_tensor(view(at1, 0, [[D0, C * H0], [1, D0]]), view(at1, 0, [[D0, C * H0], [1, D0]]),
                                    view(lsum, 0, [[1, C * H0], [0, D0]]), ALU.mult).then_inc(at_ready[0], 1)
                elif name == "out1":
                    dve.wait_ge(*raised(fo_ps, t, 1))
                    dve.wait_ge(*raised(res_b, t, 1))
                    v.tensor_tensor(y[:], m1[:, 0:S].rearrange("p (c e) -> p c e", c=C), xl[:], ALU.add).then_inc(y_ready[0], 1)
                elif name == "root2":
                    dve.wait_ge(*raised(y_sq, t, 2))
                    v.tensor_scalar(ve_b[:, 0], ss[:], 1.0 / E, RMS_EPS, ALU.mult, ALU.add).then_inc(ss_eps[0], 1)
                elif name == "scale2":
                    dve.wait_ge(*raised(rstd_y, t, 1))
                    dve.wait_ge(*raised(h2T_ps, t, 0))
                    for c in range(C):
                        a = v.tensor_scalar(h2[:, c], y[:, c], rs_b[:, 0, c:c + 1], None, ALU.mult)
                    a.then_inc(h2_ready[0], 1)
                elif name == "gate":
                    dve.wait_ge(*raised(g_ps, t, 1))
                    v.tensor_tensor(gl[:], m1[:, 0:C * NE].rearrange("p (c e) -> p c e", c=C), rbc("fbg", C), ALU.add).then_inc(g_steps[0], 1)
                    dve.wait_ge(*raised(g_steps, t, 1))
                    v.tensor_reduce(gmx[:], gl[:], AX_X, ALU.max).then_inc(g_steps[0], 1)
                    dve.wait_ge(*raised(g_steps, t, 2))
                    v.tensor_tensor(gl[:], gl[:], view(gmx, 0, [[1, C], [0, NE]]), ALU.subtract).then_inc(g_steps[0], 1)
                elif name == "gate_norm":
                    dve.wait_ge(*raised(g_exp, t, 1))
                    v.tensor_reduce(gsum[:], gl[:], AX_X, ALU.add).then_inc(gate_ready[0], 1)
                    dve.wait_ge(*raised(gate_ready, t, 1))
                    v.reciprocal(gsum[:], gsum[:]).then_inc(gate_ready[0], 1)
                    dve.wait_ge(*raised(gate_ready, t, 2))
                    v.tensor_tensor(gl[:], gl[:], view(gsum, 0, [[1, C], [0, NE]]), ALU.mult).then_inc(gate_ready[0], 1)
                elif name == "experts":
                    if n == 0:
                        dve.wait_ge(*raised(gate_ready, t, 3))
                        dve.wait_ge(*raised(x1_sum, t, 1))
                    dve.wait_ge(*raised(we_ps, t, n + 1))
                    for j in range(2):
                        e = 2 * n + j
                        for c in range(C):
                            if e:
                                dve.wait_ge(*raised(acc_e, t, (e - 1) * C + c + 1))
                            v.scalar_tensor_tensor(x2[:, c], (m0, m1)[n % 2][:, (c * 2 + j) * E:(c * 2 + j + 1) * E], gl[:, c, e:e + 1],
                                                   x2[:, c], ALU.mult, ALU.add).then_inc(acc_e[0], 1)
                elif name == "norm3":
                    dve.wait_ge(*raised(acc_e, t, 2 * NE))
                    moments(t, x2, st_b, mv_b, ve_b[:, 0], ln_c).then_inc(ln_c[0], 1)
                    dve.wait_ge(*raised(ln_c, t, 5))
                    v.tensor_scalar(ve_b[:, 1], ve_b[:, 0], NORM_GUARD, None, ALU.mult).then_inc(var_c[0], 1)
                    dve.wait_ge(*raised(var_c, t, 1))
                    v.scalar_tensor_tensor(ve_b[:, 0], mv_b[:, :, 1], 1 / E, ve_b[:, 1], ALU.mult, ALU.max).then_inc(var_c[0], 1)
                elif name == "scale3":
                    dve.wait_ge(*raised(rstd_c, t, 1))
                    dve.wait_ge(*raised(h3T_ps, t, 0))
                    normed(h3, x2, mv_b, rs_b[:, 0]).then_inc(h3_ready[0], 1)
                elif name == "qkv3":
                    dve.wait_ge(*raised(v3_ps, t, 1))
                    for c in range(C):
                        a = v.tensor_copy(view(v17, c * V17, [[D1 + 1, H1], [1, D1]]), view(m0, c * E, [[D1, H1], [1, D1]]))
                    a.then_inc(v3_ready[0], 1)
                elif name == "divide3":
                    dve.wait_ge(*raised(o3_ps, t, 1))
                    dve.wait_ge(*raised(vsum_ready, t, 1))
                    v.tensor_tensor(o17[:], view(m0, 0, [[256, C], [1, V17]]), view(vsum, 0, [[0, C], [1, V17]]), ALU.add).then_inc(o3_den[0], 1)
                    dve.wait_ge(*raised(o3_den, t, 1))
                    v.tensor_scalar(den3[:], view(o17, D1, [[V17, C], [D1 + 1, H1]]), DEN_GUARD, None, ALU.max).then_inc(o3_den[0], 1)
                    dve.wait_ge(*raised(o3_den, t, 2))
                    v.reciprocal(den3[:], den3[:]).then_inc(o3_den[0], 1)
                    dve.wait_ge(*raised(o3_den, t, 3))
                    dve.wait_ge(*raised(o3T_ps, t, 0))
                    v.tensor_tensor(view(o3, 0, [[E, C], [D1, H1], [1, D1]]), view(o17, 0, [[V17, C], [D1 + 1, H1], [1, D1]]),
                                    view(den3, 0, [[H1, C], [1, H1], [0, D1]]), ALU.mult).then_inc(o3_ready[0], 1)
                elif name == "out3":
                    dve.wait_ge(*raised(ao_ps, t, 1))
                    v.tensor_tensor(x3[:], m0[:, 0:S].rearrange("p (c e) -> p c e", c=C), x2[:], ALU.add).then_inc(x3_ready[0], 1)
                elif name == "norm4":
                    dve.wait_ge(*raised(x3_ready, t, 1))
                    moments(t, x3, st_b, mv_b, ve_b[:, 0], ln_d).then_inc(ln_d[0], 1)
                elif name == "scale4":
                    dve.wait_ge(*raised(rstd_d, t, 1))
                    dve.wait_ge(*raised(xfT_ps, t, 0))
                    normed(xf, x3, mv_b, rs_b[:, 0]).then_inc(xf_ready[0], 1)
                elif name == "route":
                    dve.wait_ge(*raised(r_ps, t, 1))
                    lgt = late_bank(t, 1)[:, 0:C * NE].rearrange("p (c e) -> p c e", c=C)
                    v.tensor_reduce(smx[:], lgt, AX_X, ALU.max).then_inc(r_steps[0], 1)
                    dve.wait_ge(*raised(r_steps, t, 1))
                    v.tensor_tensor(sc[:], lgt, view(smx, 0, [[1, C], [0, NE]]), ALU.subtract).then_inc(r_steps[0], 1)
                elif name == "rank":
                    dve.wait_ge(*raised(r_exp, t, 1))
                    v.tensor_reduce(ssum[:], sc[:], AX_X, ALU.add).then_inc(sc_steps[0], 1)
                    dve.wait_ge(*raised(sc_steps, t, 1))
                    v.reciprocal(ssum[:], ssum[:]).then_inc(sc_steps[0], 1)
                    dve.wait_ge(*raised(sc_steps, t, 2))
                    v.tensor_tensor(sc[:], sc[:], view(ssum, 0, [[1, C], [0, NE]]), ALU.mult).then_inc(sc_steps[0], 1)
                    dve.wait_ge(*raised(sc_steps, t, 3))
                    v.tensor_tensor(bi[:], sc[:], rbc("gate_b", C), ALU.add).then_inc(sc_steps[0], 1)
                    dve.wait_ge(*raised(sc_steps, t, 4))
                    mine = view(bi, 0, [[NE, C], [1, NE], [0, NE]])
                    others = view(bi, 0, [[NE, C], [0, NE], [1, NE]])
                    v.tensor_tensor(above[:], others, mine, ALU.is_gt)
                    v.tensor_tensor(tied[:], others, mine, ALU.is_equal).then_inc(sc_steps[0], 1)
                    dve.wait_ge(*raised(sc_steps, t, 5))
                    v.tensor_tensor(tied[:], tied[:], view(w, W_AT["earlier"][0], [[0, C], [NE, NE], [1, NE]]), ALU.mult).then_inc(sc_steps[0], 1)
                    dve.wait_ge(*raised(sc_steps, t, 6))
                    v.tensor_tensor(above[:], above[:], tied[:], ALU.add).then_inc(sc_steps[0], 1)
                    dve.wait_ge(*raised(sc_steps, t, 7))
                    v.tensor_reduce(rank[:], above[:], AX_X, ALU.add).then_inc(sc_steps[0], 1)
                    dve.wait_ge(*raised(sc_steps, t, 8))
                    dve.wait_ge(*raised(rwT_ps, t, 0))
                    v.scalar_tensor_tensor(rw[:, :, 0:NE], rank[:], TOP_K - 0.5, sc[:], ALU.is_lt, ALU.mult).then_inc(rw_ready[0], 1)
                elif name == "chunk":
                    if n == 0:
                        dve.wait_ge(*raised(eo_ps, t, 0))
                    if n < NCH:
                        dve.wait_ge(*raised(a_ready, t, n + 1))
                        v.scalar_tensor_tensor(hu[:, n], late_bank(t, n)[:, S:2 * S], wc("b3", n, n + 1), ha[:, n % 2],
                                               ALU.add, ALU.mult).then_inc(u_ready[0], 1)
                    if n >= 2:
                        dve.wait_ge(*raised(tanh_ready, t, n - 1))
                        v.scalar_tensor_tensor(hu[:, n - 2], ht[:, n % 2], 1.0, hu[:, n - 2], ALU.add, ALU.mult).then_inc(hid_ready[0], 1)
                elif name == "join":
                    src = late_bank(t, n + 1)
                    dve.wait_ge(*raised(eo_ps, t, n + 1))
                    if n == 0:
                        dve.wait_ge(*raised(rw_ready, t, 1))
                        dve.wait_ge(*raised(stored, t, 0))
                        for c in range(C):
                            v.tensor_tensor(xo[:, c], src[:, c * 2 * E:c * 2 * E + E], x3[:, c], ALU.add).then_inc(eo_acc[0], 1)
                    else:
                        for j in range(2):
                            e = 2 * (n - 1) + j
                            for c in range(C):
                                dve.wait_ge(*raised(eo_acc, t, e * C + c + 1))
                                v.scalar_tensor_tensor(xo[:, c], src[:, (c * 2 + j) * E:(c * 2 + j + 1) * E], rw[:, c, e:e + 1],
                                                       xo[:, c], ALU.mult, ALU.add).then_inc(eo_acc[0], 1)

            turns(dve, prepare, attention, rest)

        @block.tensor
        def _(pe):
            mm = nc.tensor.matmul

            def turned(bank_, src):
                for c in range(C):
                    a = nc.tensor.transpose(bank_[:, c * P:(c + 1) * P], src[:, c], ident)
                return a

            def chunk(ap, c):
                return ap[:, c * P:(c + 1) * P]

            def pT_wait(t, p):
                if p % DVE_MOVES:
                    pe.wait_ge(*raised(pT_act, t, p - p // DVE_MOVES))
                else:
                    pe.wait_ge(*raised(pT_dve, t, p // DVE_MOVES + 1))

            def prepare(t, name):
                if name == "turn0":
                    pe.wait_ge(*raised(xn_ready, t, 1))
                    pe.wait_ge(*raised(exp_ready, t, 0))
                    turned(b_p, xn).then_inc(xnT_ps[0], 1)
                elif name == "project0":
                    if isinstance(t, int):
                        pe.wait_ge(w_folded[0], 1)
                    pe.wait_ge(*raised(xnT_ready, t, 1))
                    mm(b_p[:, 0:S], wc("WqT"), xnT[:], start=True, stop=True)
                    mm(b_p[:, S:2 * S], wc("WkT"), xnT[:], start=True, stop=True).then_inc(qk_ps[0], 1)
                elif name == "split0":
                    pe.wait_ge(*raised(kT_ready, t, NKB))
                    for c in range(C):
                        mm(chunk(b_p, c), chunk(xnT, c), wc("WqT_dh"), start=True, stop=True)
                        a = mm(chunk(b_p, C + c), chunk(xnT, c), wc("WvT"), start=True, stop=True)
                    a.then_inc(v_ps[0], 1)

            def attention(t, step):
                if step == START:
                    pe.wait_ge(*raised(qr_in, t, 16 * QI))
                    if isinstance(t, int):
                        pe.wait_ge(tables_ready[0], 1)
                elif PAIR0 <= step < WEIGH:
                    p, part = divmod(step - PAIR0, STEPS_PER_PAIR)
                    if part == 0 and p < PAIRS:
                        scores(t, p)
                    elif part == 0:
                        weigh(t, 0, p - PAIRS)
                    elif part == 1 and p >= LAG_REL:
                        relative_values(t, p - LAG_REL)
                    elif part == 2 and 0 <= p - LAG_TURN < PAIRS:
                        turn_weights(t, p - LAG_TURN)
                elif WEIGH <= step < DIVIDE:
                    weigh(t, 1, step - WEIGH)
                elif step == TURN_OUT:
                    pe.wait_ge(*raised(on_ready, t, 1))
                    turned(b_o, on).then_inc(onT_ps[0], 1)
                elif step == PROJECT_OUT:
                    pe.wait_ge(*raised(onT_ready, t, 1))
                    for c in range(C):
                        a = mm(chunk(b_rv, c), chunk(onT, c), wc("WoT"), start=True, stop=True)
                    a.then_inc(wo_ps[0], 1)

            def weigh(t, c, part):
                if c == 0 and part == 0:
                    pe.wait_ge(*raised(exp_ready, t, PAIRS))
                    pe.wait_ge(*raised(v_ready, t, 1))
                    pe.wait_ge(*raised(v_off_ready, t, 1))
                n = H0 // PV_STEPS
                for h in range(part * n, part * n + n):
                    at = c * 256 + h * (D0 + 1)
                    for kc in range(C):
                        v0 = (kc + C * (kc != c)) * V9 + h * (D0 + 1)
                        a = mm(b_o[:, at:at + NMM], view(pT, (kc * RT + c * RTC) * P + h, [[H0, P]]),
                               v9[:, v0:v0 + NMM], start=kc == 0, stop=kc == C - 1)
                if c == C - 1 and h == H0 - 1:
                    a.then_inc(o_ps[0], 1)

            def scores(t, p):
                pe.wait_ge(*raised(exp_ready, t, p - 1))
                if p == 0:
                    pe.wait_ge(*raised(vraw_ready, t, 1))
                if p == 1:
                    pe.wait_ge(*raised(onT_ready, t, 0))
                if p % 4 == 0:
                    pe.wait_ge(*raised(qbd_ready, t, p // 4 + 1))
                    pe.wait_ge(*raised(kT_ready, t, p // 4 + 1))
                u = 2 * p * QI // KB
                at = u * KB - NEAR
                lo, hi = max(0, at), min(S, at + WIN)
                for j in range(2):
                    i = 2 * p + j
                    mm(b_s[p % 2][:, j * S:(j + 1) * S], qbd[:, i % (RT // 2)], kT[:, u], start=True, stop=False, skip_group_check=True)
                    a = mm(b_s[p % 2][:, j * S + lo:j * S + hi], qr[:, i], tkw[:, KB // QI - 1 - i % (KB // QI), lo - at:hi - at],
                           start=False, stop=True, skip_group_check=True)
                a.then_inc(s_ps[0], 1)

            def turn_weights(t, p):
                pe.wait_ge(*raised(exp_ready, t, p + 1))
                pT_wait(t, p - 2)
                for j in range(2):
                    for kc in range(C):
                        a = nc.tensor.transpose(b_t[p % 2][:, (j * 2 + kc) * P:(j * 2 + kc + 1) * P],
                                                chunk(pm[:, p % 3, j], kc), ident)
                a.then_inc(pT_ps[0], 1)

            def relative_values(t, p):
                pT_wait(t, p)
                if p % 4 == 0:
                    pe.wait_ge(*raised(rv_masked, t, p // 4))
                    pe.wait_ge(*raised(x1_ready, t, 0))
                for j in range(2):
                    i = 2 * p + j
                    c = i // RTC
                    at = i % 8 * QI * D0
                    n = QI * D0 * (2 if i % 8 < 7 else 1)
                    x = S - QI - i % RTC * QI - TV0
                    corner = RTC - CORNER <= i < RTC + CORNER
                    a = mm(b_rv[:, at:at + n], pT[:, c, i], tv[:, x * D0:x * D0 + n], start=True, stop=not corner)
                    if corner:
                        other = (RTC - 1 - i if c == 0 else RTC + CORNER - 1 - i) * QI * D0
                        a = mm(b_rv[:, at:at + n], pT[:, 1 - c, i], (tv_right, tv_left)[c][:, other:other + n], start=False, stop=True)
                if p % 4 == 3:
                    a.then_inc(rv_ps[0], 1)

            def rest(t, name, n):
                if name == "turn1":
                    pe.wait_ge(*raised(h_ready, t, 1))
                    if isinstance(t, int):
                        pe.wait_ge(w_folded[0], 2)
                        pe.wait_ge(small_in[0], 16)
                    pe.wait_ge(*raised(xfT_ready, t, 0))
                    turned(m0, hh).then_inc(hT_ps[0], 1)
                elif name == "down":
                    pe.wait_ge(*raised(hT_ready, t, 1))
                    for c in range(C):
                        mm(chunk(m0, c), chunk(hT, c), wc("fWq"), start=True, stop=True)
                    mm(m1[0:L, 0:S], wc("fWdown"), hT[:], start=True, stop=True).then_inc(qd_ps[0], 1)
                elif name == "up":
                    pe.wait_ge(*raised(dT_ready, t, 1))
                    for c in range(C):
                        a = mm(m1[:, c * S:(c + 1) * S], chunk(dT, c), wc("fWup"), start=True, stop=True)
                    a.then_inc(kv_ps[0], 1)
                elif name == "turn_mix":
                    pe.wait_ge(*raised(at_ready, t, 1))
                    turned(m0, at1).then_inc(atT_ps[0], 1)
                elif name == "out1":
                    pe.wait_ge(*raised(atT_ready, t, 1))
                    for c in range(C):
                        a = mm(chunk(m1, c), chunk(atT, c), wc("fWo"), start=True, stop=True)
                    a.then_inc(fo_ps[0], 1)
                elif name == "turn2":
                    pe.wait_ge(*raised(h2_ready, t, 1))
                    turned(m0, h2).then_inc(h2T_ps[0], 1)
                elif name == "gate":
                    pe.wait_ge(*raised(h2T_ready, t, 1))
                    for c in range(C):
                        a = mm(m1[:, c * NE:(c + 1) * NE], chunk(h2T, c), wc("fWg"), start=True, stop=True)
                    a.then_inc(g_ps[0], 1)
                elif name == "experts":
                    if n == 1:
                        pe.wait_ge(*raised(g_steps, t, 1))
                    if n >= 2:
                        pe.wait_ge(*raised(acc_e, t, 2 * C * (n - 1)))
                    for c in range(C):
                        a = mm((m0, m1)[n % 2][:, c * 2 * E:(c + 1) * 2 * E], chunk(h2T, c), wc("fWe", n * 2 * E, (n + 1) * 2 * E),
                               start=True, stop=True)
                    a.then_inc(we_ps[0], 1)
                elif name == "turn3":
                    pe.wait_ge(*raised(h3_ready, t, 1))
                    turned(m0, h3).then_inc(h3T_ps[0], 1)
                elif name == "qkv3":
                    pe.wait_ge(*raised(h3T_ready, t, 1))
                    mm(m1[:, 0:S], wc("aWq"), h3T[:], start=True, stop=True)
                    mm(m1[:, S:2 * S], wc("aWk"), h3T[:], start=True, stop=True).then_inc(qk3_ps[0], 1)
                    for c in range(C):
                        a = mm(chunk(m0, c), chunk(h3T, c), wc("aWv"), start=True, stop=True)
                    a.then_inc(v3_ps[0], 1)
                elif name == "sum3":
                    pe.wait_ge(*raised(v3_ready, t, 1))
                    pe.wait_ge(*raised(qk3_ready, t, 1))
                    for kc in range(C):
                        a = mm(m1[:, 0:V17], wc("half"), v17[:, kc * V17:(kc + 1) * V17], start=kc == 0, stop=kc == C - 1)
                    a.then_inc(vsum_ps[0], 1)
                elif name == "taylor":
                    pe.wait_ge(*raised(q3h_ready, t, n // 2 + 1))
                    if n == 1:
                        pe.wait_ge(*raised(vsum_ready, t, 1))
                    pe.wait_ge(*raised(sq_ready, t, n - 1))
                    for kc in range(C):
                        a = mm((m0, m1)[n % 2][:, kc * S:(kc + 1) * S], chunk(k3, kc), q3h[:, n], start=True, stop=True)
                    a.then_inc(s3_ps[0], 1)
                elif name == "weigh3":
                    if n == 0:
                        pe.wait_ge(*raised(sq_ready, t, H1))
                    c = n // 2
                    for h in range(n % 2 * H1 // 2, (n % 2 + 1) * H1 // 2):
                        at = h * (D1 + 1)
                        for kc in range(C):
                            a = mm(m0[:, c * 256 + at:c * 256 + at + NMM], chunk(sq[:, h, kc], c),
                                   v17[:, kc * V17 + at:kc * V17 + at + NMM], start=kc == 0, stop=kc == C - 1)
                    if n == 2 * C - 1:
                        a.then_inc(o3_ps[0], 1)
                elif name == "turn_o3":
                    pe.wait_ge(*raised(o3_ready, t, 1))
                    turned(m1, o3).then_inc(o3T_ps[0], 1)
                elif name == "out3":
                    pe.wait_ge(*raised(o3T_ready, t, 1))
                    for c in range(C):
                        a = mm(chunk(m0, c), chunk(o3T, c), wc("aWo"), start=True, stop=True)
                    a.then_inc(ao_ps[0], 1)
                elif name == "turn4":
                    pe.wait_ge(*raised(xf_ready, t, 1))
                    turned(m0, xf).then_inc(xfT_ps[0], 1)
                elif name == "route":
                    pe.wait_ge(*raised(xfT_ready, t, 1))
                    pe.wait_ge(*raised(eo_acc, t, 0))
                    if late_banks(t) == 2:
                        pe.wait_ge(*raised(exp_ready, B, 0))
                    for c in range(C):
                        a = mm(late_bank(t, 1)[:, c * NE:(c + 1) * NE], chunk(xfT, c), wc("gateT"), start=True, stop=True)
                    a.then_inc(r_ps[0], 1)
                elif name == "chunk":
                    if n < NCH:
                        if n == late_banks(t) - 1:
                            pe.wait_ge(*raised(r_steps, t, 2))
                        pe.wait_ge(*raised(u_ready, t, n + 1 - late_banks(t)))
                        bk = late_bank(t, n)
                        mm(bk[:, 0:S], wc("W1", n * P, n * P + P), xfT[:], start=True, stop=True)
                        mm(bk[:, S:2 * S], wc("W3", n * P, n * P + P), xfT[:], start=True, stop=True).then_inc(ab_ps[0], 1)
                elif name == "turn_rw":
                    pe.wait_ge(*raised(rw_ready, t, 1))
                    pe.wait_ge(*raised(u_ready, t, NCH + 1 - late_banks(t)))
                    for c in range(C):
                        a = nc.tensor.transpose(late_bank(t, NCH)[0:NX, c * P:(c + 1) * P], rw[:, c], ident)
                    a.then_inc(rwT_ps[0], 1)
                elif name == "join":
                    dst = late_bank(t, n + 1)
                    if n == 0:
                        pe.wait_ge(*raised(hid_ready, t, NCH))
                    if n <= 1:
                        pe.wait_ge(*raised(rwT_ready, t, 1))
                    if n >= late_banks(t):
                        before = n - late_banks(t)
                        pe.wait_ge(*raised(eo_acc, t, C + 2 * C * before))
                    for c in range(C):
                        o = dst[:, c * 2 * E:(c + 1) * 2 * E]
                        if n == 0:
                            mm(o[:, 0:E], chunk(rwT, c), b2s[:], start=True, stop=False)
                            for k in range(NSH):
                                mm(o[:, 0:E], chunk(hu[:, NX + k], c), wc("W2rem", (NE + k) * E, (NE + k + 1) * E), start=False, stop=False)
                            a = mm(o[:, 0:E], chunk(hu[:, NE], c), wc("W2main", NE * E, NX * E), start=False, stop=True)
                        else:
                            e = 2 * (n - 1)
                            mm(o, chunk(hu[:, NX + n - 1], c), wc("W2rem", e * E, (e + 2) * E), start=True, stop=False, skip_group_check=True)
                            for j in range(2):
                                a = mm(o[:, j * E:(j + 1) * E], chunk(hu[:, e + j], c), wc("W2main", (e + j) * E, (e + j + 1) * E),
                                       start=False, stop=True, skip_group_check=True)
                    a.then_inc(eo_ps[0], 1)

            pe.wait_ge(w_in0[0], 16)
            turns(pe, prepare, attention, rest)


def kernel(**inputs):
    import numpy as np
    import concourse.bacc as bacc
    from concourse.bass_utils import run_bass_kernel_spmd

    a = {k: np.asarray(x) for k, x in inputs.items()}
    f = np.float32
    col = lambda x: x.reshape(-1, 1)

    def tall(x):
        return np.concatenate([x, np.zeros((P - x.shape[0], x.shape[1]), f)])

    def by_chunk(first, last):
        allx = np.concatenate([first, last[..., None, :]], -2)
        out = np.zeros((*allx.shape[:-2], NCH, P), f)
        out[..., :NX, :] = allx[..., :P]
        for e in range(NE):
            out[..., NX + e // 2, e % 2 * REM:e % 2 * REM + REM] = allx[..., e, P:]
        for k in range(NSH):
            rest = allx[..., NE, P + k * SPARE:P + (k + 1) * SPARE]
            out[..., NX + k, 2 * REM:2 * REM + rest.shape[-1]] = rest
        return out

    i = np.arange(P)
    w2_all = np.concatenate([a["L1_ffn_w2"], a["L1_ffn_sw2"][None]])
    w2_rem = np.zeros((P, NE + NSH, E), f)
    for e in range(NE):
        w2_rem[e % 2 * REM:e % 2 * REM + REM, e] = w2_all[e, P:]
    for k in range(NSH):
        rest = w2_all[NE, P + k * SPARE:P + (k + 1) * SPARE]
        w2_rem[2 * REM:2 * REM + len(rest), NE + k] = rest
    kvf = a["L0_ffn_Wup"].reshape(L, H0, 2, D0)
    bkv = a["L0_ffn_bup"].reshape(H0, 2, D0)
    WqT = a["L0_attn_Wq"].T
    dh = lambda x: x.reshape(-1, H0, D0).transpose(0, 2, 1).reshape(-1, E)
    parts = {
        "ident": np.eye(P, dtype=f),
        "head_mask": (i[:, None] // D0 == np.arange(H0)).astype(f),
        "query_mask": (i[:, None] // H0 == QI - 1 - np.arange(QI)).astype(f),
        "head_mask3": (i[:, None] // D1 == np.arange(H1)).astype(f) * f(D1 ** -0.5),
        "earlier": np.broadcast_to(np.tril(np.ones((NE, NE), f), -1).reshape(1, -1), (P, NE * NE)),
        "half": np.full((P, P), 0.5, f),
        "WqT": WqT, "WqT_dh": dh(WqT), "WkT": a["L0_attn_Wk"].T, "WvT": a["L0_attn_Wv"].T, "WoT": a["L0_attn_Wo"].T,
        "bq": col(a["L0_attn_bq"]), "bk": col(a["L0_attn_bk"]),
        "rk_first": col(np.tile(a["L0_attn_rel_k"][0], H0)), "rk_last": col(np.tile(a["L0_attn_rel_k"][-1], H0)),
        "gamma1": col(a["L0_ffn_gamma1"]), "gamma2": col(a["L0_ffn_gamma2"]), "gamma3": col(a["L1_attn_gamma"]),
        "bdown": tall(col(a["L0_ffn_bdown"])),
        "b1": by_chunk(a["L1_ffn_b1"], a["L1_ffn_sb1"]).T, "b3": by_chunk(a["L1_ffn_b3"], a["L1_ffn_sb3"]).T,
        "fWq": a["L0_ffn_Wq"], "fWdown": a["L0_ffn_Wdown"], "fWo": a["L0_ffn_Wo"],
        "fWup": tall(np.concatenate([kvf[:, :, 0].reshape(L, E), kvf[:, :, 1].transpose(0, 2, 1).reshape(L, E)], 1)), "fWg": a["L0_ffn_Wg"],
        "fWe": a["L0_ffn_We"].transpose(1, 0, 2).reshape(E, NE * E),
        "aWq": a["L1_attn_w_q"], "aWk": a["L1_attn_w_kv"][:, :E], "aWv": a["L1_attn_w_kv"][:, E:], "aWo": a["L1_attn_w_out"],
        "gateT": a["L1_ffn_gate_w"].T,
        "W1": by_chunk(a["L1_ffn_w1"].transpose(1, 0, 2), a["L1_ffn_sw1"]).reshape(E, -1),
        "W3": by_chunk(a["L1_ffn_w3"].transpose(1, 0, 2), a["L1_ffn_sw3"]).reshape(E, -1),
        "W2main": w2_all[:, :P].transpose(1, 0, 2).reshape(P, -1), "W2rem": w2_rem.reshape(P, -1),
    }
    rows = {
        "bq_dh": dh(a["L0_attn_bq"][None]), "bv": a["L0_attn_bv"],
        "rv_first": a["L0_attn_rel_v"][0], "rv_last": a["L0_attn_rel_v"][-1], "bo": a["L0_attn_bo"], "fbq": a["L0_ffn_bq"],
        "fbkv": np.concatenate([bkv[:, 0].reshape(-1), bkv[:, 1].T.reshape(-1)]), "fbo": a["L0_ffn_bo"],
        "fbg": a["L0_ffn_bg"], "gate_b": a["L1_ffn_gate_b"],
    }
    arrays = {
        "x_in": a["L0_attn_hidden_states"],
        "wpack": np.concatenate([parts[n] for n, _ in W_COLS], 1),
        "rpack": np.concatenate([rows[n].reshape(-1) for n, _ in R_COLS]),
        "b2": np.concatenate([a["L1_ffn_b2"], a["L1_ffn_sb2"][None]]),
        "relkT": a["L0_attn_rel_k"].T,
        "relv": a["L0_attn_rel_v"].reshape(1, -1),
    }
    nc = bacc.Bacc("TRN2", target_bir_lowering=False, num_devices=1)
    args, maps = [], {}
    for name, x in arrays.items():
        x = np.ascontiguousarray(x)
        maps[name + "_dram"] = x
        args.append(nc.dram_tensor(name + "_dram", x.shape, F32, kind="ExternalInput").ap())
    args.append(nc.dram_tensor("out_dram", (B, S, E), F32, kind="ExternalOutput").ap())
    build(nc, *args)
    got = run_bass_kernel_spmd(nc, [maps], core_ids=[0])
    return got.results[0]["out_dram"]
```
